# Optimizing a Trainium2 kernel written in Bass

```python
import numpy as np
import jax
import jax.numpy as jnp

def _softmax(x, axis=-1):
    return jax.nn.softmax(x, axis=axis)

def _gelu(x):
    return jax.nn.gelu(x, approximate=True)

def _silu(x):
    return jax.nn.silu(x)

def _sigmoid(x):
    return jax.nn.sigmoid(x)

def _layernorm(x, axis=-1, eps=1e-05):
    m = jnp.mean(x, axis=axis, keepdims=True)
    v = jnp.var(x, axis=axis, keepdims=True)
    return (x - m) / jnp.sqrt(v + eps)

def _scatter_add(tgt, idx, src, axis=0):
    return tgt.at[idx].add(src)

def _segment_sum(src, seg, n):
    return jax.ops.segment_sum(src, seg, n)
kernel_name = 'mk_perceiver_d1_seqx_r4_c85bb1'

def setup_inputs(seed: int=0):
    np.random.seed(seed)
    _w = jnp.asarray

    def _rec_inputs():
        import jax
        import jax.numpy as jnp
        _rk = jax.random.key(seed)
        x = -0.0005207 + 1.001 * jax.random.normal(jax.random.fold_in(_rk, 1), (32, 64, 512), jnp.float32)
        _lenS = 64 - jax.random.randint(jax.random.fold_in(_rk, 7), (32,), 0, max(1, 64 // 4) + 1, jnp.int32)
        _lenS2 = 256 - jax.random.randint(jax.random.fold_in(_rk, 8), (32,), 0, max(1, 256 // 4) + 1, jnp.int32)
        _ctx_2048P = jax.random.normal(jax.random.fold_in(_rk, 12), (32, 16, 512), jnp.float32)
        _ctx_2048c = jax.random.dirichlet(jax.random.fold_in(_rk, 512), 0.3 * jnp.ones((16,), jnp.float32), (32, 256))
        _ctx_2048t = jnp.einsum('bsk,bkd->bsd', _ctx_2048c, _ctx_2048P)
        _ctx_2048t = _ctx_2048t * jax.lax.rsqrt(jnp.mean(jnp.square(_ctx_2048t)) + 1e-12) * 0.953939
        ctx_2048 = -5.72187e-05 + 0.999849 * (_ctx_2048t + 0.3 * jax.random.normal(jax.random.fold_in(_rk, 612), (32, 256, 512), jnp.float32))
        _validS = jnp.arange(64)[None, :] < _lenS[:, None]
        _validS2 = jnp.arange(256)[None, :] < _lenS2[:, None]
        _causal = jnp.tril(jnp.ones((64, 64), dtype=bool))
        mask_BxSx4224_bf0 = jnp.logical_not(jnp.ones((32, 64, 1056), dtype=bool))
        return (x, ctx_2048, mask_BxSx4224_bf0)
    x, ctx_2048, mask_BxSx4224_bf0 = _rec_inputs()

    def _L0_xattn_setup():
        import jax, jax.numpy as jnp
        import numpy as np
        import math
        DIM = 512
        B, Q_LEN, KV_LEN = (8, 128, 1024)
        key = jax.random.key(seed)
        ks = jax.random.split(key, 8)
        x = jax.random.normal(ks[0], (B, Q_LEN, DIM), dtype=jnp.float32)
        mask = jnp.zeros((B, Q_LEN, KV_LEN + Q_LEN), dtype=bool)
        k_cache = jax.random.normal(ks[1], (B, KV_LEN, DIM), dtype=jnp.float32)
        v_cache = jax.random.normal(ks[2], (B, KV_LEN, DIM), dtype=jnp.float32)
        scale = 1.0 / math.sqrt(DIM)
        wq = jax.random.normal(ks[3], (DIM, DIM), dtype=jnp.float32) * scale
        wk = jax.random.normal(ks[4], (DIM, DIM), dtype=jnp.float32) * scale
        wv = jax.random.normal(ks[5], (DIM, DIM), dtype=jnp.float32) * scale
        wo = jax.random.normal(ks[6], (DIM, DIM), dtype=jnp.float32) * scale
        return {'x': x, 'mask': mask, 'k_cache': k_cache, 'v_cache': v_cache, 'wq': wq, 'wk': wk, 'wv': wv, 'wo': wo}
    _L0_xattn_all = _L0_xattn_setup()
    _L0_xattn_in = {k: v for k, v in _L0_xattn_all.items() if k in ('wq', 'wk', 'wv', 'wo')}
    del _L0_xattn_all

    def _L0_attn_setup():
        import jax, jax.numpy as jnp
        import numpy as np
        import math
        N_HEADS, D_MODEL, D_HEAD = (16, 512, 128)
        BATCH, SEQ = (4, 512)
        ROPE_THETA = 10000.0

        def _rope_cos_sin(seq_len, head_dim, dtype=jnp.float32):
            inv_freq = 1.0 / ROPE_THETA ** (jnp.arange(0, head_dim, 2, dtype=jnp.float32) / head_dim)
            m = jnp.arange(seq_len, dtype=jnp.float32)
            freqs = jnp.outer(m, inv_freq)
            return (jnp.cos(freqs).astype(dtype), jnp.sin(freqs).astype(dtype))

        def _apply_rope(x, cos, sin):
            x1 = x[..., 0::2]
            x2 = x[..., 1::2]
            cos = cos[None, :, None, :]
            sin = sin[None, :, None, :]
            r1 = x1 * cos - x2 * sin
            r2 = x1 * sin + x2 * cos
            out = jnp.stack([r1, r2], axis=-1)
            return out.reshape(x.shape)
        key = jax.random.key(seed)
        ks = jax.random.split(key, 9)
        std = 0.02
        return {'normalized_resid_pre': jax.random.normal(ks[0], (BATCH, SEQ, D_MODEL), jnp.float32), 'W_Q': jax.random.normal(ks[1], (N_HEADS, D_MODEL, D_HEAD), jnp.float32) * std, 'b_Q': jnp.zeros((N_HEADS, D_HEAD), jnp.float32), 'W_K': jax.random.normal(ks[2], (N_HEADS, D_MODEL, D_HEAD), jnp.float32) * std, 'b_K': jnp.zeros((N_HEADS, D_HEAD), jnp.float32), 'W_V': jax.random.normal(ks[3], (N_HEADS, D_MODEL, D_HEAD), jnp.float32) * std, 'b_V': jnp.zeros((N_HEADS, D_HEAD), jnp.float32), 'W_O': jax.random.normal(ks[4], (N_HEADS, D_HEAD, D_MODEL), jnp.float32) * std, 'b_O': jnp.zeros((D_MODEL,), jnp.float32)}
    _L0_attn_all = _L0_attn_setup()
    _L0_attn_in = {k: v for k, v in _L0_attn_all.items() if k in ('W_Q', 'b_Q', 'W_K', 'b_K', 'W_V', 'b_V', 'W_O', 'b_O')}
    del _L0_attn_all

    def _L0_ffn_setup():
        import jax, jax.numpy as jnp
        import numpy as np
        _FP4_LUT = jnp.array([0.0, 0.5, 1.0, 1.5, 2.0, 3.0, 4.0, 6.0, -0.0, -0.5, -1.0, -1.5, -2.0, -3.0, -4.0, -6.0], dtype=jnp.float32)
        GROUP_SIZE = 128
        EPS = 1e-06

        def _dequant_fp4(packed_i32, scales_f16, group_size):
            out_f, in_p = packed_i32.shape
            w = packed_i32.astype(jnp.uint32)
            shifts = jnp.arange(8, dtype=jnp.uint32) * 4
            nib = w[:, :, None] >> shifts & jnp.uint32(15)
            vals = _FP4_LUT[nib.astype(jnp.int32)].reshape(out_f, in_p * 8)
            s = scales_f16.astype(jnp.float32).T
            s_full = jnp.repeat(s, group_size, axis=1)
            return vals * s_full
        key = jax.random.key(seed)
        k1, k2, k3, k4, k5 = jax.random.split(key, 5)
        B, S, H, I = (4, 512, 512, 1408)
        x = jax.random.normal(k1, (B, S, H), dtype=jnp.float32)
        gate_up_packed = jax.random.randint(k2, (2 * I, H // 8), 0, 2147483647, dtype=jnp.int32)
        gate_up_scales = jax.random.uniform(k3, (H // GROUP_SIZE, 2 * I), dtype=jnp.float32).astype(jnp.float16)
        down_packed = jax.random.randint(k4, (H, I // 8), 0, 2147483647, dtype=jnp.int32)
        down_scales = jax.random.uniform(k5, (I // GROUP_SIZE, H), dtype=jnp.float32).astype(jnp.float16)
        return {'x': x, 'gate_up_packed': gate_up_packed, 'gate_up_scales': gate_up_scales, 'down_packed': down_packed, 'down_scales': down_scales}
    _L0_ffn_all = _L0_ffn_setup()
    _L0_ffn_in = {k: v for k, v in _L0_ffn_all.items() if k in ('gate_up_packed', 'gate_up_scales', 'down_packed', 'down_scales')}
    del _L0_ffn_all
    return {'x': x, 'ctx_2048': ctx_2048, 'mask_BxSx4224_bf0': mask_BxSx4224_bf0, 'L0_xattn_wq': _L0_xattn_in['wq'], 'L0_xattn_wk': _L0_xattn_in['wk'], 'L0_xattn_wv': _L0_xattn_in['wv'], 'L0_xattn_wo': _L0_xattn_in['wo'], 'L0_attn_W_Q': _L0_attn_in['W_Q'], 'L0_attn_b_Q': _L0_attn_in['b_Q'], 'L0_attn_W_K': _L0_attn_in['W_K'], 'L0_attn_b_K': _L0_attn_in['b_K'], 'L0_attn_W_V': _L0_attn_in['W_V'], 'L0_attn_b_V': _L0_attn_in['b_V'], 'L0_attn_W_O': _L0_attn_in['W_O'], 'L0_attn_b_O': _L0_attn_in['b_O'], 'L0_ffn_gate_up_packed': _L0_ffn_in['gate_up_packed'], 'L0_ffn_gate_up_scales': _L0_ffn_in['gate_up_scales'], 'L0_ffn_down_packed': _L0_ffn_in['down_packed'], 'L0_ffn_down_scales': _L0_ffn_in['down_scales']}

def reference(x, ctx_2048, mask_BxSx4224_bf0, L0_xattn_wq, L0_xattn_wk, L0_xattn_wv, L0_xattn_wo, L0_attn_W_Q, L0_attn_b_Q, L0_attn_W_K, L0_attn_b_K, L0_attn_W_V, L0_attn_b_V, L0_attn_W_O, L0_attn_b_O, L0_ffn_gate_up_packed, L0_ffn_gate_up_scales, L0_ffn_down_packed, L0_ffn_down_scales):
    import jax
    import jax.numpy as jnp

    def _L0_xattn_ref(x, mask, k_cache, v_cache, wq, wk, wv, wo):
        import jax, jax.numpy as jnp
        import numpy as np
        import math
        DIM = 512
        B, Q_LEN, KV_LEN = (8, 128, 1024)
        q = jnp.einsum('bsd,ed->bse', x, wq)
        k_new = jnp.einsum('bsd,ed->bse', x, wk)
        v_new = jnp.einsum('bsd,ed->bse', x, wv)
        k = jnp.concatenate([k_cache, k_new], axis=1)
        v = jnp.concatenate([v_cache, v_new], axis=1)
        scale = 1.0 / math.sqrt(q.shape[-1])
        scores = jnp.einsum('bqd,bkd->bqk', q, k) * scale
        attn = jax.nn.softmax(scores, axis=-1)
        out = jnp.einsum('bqk,bkd->bqd', attn, v)
        return jnp.einsum('bqd,ed->bqe', out, wo)

    def _L0_attn_ref(normalized_resid_pre, W_Q, b_Q, W_K, b_K, W_V, b_V, W_O, b_O):
        import jax, jax.numpy as jnp
        import numpy as np
        import math
        N_HEADS, D_MODEL, D_HEAD = (16, 512, 128)
        BATCH, SEQ = (4, 512)
        ROPE_THETA = 10000.0

        def _rope_cos_sin(seq_len, head_dim, dtype=jnp.float32):
            inv_freq = 1.0 / ROPE_THETA ** (jnp.arange(0, head_dim, 2, dtype=jnp.float32) / head_dim)
            m = jnp.arange(seq_len, dtype=jnp.float32)
            freqs = jnp.outer(m, inv_freq)
            return (jnp.cos(freqs).astype(dtype), jnp.sin(freqs).astype(dtype))

        def _apply_rope(x, cos, sin):
            x1 = x[..., 0::2]
            x2 = x[..., 1::2]
            cos = cos[None, :, None, :]
            sin = sin[None, :, None, :]
            r1 = x1 * cos - x2 * sin
            r2 = x1 * sin + x2 * cos
            out = jnp.stack([r1, r2], axis=-1)
            return out.reshape(x.shape)
        x = normalized_resid_pre
        T = x.shape[1]
        d_head = W_Q.shape[-1]
        Q = jnp.einsum('btc,ncd->btnd', x, W_Q) + b_Q
        K = jnp.einsum('btc,ncd->btnd', x, W_K) + b_K
        V = jnp.einsum('btc,ncd->btnd', x, W_V) + b_V
        cos, sin = _rope_cos_sin(T, d_head, x.dtype)
        Q = _apply_rope(Q, cos, sin)
        K = _apply_rope(K, cos, sin)
        scores = jnp.einsum('bqnd,bknd->bnqk', Q, K) / math.sqrt(d_head)
        causal = jnp.tril(jnp.ones((T, T), dtype=bool))
        scores = jnp.where(causal[None, None], scores, -jnp.inf)
        probs = jax.nn.softmax(scores, axis=-1)
        z = jnp.einsum('bnqk,bknd->bqnd', probs, V)
        out = jnp.einsum('bqnd,ndm->bqm', z, W_O) + b_O
        return out

    def _L0_ffn_ref(x, gate_up_packed, gate_up_scales, down_packed, down_scales):
        import jax, jax.numpy as jnp
        import numpy as np
        _FP4_LUT = jnp.array([0.0, 0.5, 1.0, 1.5, 2.0, 3.0, 4.0, 6.0, -0.0, -0.5, -1.0, -1.5, -2.0, -3.0, -4.0, -6.0], dtype=jnp.float32)
        GROUP_SIZE = 128
        EPS = 1e-06

        def _dequant_fp4(packed_i32, scales_f16, group_size):
            out_f, in_p = packed_i32.shape
            w = packed_i32.astype(jnp.uint32)
            shifts = jnp.arange(8, dtype=jnp.uint32) * 4
            nib = w[:, :, None] >> shifts & jnp.uint32(15)
            vals = _FP4_LUT[nib.astype(jnp.int32)].reshape(out_f, in_p * 8)
            s = scales_f16.astype(jnp.float32).T
            s_full = jnp.repeat(s, group_size, axis=1)
            return vals * s_full
        I = gate_up_packed.shape[0] // 2
        w_gu = _dequant_fp4(gate_up_packed, gate_up_scales, GROUP_SIZE)
        w_down = _dequant_fp4(down_packed, down_scales, GROUP_SIZE)
        gate_up = jnp.einsum('bsh,oh->bso', x, w_gu)
        gate, up = (gate_up[..., :I], gate_up[..., I:])
        h = jax.nn.silu(gate) * up
        y = jnp.einsum('bsi,hi->bsh', h, w_down)
        rms = jnp.sqrt(jnp.mean(y * y, axis=-1, keepdims=True) + EPS)
        return y / rms
    x = x + _L0_xattn_ref(_layernorm(x, axis=-1), mask_BxSx4224_bf0, ctx_2048, ctx_2048, L0_xattn_wq, L0_xattn_wk, L0_xattn_wv, L0_xattn_wo)
    x = x + _L0_attn_ref(_layernorm(x, axis=-1), L0_attn_W_Q, L0_attn_b_Q, L0_attn_W_K, L0_attn_b_K, L0_attn_W_V, L0_attn_b_V, L0_attn_W_O, L0_attn_b_O)
    x = x + _L0_ffn_ref(_layernorm(x, axis=-1), L0_ffn_gate_up_packed, L0_ffn_gate_up_scales, L0_ffn_down_packed, L0_ffn_down_scales)
    return x

_drawn_inputs = setup_inputs


def setup_inputs(seed=0):
    import zlib

    import numpy as np

    out = dict(_drawn_inputs(seed))
    spreads = {'L0_attn_b_Q': (0.0, 0.8),
     'L0_attn_b_K': (0.0, 0.8),
     'L0_attn_b_V': (0.0, 0.1),
     'L0_attn_b_O': (0.0, 0.1)}
    factors = {'L0_attn_W_Q': 3.168, 'L0_attn_W_K': 3.107}
    for name, (base, spread) in spreads.items():
        noise = np.random.default_rng([zlib.crc32(name.encode()), seed]).standard_normal(out[name].shape)
        drawn = base * np.exp(spread * noise) if base else spread * noise
        out[name] = jnp.asarray(drawn.astype(out[name].dtype))
    for name, factor in factors.items():
        out[name] = (out[name] * factor).astype(out[name].dtype)
    return out
```

```python
from contextlib import ExitStack

import concourse.bass as bass
from concourse import mybir

F32 = mybir.dt.float32
F16 = mybir.dt.float16
I32 = mybir.dt.int32
ALU = mybir.AluOpType
ACT = mybir.ActivationFunctionType

P = 128
B, S, D = 32, 64, 512
KV = 256
TOK = B * S
TILE = 512
NT = TOK // TILE
TT = TILE // P
KD = D // P
HEADS, DH = 16, 128
HALF = DH // 2
PAIRS = HEADS // 2
FF = 1408
FB = FF // P
LN_EPS = 1e-5
RMS_EPS = 1e-6
LOWEST = -3.0e38

XS = 2.0 ** 8
WS = 2.0 ** 11
AS = 2.0 ** 6
XATTN_SCALE = float(D) ** -0.5
HEAD_SCALE = float(DH) ** -0.5
RSQRT_MAGIC = 0x5F3759DF


class Banks:

    def __init__(self, nc, ctx, name, before, body):
        self.filled = [ctx.enter_context(nc.semaphore(f"{name}_bank{b}_filled")) for b in range(8)]
        self.moved = [ctx.enter_context(nc.semaphore(f"{name}_bank{b}_moved")) for b in range(8)]
        self.ahead, self.uses, self.at = [0] * 8, [0] * 8, {}
        for unit, bank in before:
            self.at["before", unit] = (bank, self.ahead[bank])
            self.ahead[bank] += 1
        for unit, bank in body:
            self.at["body", unit] = (bank, self.uses[bank])
            self.uses[bank] += 1

    def place(self, t, unit):
        if t is None:
            return self.at["before", unit]
        bank, k = self.at["body", unit]
        return bank, t * self.uses[bank] + (self.ahead[bank] + k)

    def bank(self, t, unit):
        return self.place(t, unit)[0]

    def wait_room(self, pe, t, unit):
        bank, earlier = self.place(t, unit)
        if not (isinstance(earlier, int) and earlier == 0):
            pe.wait_ge(self.moved[bank], earlier)

    def wait_filled(self, eng, t, unit):
        bank, earlier = self.place(t, unit)
        eng.wait_ge(self.filled[bank], earlier + 1)

    def wait_moved(self, eng, t, unit):
        bank, earlier = self.place(t, unit)
        eng.wait_ge(self.moved[bank], earlier + 1)

    def before(self, t, unit):
        bank, k = self.at["body", unit]
        behind = self.ahead[bank] + k + 1 - self.uses[bank]
        assert behind >= 0
        return bank, t * self.uses[bank] + behind

    def wait_filled_before(self, eng, t, unit):
        bank, count = self.before(t, unit)
        eng.wait_ge(self.filled[bank], count)

    def wait_moved_before(self, eng, t, unit):
        bank, count = self.before(t, unit)
        eng.wait_ge(self.moved[bank], count)

    def fills(self, ins, t, unit):
        ins.then_inc(self.filled[self.bank(t, unit)], 1)

    def moves(self, ins, t, unit):
        ins.then_inc(self.moved[self.bank(t, unit)], 1)


ROOT_STEPS = 2 + 9
LN_STEPS = 2 * TT + 1 + ROOT_STEPS + 1
RMS_STEPS = 1 + ROOT_STEPS


def inverse_root(dve, stat, done):
    var, half, y, y2 = stat["var"], stat["half"], stat["y"], stat["y2"]
    done(dve.tensor_scalar(half[:, :], var[:, :].bitcast(I32), 1, None, ALU.logical_shift_right))
    done(dve.tensor_scalar(y[:, :].bitcast(I32), half[:, :], -1, RSQRT_MAGIC, ALU.mult, ALU.add))
    for _ in range(3):
        done(dve.tensor_tensor(y2[:, :], y[:, :], y[:, :], ALU.mult))
        done(dve.scalar_tensor_tensor(y2[:, :], y2[:, :], -0.5, var[:, :], ALU.mult, ALU.mult))
        done(dve.scalar_tensor_tensor(y[:, :], y2[:, :], 1.5, y[:, :], ALU.add, ALU.mult))


def layernorm(dve, t, src, dst, stat, step, ready, by_code=False):
    n = [0]

    def all_done():
        dve.wait_ge(step, t * LN_STEPS + n[0])
        if not isinstance(t, int):
            dve.nop(nofuse=True)

    def done(ins, wait=True):
        ins.then_inc(step, 1)
        n[0] += 1
        if wait:
            all_done()

    for i in range(TT):
        done(dve.bn_stats(stat["six"][:, i, :], src[:, i, :]), wait=(i == TT - 1))
    for i in range(TT):
        done(dve.bn_aggr(stat["meanvar"][:, i, :], stat["six"][:, i, :]), wait=(i == TT - 1))
    done(dve.tensor_scalar(stat["var"][:, :], stat["meanvar"][:, :, 1], LN_EPS, None, ALU.add))
    inverse_root(dve, stat, done)
    y = stat["y"]
    done(dve.tensor_scalar(y[:, :], y[:, :], XS, None, ALU.mult))
    for i in range(TT):
        to, from_ = dst[:, i, :], src[:, i, :]
        if by_code:
            to = to.rearrange("p (j u w) -> p j u w", j=4, u=2)
            from_ = from_.rearrange("p (w u j) -> p j u w", j=4, u=2)
        dve.tensor_scalar(to, from_, stat["meanvar"][:, i, 0:1], y[:, i:i + 1], ALU.subtract, ALU.mult).then_inc(ready, 1)
    assert n[0] == LN_STEPS


def three_passes(pe, out, left, right):
    k = len(left)
    for i in range(k):
        (lh, ll), (rh, rl) = left[i], right[i]
        pe.matmul(out, lh, rh, start=(i == 0), stop=False)
        pe.matmul(out, lh, rl, start=False, stop=False)
        last = pe.matmul(out, ll, rh, start=False, stop=(i == k - 1))
    return last


def stat_buffers(sb):
    return {"six": sb("ln_six", [P, TT, 6], F32), "meanvar": sb("ln_meanvar", [P, TT, 2], F32),
            "var": sb("ln_var", [P, TT], F32), "half": sb("ln_half", [P, TT], I32),
            "y": sb("ln_y", [P, TT], F32), "y2": sb("ln_y2", [P, TT], F32)}


def xattn_phase(nc, psum, ident, x_rows, ctx_kv, wq, wk, wv, wo, own_new, x1_rows):
    with ExitStack() as ctx:
        def sb(name, shape, dt):
            return ctx.enter_context(nc.sbuf_tensor("xa_" + name, shape, dt))

        def sem(name):
            return ctx.enter_context(nc.semaphore("xa_" + name))

        w_rows = sb("w_rows", [P, 4, KD, D], F32)
        w_hi, w_lo = sb("w_hi", [P, 4, KD, D], F16), sb("w_lo", [P, 4, KD, D], F16)
        x_in = sb("x_in", [P, TT, D], F32)
        xn = sb("xn", [P, TT, D], F32)
        xt_hi, xt_lo = sb("xt_hi", [P, KD, TILE], F16), sb("xt_lo", [P, KD, TILE], F16)
        q_t, k_t = sb("q_t", [P, KD, TILE], F32), sb("k_t", [P, KD, TILE], F32)
        v_new = sb("v_new", [P, TT, D], F32)
        kv = sb("kv", [P, 2, 4, D], F32)
        kv_t = sb("kv_t", [P, KD, 2 * KV], F32)
        mask = sb("mask", [P, KV + P], F32)
        masked, probs = sb("masked", [P, KV + P], F32), sb("probs", [P, KV + P], F32)
        probs_t = sb("probs_t", [P, 3, P], F32)
        top, low_top = sb("top", [P, TT], F32), sb("low_top", [P, TT], F32)
        total, inv_total = sb("total", [P, TT], F32), sb("inv_total", [P, TT], F32)
        att = sb("att", [P, D], F32)
        att_hi, att_lo = sb("att_hi", [P, KD, P], F16), sb("att_lo", [P, KD, P], F16)
        x_res, x1 = sb("x_res", [P, TT, D], F32), sb("x1", [P, TT, D], F32)
        stat = stat_buffers(sb)

        w_loaded = [sem(f"w{i}_loaded") for i in range(4)]
        x_loaded, res_loaded = sem("x_loaded"), sem("res_loaded")
        kv_loaded = [sem("kv0_loaded"), sem("kv1_loaded")]
        w_hi_done, w_lo_done, ln_step, xn_ready, xt_hi_done = sem("w_hi_done"), sem("w_lo_done"), sem("ln_step"), sem("xn_ready"), sem("xt_hi_done")
        low_top_ready, exp_done = sem("low_top_ready"), sem("exp_done")
        inv_ready, att_hi_done = sem("inv_ready"), sem("att_hi_done")
        mask_loaded_x1_stored = sem("mask_loaded_x1_stored")

        turn_x = [(("x", k), 4 + k) for k in range(KD)]
        warm = [(("warm", i), i % 4) for i in range(8)]
        before = warm + turn_x
        body = [(("q", e), e) for e in range(4)] + [(("k", e), 4 + e) for e in range(4)] + [(("v", p), p) for p in range(TT)]

        def turn_kv(p):
            return [(("kv", p, k), 4 + k) for k in range(KD)]

        body += turn_kv(0) + [(("scores", 0), 0)]
        for p in range(TT):
            body += turn_kv(p + 1) if p + 1 < TT else []
            body += [(("probs", p), 1)]
            body += [(("scores", p + 1), 0)] if p + 1 < TT else turn_x
            body += [(("turn", p - 1), 3)] if p else []
            body += [(("att", p), 2)]
            body += [(("out", p - 1), 1)] if p else []
        body += [(("turn", TT - 1), 3), (("out", TT - 1), 1)]
        banks = Banks(nc, ctx, "xa", before, body)

        def psum_of(t, unit, n=512):
            return psum[:, banks.bank(t, unit), 0:n]

        def rows_of(tensor, first, n):
            return tensor[bass.ds(first, n), :].rearrange("(b p) d -> p b d", p=P)

        block = ctx.enter_context(nc.Block())

        @block.sync
        def _(sp):
            sp.dma_start(x_in[:, :, :], rows_of(x_rows, 0, TILE)).then_inc(x_loaded, 16)
            for i, w in enumerate((wq, wk, wv, wo)):
                sp.dma_start(w_rows[:, i, :, :], rows_of(w, 0, D)).then_inc(w_loaded[i], 16)

            def tile(t, last_tile):
                for p in range(TT):
                    if p < 2:
                        banks.wait_filled_before(sp, t, ("att", p + 2))
                    else:
                        banks.wait_filled(sp, t, ("att", p - 2))
                    for s in range(2):
                        sp.dma_start(kv[:, p % 2, 2 * s:2 * s + 2, :],
                                     ctx_kv[bass.ds(t * (2 * TT * KV) + (2 * p + s) * KV, KV), :]
                                     .rearrange("(b p) d -> p b d", p=P)).then_inc(kv_loaded[p % 2], 16)
                    if p == 0:
                        banks.wait_moved_before(sp, t, ("out", TT - 1))
                        sp.dma_start(x_res[:, :, :], rows_of(x_rows, t * TILE, TILE)).then_inc(res_loaded, 16)
                        if not last_tile:
                            sp.wait_ge(xn_ready, t * TT + TT)
                            sp.dma_start(x_in[:, :, :], rows_of(x_rows, t * TILE + TILE, TILE)).then_inc(x_loaded, 16)

            with nc.sync.Fori(0, NT - 1) as t:
                tile(t, False)
            tile(NT - 1, True)

        @block.gpsimd
        def _(pool):
            pool.dma_start(mask[:, :], own_new).then_inc(mask_loaded_x1_stored, 16)
            with nc.gpsimd.Fori(0, NT) as t:
                for p in range(TT):
                    banks.wait_moved(pool, t, ("out", p))
                    pool.dma_start(x1_rows[bass.ds(t * TILE + p * P, P), :], x1[:, p, :]).then_inc(mask_loaded_x1_stored, 16)
            pool.wait_ge(mask_loaded_x1_stored, 16 + 16 * NT * TT)

        @block.tensor
        def _(pe):
            def transposes(t, unit, blocks):
                banks.wait_room(pe, t, unit)
                for i, from_ in enumerate(blocks):
                    last = pe.transpose(psum[:, banks.bank(t, unit), i * P:(i + 1) * P], from_, ident[:, :])
                banks.fills(last, t, unit)

            def turn_xn(t, nth):
                pe.wait_ge(xn_ready, nth * TT + TT)
                for k in range(KD):
                    transposes(t, ("x", k), [xn[:, i, k * P:(k + 1) * P] for i in range(TT)])

            for unit, _ in warm:
                transposes(None, unit, [ident[:, :]])
            turn_xn(None, 0)
            pe.wait_ge(w_lo_done, 4 * KD)

            def cols(hi, lo, at):
                return [(hi[:, k, at], lo[:, k, at]) for k in range(KD)]

            def weight(w, at):
                return cols(w_hi[:, w, :, :], w_lo[:, w, :, :], at)

            def block_of(i):
                return slice(i * P, (i + 1) * P)

            def tile(t, last_tile):
                def project(unit, left, right):
                    banks.wait_room(pe, t, unit)
                    banks.fills(three_passes(pe, psum_of(t, unit), left, right), t, unit)

                def turn_ctx(p):
                    pe.wait_ge(kv_loaded[p % 2], t * 64 + 32 * (p // 2 + 1))
                    for k in range(KD):
                        transposes(t, ("kv", p, k), [kv[:, p % 2, i, block_of(k)] for i in range(4)])

                def scores(p):
                    unit = ("scores", p)
                    for k in range(KD):
                        banks.wait_moved(pe, t, ("kv", p, k))
                    banks.wait_room(pe, t, unit)
                    b = banks.bank(t, unit)
                    for k in range(KD):
                        pe.matmul(psum[:, b, KV:KV + P], q_t[:, k, block_of(p)], k_t[:, k, block_of(p)],
                                  start=(k == 0), stop=(k == KD - 1), skip_group_check=True)
                    for s in range(2):
                        for k in range(KD):
                            last = pe.matmul(psum[s * S:(s + 1) * S, b, 0:KV], q_t[:, k, p * P + s * S:p * P + (s + 1) * S],
                                             kv_t[:, k, s * KV:(s + 1) * KV], start=False, stop=(k == KD - 1),
                                             skip_group_check=True)
                    banks.fills(last, t, unit)

                def attend(p):
                    unit = ("att", p)
                    banks.wait_moved(pe, t, ("probs", p))
                    banks.wait_room(pe, t, unit)
                    b = banks.bank(t, unit)
                    pe.matmul(psum[:, b, :], probs_t[:, 2, :], v_new[:, p, :], start=True, stop=True, skip_group_check=True)
                    for s in range(2):
                        for i in range(2):
                            last = pe.matmul(psum[s * S:(s + 1) * S, b, :], probs_t[:, i, s * S:(s + 1) * S],
                                             kv[:, p % 2, 2 * s + i, :], start=False, stop=(i == 1), skip_group_check=True)
                    banks.fills(last, t, unit)

                def turn_att(p):
                    banks.wait_moved(pe, t, ("att", p))
                    transposes(t, ("turn", p), [att[:, block_of(k)] for k in range(KD)])

                def project_out(p):
                    banks.wait_moved(pe, t, ("turn", p))
                    project(("out", p), cols(att_hi, att_lo, slice(0, P)), weight(3, slice(0, D)))

                for k in range(KD):
                    banks.wait_moved_before(pe, t, ("x", k))
                xt = cols(xt_hi, xt_lo, slice(0, TILE))
                for e in range(4):
                    project(("q", e), weight(0, block_of(e)), xt)
                for e in range(4):
                    project(("k", e), weight(1, block_of(e)), xt)
                for p in range(TT):
                    project(("v", p), cols(xt_hi, xt_lo, block_of(p)), weight(2, slice(0, D)))
                turn_ctx(0)
                scores(0)
                for p in range(TT):
                    if p + 1 < TT:
                        turn_ctx(p + 1)
                    pe.wait_ge(exp_done, t * TT + (p + 1))
                    transposes(t, ("probs", p), [probs[:, block_of(i)] for i in range(3)])
                    if p + 1 < TT:
                        scores(p + 1)
                    elif not last_tile:
                        turn_xn(t, t + 1)
                    if p:
                        turn_att(p - 1)
                    attend(p)
                    if p:
                        project_out(p - 1)
                turn_att(TT - 1)
                project_out(TT - 1)

            with nc.tensor.Fori(0, NT - 1) as t:
                tile(t, False)
            tile(NT - 1, True)

        unscale = 1.0 / (XS * WS)
        acts_part = {"q": (0, 2), "k": (0, 2), "v": (0, 2), "kv": (0, 1)}
        dves_part = {"q": (1, 3), "k": (1, 3), "v": (1, 3), "kv": (2, 3)}
        home = {"q": q_t, "k": k_t, "v": v_new}

        @block.scalar
        def _(act):
            def first_halves(t):
                for k in range(KD):
                    banks.wait_filled(act, t, ("x", k))
                    act.activation(xt_hi[:, k, :], psum_of(t, ("x", k)), ACT.Copy).then_inc(xt_hi_done, 1)

            for unit, _ in warm:
                banks.wait_filled(act, None, unit)
                banks.moves(act.activation(att[:, unit[1]:unit[1] + 1], psum_of(None, unit, 1), ACT.Copy), None, unit)
            first_halves(None)
            for w in range(4):
                act.wait_ge(w_loaded[w], 16)
                for k in range(KD):
                    act.activation(w_hi[:, w, k, :], w_rows[:, w, k, :], ACT.Copy, scale=WS).then_inc(w_hi_done, 1)

            def tile(t, last_tile):
                def move(unit, out, scale=1.0):
                    banks.wait_filled(act, t, unit)
                    n = 3 * P if unit[0] == "probs" else 512
                    banks.moves(act.activation(out, psum_of(t, unit, n), ACT.Copy, scale=scale), t, unit)

                def softmax(p):
                    act.wait_ge(low_top_ready, t * TT + (p + 1))
                    act.activation(probs[:, :], masked[:, :], ACT.Exp, bias=low_top[:, p:p + 1], scale=XATTN_SCALE,
                                   accum_out=total[:, p:p + 1]).then_inc(exp_done, 1)

                def move_ctx(p):
                    for k in acts_part["kv"]:
                        move(("kv", p, k), kv_t[:, k, :])

                def att_first_half(p):
                    banks.wait_filled(act, t, ("turn", p))
                    act.activation(att_hi[:, :, :].rearrange("p a b -> p (a b)"), psum_of(t, ("turn", p)), ACT.Copy,
                                   scale=AS).then_inc(att_hi_done, 1)

                for kind in "qkv":
                    for e in acts_part[kind]:
                        move((kind, e), home[kind][:, e, :], unscale)
                move_ctx(0)
                softmax(0)
                for p in range(TT):
                    if p + 1 < TT:
                        move_ctx(p + 1)
                    move(("probs", p), probs_t[:, :, :].rearrange("p a b -> p (a b)"))
                    if p + 1 < TT:
                        softmax(p + 1)
                    elif not last_tile:
                        first_halves(t)
                    if p:
                        att_first_half(p - 1)
                    act.wait_ge(inv_ready, t * TT + (p + 1))
                    move(("att", p), att[:, :], inv_total[:, p:p + 1])
                att_first_half(TT - 1)

            with nc.scalar.Fori(0, NT - 1) as t:
                tile(t, False)
            tile(NT - 1, True)

        @block.vector
        def _(dve):
            def second_halves(t, nth):
                for k in range(KD):
                    dve.wait_ge(xt_hi_done, nth * KD + (k + 1))
                    banks.moves(dve.tensor_tensor(xt_lo[:, k, :], psum_of(t, ("x", k)), xt_hi[:, k, :], ALU.subtract), t, ("x", k))

            dve.wait_ge(x_loaded, 16)
            layernorm(dve, 0, x_in, xn, stat, ln_step, xn_ready)
            second_halves(None, 0)
            for w in range(4):
                for k in range(KD):
                    dve.wait_ge(w_hi_done, w * KD + k + 1)
                    dve.scalar_tensor_tensor(w_lo[:, w, k, :], w_rows[:, w, k, :], WS, w_hi[:, w, k, :],
                                             ALU.mult, ALU.subtract).then_inc(w_lo_done, 1)
            dve.wait_ge(mask_loaded_x1_stored, 16)

            def tile(t, last_tile):
                def move(unit, out, scale=1.0):
                    banks.wait_filled(dve, t, unit)
                    banks.moves(dve.tensor_scalar(out, psum_of(t, unit), scale, None, ALU.mult), t, unit)

                def move_ctx(p):
                    for k in dves_part["kv"]:
                        banks.wait_filled(dve, t, ("kv", p, k))
                        banks.moves(dve.tensor_copy(kv_t[:, k, :], psum_of(t, ("kv", p, k))), t, ("kv", p, k))

                def maximum(p):
                    unit = ("scores", p)
                    banks.wait_filled(dve, t, unit)
                    dve.nop(nofuse=True)
                    banks.moves(dve.tensor_tensor_reduce(masked[:, :], psum_of(t, unit, KV + P), mask[:, :], 1.0, LOWEST,
                                                         ALU.add, ALU.max, top[:, p:p + 1]), t, unit)
                    banks.wait_moved(dve, t, unit)
                    dve.tensor_scalar(low_top[:, p:p + 1], top[:, p:p + 1], -XATTN_SCALE, None, ALU.mult).then_inc(low_top_ready, 1)

                def inverse(p):
                    dve.wait_ge(exp_done, t * TT + (p + 1))
                    dve.reciprocal(inv_total[:, p:p + 1], total[:, p:p + 1]).then_inc(inv_ready, 1)

                def att_second_half(p):
                    dve.wait_ge(att_hi_done, t * TT + (p + 1))
                    banks.moves(dve.scalar_tensor_tensor(att_lo[:, :, :].rearrange("p a b -> p (a b)"), psum_of(t, ("turn", p)), AS,
                                                         att_hi[:, :, :].rearrange("p a b -> p (a b)"), ALU.mult, ALU.subtract),
                                t, ("turn", p))

                def residual(p):
                    if p == 0:
                        dve.wait_ge(res_loaded, t * 16 + 16)
                        dve.wait_ge(mask_loaded_x1_stored, t * (16 * TT) + 16)
                    banks.wait_filled(dve, t, ("out", p))
                    banks.moves(dve.scalar_tensor_tensor(x1[:, p, :], psum_of(t, ("out", p)), 1.0 / (AS * WS), x_res[:, p, :],
                                                         ALU.mult, ALU.add), t, ("out", p))

                for e in dves_part["q"]:
                    move(("q", e), q_t[:, e, :], unscale)
                if not last_tile:
                    dve.wait_ge(x_loaded, t * 16 + 32)
                    layernorm(dve, t + 1, x_in, xn, stat, ln_step, xn_ready)
                for kind in "kv":
                    for e in dves_part[kind]:
                        move((kind, e), home[kind][:, e, :], unscale)
                move_ctx(0)
                maximum(0)
                for p in range(TT):
                    if p + 1 < TT:
                        move_ctx(p + 1)
                    inverse(p)
                    if p + 1 < TT:
                        maximum(p + 1)
                    elif not last_tile:
                        second_halves(t, t + 1)
                    if p:
                        att_second_half(p - 1)
                        residual(p - 1)
                att_second_half(TT - 1)
                residual(TT - 1)

            with nc.vector.Fori(0, NT - 1) as t:
                tile(t, False)
            tile(NT - 1, True)


class Sections:

    def __init__(self, nc, ctx, name, sections):
        self.filled = [ctx.enter_context(nc.semaphore(f"{name}_bank{b}_filled")) for b in range(8)]
        self.moved = [ctx.enter_context(nc.semaphore(f"{name}_bank{b}_moved")) for b in range(8)]
        self.uses = {s: [0] * 8 for s in sections}
        self.where = {}
        for s, units in sections.items():
            for unit, bank in units:
                self.where[unit] = (bank, self.uses[s][bank])
                self.uses[s][bank] += 1

    def bank(self, unit):
        return self.where[unit][0]

    def earlier(self, runs, unit):
        bank, count = self.where[unit]
        for s, n in runs.items():
            if self.uses[s][bank]:
                count = n * self.uses[s][bank] + count
        return count

    def wait_room(self, pe, runs, unit):
        n = self.earlier(runs, unit)
        if not (isinstance(n, int) and n == 0):
            pe.wait_ge(self.moved[self.bank(unit)], n)

    def wait_filled(self, eng, runs, unit):
        eng.wait_ge(self.filled[self.bank(unit)], self.earlier(runs, unit) + 1)

    def wait_moved(self, eng, runs, unit):
        eng.wait_ge(self.moved[self.bank(unit)], self.earlier(runs, unit) + 1)

    def fills(self, ins, unit):
        ins.then_inc(self.filled[self.bank(unit)], 1)

    def moves(self, ins, unit):
        ins.then_inc(self.moved[self.bank(unit)], 1)


def heads_phase(nc, psum, ident, x1_rows, w_q, w_k, w_v, b_q, b_k, b_v, rope_cos, rope_sin, causal, z_scratch):
    with ExitStack() as ctx:
        def sb(name, shape, dt):
            return ctx.enter_context(nc.sbuf_tensor("hd_" + name, shape, dt))

        def sem(name):
            return ctx.enter_context(nc.semaphore("hd_" + name))

        WIDE = HEADS * DH
        w_hi, w_lo = sb("w_hi", [P, 3, KD, WIDE], F16), sb("w_lo", [P, 3, KD, WIDE], F16)
        w_rows = sb("w_rows", [P, 2, WIDE], F32)
        x_in, xn = sb("x_in", [P, TT, D], F32), sb("xn", [P, TT, D], F32)
        xt_hi, xt_lo = sb("xt_hi", [P, KD, TILE], F16), sb("xt_lo", [P, KD, TILE], F16)
        bias = sb("bias", [P, 2, 2, PAIRS], F32)
        bias_v = sb("bias_v", [P, HEADS], F32)
        cos, sin = sb("cos", [P, S], F32), sb("sin", [P, S], F32)
        mask = sb("mask", [P, P], F32)
        products = sb("products", [P, 2, 4, TILE], F32)
        rotated = sb("rotated", [P, 2, 2, TILE], F32)
        v = sb("v", [P, TT, 2 * DH], F32)
        masked, probs = sb("masked", [P, 2, TT, P], F32), sb("probs", [P, 2, TT, P], F32)
        probs_t = sb("probs_t", [P, 2, TT, P], F32)
        top, low_top = sb("top", [P, 2, TT], F32), sb("low_top", [P, 2, TT], F32)
        total, inv_total = sb("total", [P, 2, TT], F32), sb("inv_total", [P, 2, TT], F32)
        z_hi, z_lo = sb("z_hi", [P, 2, TILE], F16), sb("z_lo", [P, 2, TILE], F16)
        stat = stat_buffers(lambda name, shape, dt: sb(name, shape, dt))

        loaded = [sem("rows0_loaded"), sem("rows1_loaded")]
        w_hi_done, w_lo_done = sem("w_hi_done"), sem("w_lo_done")
        small_loaded_z_stored = sem("small_loaded_z_stored")
        x_loaded, bias_scaled = sem("x_loaded"), sem("bias_scaled")
        ln_step, xn_ready, xt_hi_done = sem("ln_step"), sem("xn_ready"), sem("xt_hi_done")
        added_dve, added_pool = sem("added_dve"), sem("added_pool")
        low_top_ready, exp_done, inv_done, probs_ready = sem("low_top_ready"), sem("exp_done"), sem("inv_done"), sem("probs_ready")
        z_hi_done = sem("z_hi_done")
        SMALL = 6

        banks = Sections(nc, ctx, "hd", {
            "turn": [(("x", 2), 6), (("x", 3), 7), (("x", 0), 4), (("x", 1), 5)],
            "proj": [(("q", 0), 0), (("q", 1), 1), (("k", 0), 2), (("k", 1), 3), (("v", 0), 6), (("v", 1), 7)],
            "scores": [(("scores", 0), 4), (("scores", 1), 5)],
            "att": [(("probs", 0), 4), (("probs", 1), 5), (("z", 0), 0), (("z", 1), 1)],
        })

        def psum_of(unit):
            return psum[:, banks.bank(unit), :]

        def rows_of(first):
            return x1_rows[bass.ds(first, TILE), :].rearrange("(b p) d -> p b d", p=P)

        blocks = [(w, k) for w in range(3) for k in range(KD)]

        class Step:

            def __init__(self, a, turns, pair, next_pair, turn_next=False, att=True, proj=True):
                self.a, self.pair, self.next_pair = a, pair, next_pair
                self.first_token = (turns - 1) * TILE
                self.turn_next, self.att, self.proj = turn_next, att, proj
                self.turns = turns
                self.runs_scores = {"turn": turns, "scores": a, "att": a}
                self.runs_turn = {"turn": turns, "proj": a + 1, "scores": a + 1, "att": a}
                self.turns_now = turns + 1 if turn_next else turns
                g = a + 1
                self.runs_proj = {"turn": self.turns_now, "proj": g, "att": a if att else 0}
                self.runs_probs = {"turn": self.turns_now, "scores": a + 1, "att": a}
                self.runs_z = {"proj": g + 1 if proj else g, "att": a}

        def for_each_step(eng, before_tile, step):
            step(Step(-1, 1, None, 0, att=False))
            def tile(t, last_tile):
                before_tile(t, last_tile)
                with eng.Fori(0, PAIRS - 1) as n:
                    step(Step(t * PAIRS + n, t + 1, n, n + 1))
                if not last_tile:
                    step(Step(t * PAIRS + (PAIRS - 1), t + 1, PAIRS - 1, 0, turn_next=True))
            with eng.Fori(0, NT - 1) as t:
                tile(t, False)
            tile(NT - 1, True)
            step(Step(NT * PAIRS - 1, NT, PAIRS - 1, None, proj=False))

        block = ctx.enter_context(nc.Block())

        @block.sync
        def _(sp):
            sp.dma_start(x_in[:, :, :], rows_of(0)).then_inc(x_loaded, 16)
            for i, (w, k) in enumerate(blocks):
                if i >= 2:
                    sp.wait_ge(w_lo_done, i - 1)
                sp.dma_start(w_rows[:, i % 2, :], (w_q, w_k, w_v)[w][k * P:(k + 1) * P, :]).then_inc(loaded[i % 2], 16)
                if i == 1:
                    for dst, src in ((cos, rope_cos), (sin, rope_sin), (mask, causal)):
                        sp.dma_start(dst[:, :], src).then_inc(small_loaded_z_stored, 16)
                    for w_, b in enumerate((b_q, b_k)):
                        sp.dma_start(bias[:, w_, :, :], b).then_inc(small_loaded_z_stored, 16)
                    sp.dma_start(bias_v[:, :], b_v).then_inc(small_loaded_z_stored, 16)

            def before_tile(t, last_tile):
                if not last_tile:
                    sp.wait_ge(xn_ready, t * TT + TT)
                    sp.dma_start(x_in[:, :, :], rows_of(t * TILE + TILE)).then_inc(x_loaded, 16)

            def step(s):
                if not s.att:
                    return
                for h in range(2):
                    banks.wait_moved(sp, s.runs_z, ("z", h))
                for half, z in enumerate((z_hi, z_lo)):
                    sp.dma_start(z_scratch[half, bass.ds(s.pair * 2, 2), :, bass.ds(s.first_token, TILE)].rearrange("h d t -> d h t"),
                                 z[:, :, :]).then_inc(small_loaded_z_stored, 16)

            for_each_step(nc.sync, before_tile, step)
            sp.wait_ge(small_loaded_z_stored, 16 * (SMALL + 2 * NT * PAIRS))

        @block.gpsimd
        def _(pool):
            def step(s):
                if not s.proj:
                    return
                for w in range(2):
                    banks.wait_moved(pool, s.runs_proj, ("qk"[w], 1))
                    pool.tensor_tensor(rotated[0:HALF, w, 0, :], products[0:HALF, w, 0, :], products[0:HALF, w, 2, :], ALU.subtract)
                    pool.tensor_tensor(rotated[HALF:P, w, 1, :], products[HALF:P, w, 1, :], products[HALF:P, w, 3, :],
                                       ALU.add).then_inc(added_pool, 1)
            for_each_step(nc.gpsimd, lambda t, last_tile: None, step)

        @block.tensor
        def _(pe):
            def turn_xn(runs, nth):
                pe.wait_ge(xn_ready, nth * TT + TT)
                for k in (2, 3, 0, 1):
                    banks.wait_room(pe, runs, ("x", k))
                    for i in range(TT):
                        last = pe.transpose(psum_of(("x", k))[:, i * P:(i + 1) * P], xn[:, i, k * P:(k + 1) * P], ident[:, :])
                    banks.fills(last, ("x", k))

            turn_xn({}, 0)
            for k in range(KD):
                banks.wait_moved(pe, {}, ("x", k))
            pe.wait_ge(w_lo_done, len(blocks))
            xt = [(xt_hi[:, k, :], xt_lo[:, k, :]) for k in range(KD)]

            def project(s, w, half):
                unit = ("qk"[w], half)
                banks.wait_room(pe, s.runs_proj, unit)
                pair = s.next_pair
                cols = bass.ds(pair * DH + half * (WIDE // 2), DH)
                left = [(w_hi[:, w, k, cols], w_lo[:, w, k, cols]) for k in range(KD)]
                banks.fills(three_passes(pe, psum_of(unit), left, xt), unit)

            def step(s):
                if s.att:
                    pe.wait_ge(added_dve, s.a * 2 + 2)
                    pe.wait_ge(added_pool, s.a * 2 + 2)
                    for h in range(2):
                        unit = ("scores", h)
                        banks.wait_room(pe, s.runs_scores, unit)
                        for i in range(TT):
                            cols = slice(i * P, (i + 1) * P)
                            last = pe.matmul(psum_of(unit)[:, cols], rotated[:, 0, h, cols], rotated[:, 1, h, cols], start=True, stop=True)
                        banks.fills(last, unit)
                if s.turn_next:
                    turn_xn(s.runs_turn, s.turns)
                    for k in range(KD):
                        banks.wait_moved(pe, s.runs_turn, ("x", k))
                if s.proj:
                    project(s, 0, 0)
                    project(s, 0, 1)
                    project(s, 1, 0)
                if s.att:
                    for h in range(2):
                        unit = ("probs", h)
                        pe.wait_ge(probs_ready, s.a * 2 + (h + 1))
                        banks.wait_room(pe, s.runs_probs, unit)
                        for i in range(TT):
                            last = pe.transpose(psum_of(unit)[:, i * P:(i + 1) * P], probs[:, h, i, :], ident[:, :])
                        banks.fills(last, unit)
                if s.proj:
                    project(s, 1, 1)
                if s.att:
                    for half in range(2):
                        banks.wait_moved(pe, {"turn": s.turns, "proj": s.a}, ("v", half))
                    for h in range(2):
                        unit = ("z", h)
                        banks.wait_moved(pe, s.runs_probs, ("probs", h))
                        banks.wait_room(pe, s.runs_z, unit)
                        for i in range(TT):
                            last = pe.matmul(psum_of(unit)[:, i * P:(i + 1) * P], v[:, i, h * DH:(h + 1) * DH], probs_t[:, h, i, :],
                                             start=True, stop=True)
                        banks.fills(last, unit)
                if s.proj:
                    for half in range(2):
                        unit = ("v", half)
                        banks.wait_room(pe, s.runs_proj, unit)
                        pair_cols = bass.ds(s.next_pair * (2 * DH), 2 * DH)
                        right = [(w_hi[:, 2, k, pair_cols], w_lo[:, 2, k, pair_cols]) for k in range(KD)]
                        for i in range(2):
                            cols = slice((2 * half + i) * P, (2 * half + i + 1) * P)
                            last = three_passes(pe, psum_of(unit)[:, i * 2 * DH:(i + 1) * 2 * DH],
                                                [(xt_hi[:, k, cols], xt_lo[:, k, cols]) for k in range(KD)], right)
                        banks.fills(last, unit)

            for_each_step(nc.tensor, lambda t, last_tile: None, step)

        @block.scalar
        def _(act):
            def first_halves(runs):
                for k in (2, 3, 0, 1):
                    banks.wait_filled(act, runs, ("x", k))
                    act.activation(xt_hi[:, k, :], psum_of(("x", k)), ACT.Copy).then_inc(xt_hi_done, 1)

            first_halves({})
            for i, (w, k) in enumerate(blocks):
                act.wait_ge(loaded[i % 2], 16 * (i // 2 + 1))
                act.activation(w_hi[:, w, k, :], w_rows[:, i % 2, :], ACT.Copy, scale=WS).then_inc(w_hi_done, 1)

            def step(s):
                if s.turn_next:
                    first_halves(s.runs_turn)
                if s.att:
                    for h in range(2):
                        act.wait_ge(low_top_ready, s.a * 2 + (h + 1))
                        for i in range(TT):
                            last = act.activation(probs[:, h, i, :], masked[:, h, i, :], ACT.Exp, bias=low_top[:, h, i:i + 1],
                                                  scale=HEAD_SCALE, accum_out=total[:, h, i:i + 1])
                        last.then_inc(exp_done, 1)
                    for h in range(2):
                        unit = ("probs", h)
                        banks.wait_filled(act, s.runs_probs, unit)
                        banks.moves(act.activation(probs_t[:, h, :, :].rearrange("p i k -> p (i k)"), psum_of(unit), ACT.Copy), unit)
                    for h in range(2):
                        banks.wait_filled(act, s.runs_z, ("z", h))
                        if h == 0:
                            act.wait_ge(small_loaded_z_stored, s.a * 32 + 16 * SMALL)
                            act.nop(nofuse=True)
                        act.activation(z_hi[:, h, :], psum_of(("z", h)), ACT.Identity,
                                       bias=bias_v[:, bass.ds(s.pair * 2 + h, 1)]).then_inc(z_hi_done, 1)
                if s.proj:
                    for half in range(2):
                        unit = ("v", half)
                        banks.wait_filled(act, s.runs_proj, unit)
                        banks.moves(act.activation(v[:, 2 * half:2 * half + 2, :].rearrange("p i d -> p (i d)"), psum_of(unit), ACT.Copy,
                                                   scale=AS / (XS * WS)), unit)

            act.wait_ge(bias_scaled, 2)
            for_each_step(nc.scalar, lambda t, last_tile: None, step)

        @block.vector
        def _(dve):
            def second_halves(runs, nth):
                for n, k in enumerate((2, 3, 0, 1)):
                    dve.wait_ge(xt_hi_done, nth * KD + (n + 1))
                    banks.moves(dve.tensor_tensor(xt_lo[:, k, :], psum_of(("x", k)), xt_hi[:, k, :], ALU.subtract), ("x", k))

            dve.wait_ge(x_loaded, 16)
            layernorm(dve, 0, x_in, xn, stat, ln_step, xn_ready)
            second_halves({}, 0)
            for i, (w, k) in enumerate(blocks):
                dve.wait_ge(w_hi_done, i + 1)
                dve.scalar_tensor_tensor(w_lo[:, w, k, :], w_rows[:, i % 2, :], WS, w_hi[:, w, k, :],
                                         ALU.mult, ALU.subtract).then_inc(w_lo_done, 1)
            dve.wait_ge(small_loaded_z_stored, 16 * SMALL)
            dve.tensor_scalar(bias[:, :, :, :].rearrange("p a b q -> p (a b q)"), bias[:, :, :, :].rearrange("p a b q -> p (a b q)"),
                              XS * WS, None, ALU.mult).then_inc(bias_scaled, 1)
            dve.tensor_scalar(bias_v[:, :], bias_v[:, :], AS, None, ALU.mult).then_inc(bias_scaled, 1)
            dve.wait_ge(bias_scaled, 2)

            def by_sequence(ap):
                return ap.rearrange("p (s n) -> p s n", n=S)

            def table(t):
                return t[:, :].unsqueeze(1).broadcast_to([P, TILE // S, S])

            def before_tile(t, last_tile):
                if not last_tile:
                    dve.wait_ge(x_loaded, t * 16 + 32)
                    layernorm(dve, t + 1, x_in, xn, stat, ln_step, xn_ready)

            def rotate(s, w):
                for half, (first, second) in enumerate((((cos, 0), (sin, 1)), ((sin, 2), (cos, 3)))):
                    unit = ("qk"[w], half)
                    banks.wait_filled(dve, s.runs_proj, unit)
                    for tab, slot in (first, second):
                        last = dve.scalar_tensor_tensor(by_sequence(products[:, w, slot, :]), by_sequence(psum_of(unit)),
                                                        bias[:, w, half, bass.ds(s.next_pair, 1)], table(tab), ALU.add, ALU.mult)
                    banks.moves(last, unit)
                banks.wait_moved(dve, s.runs_proj, ("qk"[w], 1))
                dve.tensor_tensor(rotated[HALF:P, w, 0, :], products[0:HALF, w, 1, :], products[0:HALF, w, 3, :], ALU.add)
                dve.tensor_tensor(rotated[0:HALF, w, 1, :], products[HALF:P, w, 0, :], products[HALF:P, w, 2, :],
                                  ALU.subtract).then_inc(added_dve, 1)

            def step(s):
                if s.att:
                    for h in range(2):
                        unit = ("scores", h)
                        banks.wait_filled(dve, s.runs_scores, unit)
                        dve.nop(nofuse=True)
                        for i in range(TT):
                            last = dve.tensor_tensor_reduce(masked[:, h, i, :], psum_of(unit)[:, i * P:(i + 1) * P], mask[:, :], 1.0, LOWEST,
                                                            ALU.add, ALU.max, top[:, h, i:i + 1])
                        banks.moves(last, unit)
                        banks.wait_moved(dve, s.runs_scores, unit)
                        dve.tensor_scalar(low_top[:, h, :], top[:, h, :], -HEAD_SCALE, None, ALU.mult).then_inc(low_top_ready, 1)
                if s.turn_next:
                    second_halves(s.runs_turn, s.turns)
                if s.att:
                    for h in range(2):
                        dve.wait_ge(exp_done, s.a * 2 + (h + 1))
                        dve.reciprocal(inv_total[:, h, :], total[:, h, :]).then_inc(inv_done, 1)
                        dve.wait_ge(inv_done, s.a * 2 + (h + 1))
                        dve.tensor_tensor(probs[:, h, :, :], probs[:, h, :, :], inv_total[:, h, :].unsqueeze(2).broadcast_to([P, TT, P]),
                                          ALU.mult).then_inc(probs_ready, 1)
                if s.proj:
                    rotate(s, 0)
                    rotate(s, 1)
                if s.att:
                    for h in range(2):
                        dve.wait_ge(z_hi_done, s.a * 2 + (h + 1))
                        banks.moves(dve.scalar_tensor_tensor(z_lo[:, h, :], psum_of(("z", h)), bias_v[:, bass.ds(s.pair * 2 + h, 1)],
                                                             z_hi[:, h, :], ALU.add, ALU.subtract), ("z", h))

            for_each_step(nc.vector, before_tile, step)


ZW_UNSCALE = 1.0 / (AS * WS)
FS = 2.0 ** 6
HS = 1.0 / FS
FP4_AS_F16 = 2.0 ** 14
GU = 2 * FF
WORDS_GU, WORDS_DOWN = D // 8, FF // 8
WHOLE = P
REST = (WORDS_DOWN - WHOLE) // 16


def decode_fp4(dve, last, codes, sign, magnitude, shift):
    dve.tensor_scalar(sign, codes, 12 - shift, 0x8000, ALU.logical_shift_left, ALU.bitwise_and)
    if shift <= 9:
        last(dve.tensor_scalar(magnitude, codes, 9 - shift, 0x0E00, ALU.logical_shift_left, ALU.bitwise_and))
    else:
        last(dve.tensor_scalar(magnitude, codes, shift - 9, 0x0E00, ALU.logical_shift_right, ALU.bitwise_and))
    last(dve.tensor_tensor(sign, sign, magnitude, ALU.bitwise_or))


def ffn_weights(nc, gu_codes, gu_scales, down_codes, down_scales, shifts, w_o, gu_hi, gu_lo, down_hi, down_lo, wo_hi, wo_lo):
    with ExitStack() as ctx:
        def sb(name, shape, dt):
            return ctx.enter_context(nc.sbuf_tensor("fw_" + name, shape, dt))

        def sem(name):
            return ctx.enter_context(nc.semaphore("fw_" + name))

        codes = sb("codes", [P, GU], I32)
        gu_scale = sb("gu_scale", [P, GU], F16)
        down_c = sb("down_c", [P, 1 + REST, D], I32)
        down_scale = sb("down_scale", [P, 1 + REST, D], F16)
        shift = sb("shift", [P, 1], I32)
        sign, magnitude = sb("sign", [P, GU], I32), sb("magnitude", [P, GU], I32)
        value = sb("value", [P, 2, GU], F32)
        rows = sb("rows", [P, 2, 4 * D], F32)
        gu_loaded, down_loaded, step = sem("gu_loaded"), sem("down_loaded"), sem("step")
        rows_loaded = [sem("rows0_loaded"), sem("rows1_loaded")]
        hi_done, lo_done, value_ready = sem("hi_done"), sem("lo_done"), sem("value_ready")
        block = ctx.enter_context(nc.Block())

        jobs = [(codes[:, :], 4 * j, gu_scale[:, :], gu_hi[:, j, :], gu_lo[:, j, :]) for j in range(4)]
        jobs += [(down_c[:, 0, :], 4 * j, down_scale[:, 0, :], down_hi[:, j, :], down_lo[:, j, :]) for j in range(8)]
        jobs += [(down_c[:, 1 + q, :], 0, down_scale[:, 1 + q, :], down_hi[:, 8 + q, :], down_lo[:, 8 + q, :]) for q in range(REST)]
        NW = 4
        GU_LOADS, DOWN_LOADS = 2 + 8, 1 + REST + 8 + REST + 1

        @block.sync
        def _(sp):
            for u in range(2):
                sp.dma_start(codes[u * 64:(u + 1) * 64, :], gu_codes).then_inc(gu_loaded, 16)
                for g in range(4):
                    first = u * 64 + g * 16
                    sp.dma_start(gu_scale[first:first + 16, :], gu_scales[g:g + 1, :].broadcast_to([16, GU])).then_inc(gu_loaded, 16)
            sp.dma_start(shift[:, :], shifts).then_inc(down_loaded, 16)
            sp.dma_start(down_c[:, 0, :], down_codes[0:WHOLE, :]).then_inc(down_loaded, 16)
            for g in range(8):
                sp.dma_start(down_scale[16 * g:16 * g + 16, 0, :], down_scales[g:g + 1, :].broadcast_to([16, D])).then_inc(down_loaded, 16)
            for q in range(REST):
                words = down_codes[WHOLE + 16 * q:WHOLE + 16 * q + 16, :]
                sp.dma_start(down_c[:, 1 + q, :], words.unsqueeze(0).broadcast_to([8, 16, D])).then_inc(down_loaded, 16)
                sp.dma_start(down_scale[:, 1 + q, :], down_scales[8 + q:9 + q, :].broadcast_to([P, D])).then_inc(down_loaded, 16)
            for i in range(NW):
                if i >= 2:
                    sp.wait_ge(lo_done, i - 1)
                sp.dma_start(rows[:, i % 2, :].rearrange("p (n m) -> p n m", n=4),
                             w_o[4 * i:4 * i + 4, :, :].rearrange("n d m -> d n m")).then_inc(rows_loaded[i % 2], 16)

        @block.scalar
        def _(act):
            def whole(i):
                act.wait_ge(rows_loaded[i % 2], 16 * (i // 2 + 1))
                act.activation(wo_hi[:, 4 * i:4 * i + 4, :].rearrange("p n m -> p (n m)"), rows[:, i % 2, :], ACT.Copy,
                               scale=WS).then_inc(hi_done, 1)
            for i in range(NW):
                whole(i)
            for n, (_, _, _, hi, _) in enumerate(jobs):
                act.wait_ge(value_ready, n + 1)
                act.activation(hi, value[:, n % 2, 0:hi.shape[-1]], ACT.Copy).then_inc(hi_done, 1)

        @block.vector
        def _(dve):
            n = [0]

            def last(ins):
                n[0] += 1
                ins.then_inc(step, 1)
                dve.wait_ge(step, n[0])

            def second_half(job):
                _, _, _, hi, lo = jobs[job]
                dve.wait_ge(hi_done, NW + job + 1)
                dve.tensor_tensor(lo, value[:, job % 2, 0:hi.shape[-1]], hi, ALU.subtract).then_inc(lo_done, 1)

            for i in range(NW):
                dve.wait_ge(hi_done, i + 1)
                dve.scalar_tensor_tensor(wo_lo[:, 4 * i:4 * i + 4, :].rearrange("p n m -> p (n m)"), rows[:, i % 2, :], WS,
                                         wo_hi[:, 4 * i:4 * i + 4, :].rearrange("p n m -> p (n m)"), ALU.mult, ALU.subtract).then_inc(lo_done, 1)
            dve.wait_ge(gu_loaded, 16 * GU_LOADS)
            last(dve.tensor_scalar(codes[64:P, :], codes[64:P, :], 16, None, ALU.logical_shift_right))
            for job, (c, bit, scale, hi, lo) in enumerate(jobs):
                if job == 4:
                    dve.wait_ge(down_loaded, 16 * DOWN_LOADS)
                    for q in range(REST):
                        last(dve.tensor_scalar(down_c[:, 1 + q, :], down_c[:, 1 + q, :], shift[:, 0:1], None, ALU.logical_shift_right))
                w = hi.shape[-1]
                if bit > 12:
                    last(dve.tensor_scalar(magnitude[:, GU - w:GU], c, 16, None, ALU.logical_shift_right))
                    c, bit = magnitude[:, GU - w:GU], bit - 16
                if job:
                    dve.wait_ge(value_ready, job)
                decode_fp4(dve, last, c, sign[:, 0:w], magnitude[:, 0:w], bit)
                as_f16 = sign[:, 0:w].bitcast(F16).rearrange("p (n two) -> p n two", two=2)[:, :, 0]
                if job >= 2:
                    dve.wait_ge(lo_done, NW + job - 1)
                dve.scalar_tensor_tensor(value[:, job % 2, 0:w], as_f16, FP4_AS_F16 * FS, scale, ALU.mult, ALU.mult).then_inc(value_ready, 1)
                if job:
                    second_half(job - 1)
            second_half(len(jobs) - 1)


def ffn_phase(nc, psum, ident, z_scratch, x1_rows, w_o, b_o, gu_codes, gu_scales, down_codes, down_scales, shifts, out_rows):
    with ExitStack() as ctx:
        def sb(name, shape, dt):
            return ctx.enter_context(nc.sbuf_tensor("ff_" + name, shape, dt))

        def sem(name):
            return ctx.enter_context(nc.semaphore("ff_" + name))

        gu_hi, gu_lo = sb("gu_hi", [P, KD, GU], F16), sb("gu_lo", [P, KD, GU], F16)
        down_hi, down_lo = sb("down_hi", [P, FB, D], F16), sb("down_lo", [P, FB, D], F16)
        wo_hi, wo_lo = sb("wo_hi", [P, HEADS, D], F16), sb("wo_lo", [P, HEADS, D], F16)
        ffn_weights(nc, gu_codes, gu_scales, down_codes, down_scales, shifts, w_o, gu_hi, gu_lo, down_hi, down_lo, wo_hi, wo_lo)

        z_hi, z_lo = sb("z_hi", [P, HEADS, TILE], F16), sb("z_lo", [P, HEADS, TILE], F16)
        x1 = sb("x1", [P, TT, D], F32)
        x2_next, x2 = sb("x2_next", [P, TT, D], F32), sb("x2", [P, TT, D], F32)
        xn = sb("xn", [P, TT, D], F32)
        xt_hi, xt_lo = sb("xt_hi", [P, KD, TILE], F16), sb("xt_lo", [P, KD, TILE], F16)
        gate = sb("gate", [P, 2, TILE], F32)
        hidden = sb("hidden", [P, 2, TILE], F32)
        h_hi, h_lo = sb("h_hi", [P, FB, TILE], F16), sb("h_lo", [P, FB, TILE], F16)
        b_o_all = sb("b_o_all", [P, D], F32)
        squares = sb("squares", [P, TT], F32)
        stat = stat_buffers(sb)
        rms = {k: sb("rms_" + k, [P, TT], I32 if k == "half" else F32) for k in ("var", "half", "y", "y2")}

        b_loaded, z_loaded, x1_loaded, out_stored = sem("b_loaded"), sem("z_loaded"), sem("x1_loaded"), sem("out_stored")
        x1_ready, x2_copied = sem("x1_ready"), sem("x2_copied")
        ln_step, xn_ready, xt_hi_done = sem("ln_step"), sem("xn_ready"), sem("xt_hi_done")
        h_hi_done, h_lo_done = sem("h_hi_done"), sem("h_lo_done")
        squares_done, rms_step = sem("squares_done"), sem("rms_step")

        warm = [(("warm", i), i) for i in range(4)]
        turn = [(("x", k), 4 + k) for k in range(KD)]
        merge = [(("merge", i), 4 + i) for i in range(TT)]
        hid = [((kind, b), (2 * b + (kind == "up")) % 8) for b in range(FB) for kind in ("gate", "up")]
        banks = Banks(nc, ctx, "ff", warm + merge + turn,
                      hid + merge + [(("y", i), i) for i in range(TT - 1)] + turn + [(("y", TT - 1), TT - 1)])

        def psum_of(t, unit):
            return psum[:, banks.bank(t, unit), :]

        def rows_of(tensor, first):
            return tensor[bass.ds(first, TILE), :].rearrange("(b p) d -> p b d", p=P)

        block = ctx.enter_context(nc.Block())

        @block.sync
        def _(sp):
            def load(first):
                for half, z in enumerate((z_hi, z_lo)):
                    sp.dma_start(z[:, :, :], z_scratch[half, :, :, bass.ds(first, TILE)].rearrange("h d t -> d h t")).then_inc(z_loaded, 16)
                sp.dma_start(x1[:, :, :], rows_of(x1_rows, first)).then_inc(x1_loaded, 16)

            sp.dma_start(b_o_all[:, :], b_o.broadcast_to([P, D])).then_inc(b_loaded, 16)
            load(0)

            def tile(t, last_tile):
                if not last_tile:
                    sp.wait_ge(xn_ready, t * TT + TT)
                    load(t * TILE + TILE)
                banks.wait_moved(sp, t, ("y", TT - 1))
                sp.dma_start(rows_of(out_rows, t * TILE), x2[:, :, :]).then_inc(out_stored, 16)

            with nc.sync.Fori(0, NT - 1) as t:
                tile(t, False)
            tile(NT - 1, True)
            sp.wait_ge(out_stored, 16 * NT)

        @block.gpsimd
        def _(pool):
            def add_bias(nth):
                pool.wait_ge(x1_loaded, nth * 16 + 16)
                for i in range(TT):
                    pool.tensor_tensor(x1[:, i, :], x1[:, i, :], b_o_all[:, :], ALU.add).then_inc(x1_ready, 1)

            def copy_x2(nth):
                pool.wait_ge(xn_ready, nth * TT + TT)
                pool.nop(nofuse=True)
                pool.tensor_copy(x2[:, :, :], x2_next[:, :, :]).then_inc(x2_copied, 1)

            pool.wait_ge(b_loaded, 16)
            add_bias(0)
            copy_x2(0)

            def tile(t, last_tile):
                if not last_tile:
                    add_bias(t + 1)
                for b in range(FB):
                    pool.wait_ge(h_hi_done, t * FB + (b + 1))
                    pool.tensor_tensor(h_lo[:, b, :], hidden[:, b % 2, :], h_hi[:, b, :], ALU.subtract).then_inc(h_lo_done, 1)
                if not last_tile:
                    pool.wait_ge(out_stored, t * 16 + 16)
                    copy_x2(t + 1)

            with nc.gpsimd.Fori(0, NT - 1) as t:
                tile(t, False)
            tile(NT - 1, True)

        @block.tensor
        def _(pe):
            def block_of(i):
                return slice(i * P, (i + 1) * P)

            def turn_xn(t, nth):
                pe.wait_ge(xn_ready, nth * TT + TT)
                for k in range(KD):
                    banks.wait_room(pe, t, ("x", k))
                    for i in range(TT):
                        last = pe.transpose(psum_of(t, ("x", k))[:, block_of(i)], xn[:, i, block_of(k)], ident[:, :])
                    banks.fills(last, t, ("x", k))

            def project(t, unit, left, right):
                banks.wait_room(pe, t, unit)
                banks.fills(three_passes(pe, psum_of(t, unit), left, right), t, unit)

            def merge_heads(t, nth):
                pe.wait_ge(z_loaded, nth * 32 + 32)
                for i in range(TT):
                    project(t, ("merge", i), [(z_hi[:, n, block_of(i)], z_lo[:, n, block_of(i)]) for n in range(HEADS)],
                            [(wo_hi[:, n, :], wo_lo[:, n, :]) for n in range(HEADS)])

            for unit, _ in warm:
                last = pe.transpose(psum_of(None, unit)[:, 0:P], ident[:, :], ident[:, :])
                banks.fills(last, None, unit)
            merge_heads(None, 0)
            turn_xn(None, 0)

            def tile(t, last_tile):
                for k in range(KD):
                    banks.wait_moved_before(pe, t, ("x", k))
                for b in range(FB):
                    for first, kind in ((0, "gate"), (FF, "up")):
                        cols = slice(first + b * P, first + (b + 1) * P)
                        project(t, (kind, b), [(gu_hi[:, k, cols], gu_lo[:, k, cols]) for k in range(KD)],
                                [(xt_hi[:, k, :], xt_lo[:, k, :]) for k in range(KD)])
                if not last_tile:
                    merge_heads(t, t + 1)
                pe.wait_ge(h_lo_done, t * FB + FB)
                for i in range(TT):
                    if i == TT - 1 and not last_tile:
                        turn_xn(t, t + 1)
                    project(t, ("y", i), [(h_hi[:, b, block_of(i)], h_lo[:, b, block_of(i)]) for b in range(FB)],
                            [(down_hi[:, b, :], down_lo[:, b, :]) for b in range(FB)])

            with nc.tensor.Fori(0, NT - 1) as t:
                tile(t, False)
            tile(NT - 1, True)

        @block.scalar
        def _(act):
            def first_halves(t):
                for k in range(KD):
                    banks.wait_filled(act, t, ("x", k))
                    act.activation(xt_hi[:, k, :], psum_of(t, ("x", k)), ACT.Copy).then_inc(xt_hi_done, 1)

            for i, (unit, _) in enumerate(warm):
                banks.wait_filled(act, None, unit)
                banks.moves(act.activation(gate[:, 0, i:i + 1], psum_of(None, unit)[:, 0:1], ACT.Copy), None, unit)
            first_halves(None)

            def tile(t, last_tile):
                def hidden_first_half(b):
                    banks.wait_moved(act, t, ("up", b))
                    act.activation(h_hi[:, b, :], hidden[:, b % 2, :], ACT.Copy).then_inc(h_hi_done, 1)

                for b in range(FB):
                    banks.wait_filled(act, t, ("gate", b))
                    banks.moves(act.activation(gate[:, b % 2, :], psum_of(t, ("gate", b)), ACT.Silu, scale=1.0 / (XS * FS)), t, ("gate", b))
                    if b:
                        hidden_first_half(b - 1)
                hidden_first_half(FB - 1)
                for i in range(TT):
                    if i == TT - 1 and not last_tile:
                        first_halves(t)
                    if i >= 2:
                        act.wait_ge(squares_done, t * TT + (i - 1))
                    banks.wait_filled(act, t, ("y", i))
                    act.activation(gate[:, i % 2, :], psum_of(t, ("y", i)), ACT.Square,
                                   accum_out=squares[:, i:i + 1]).then_inc(squares_done, 1)

            with nc.scalar.Fori(0, NT - 1) as t:
                tile(t, False)
            tile(NT - 1, True)

        @block.vector
        def _(dve):
            def second_halves(t, nth):
                for k in range(KD):
                    dve.wait_ge(xt_hi_done, nth * KD + (k + 1))
                    banks.moves(dve.tensor_tensor(xt_lo[:, k, :], psum_of(t, ("x", k)), xt_hi[:, k, :], ALU.subtract), t, ("x", k))

            def merge_and_normalise(t, nth):
                if t is not None:
                    dve.wait_ge(x2_copied, nth)
                for i in range(TT):
                    dve.wait_ge(x1_ready, nth * TT + (i + 1))
                    banks.wait_filled(dve, t, ("merge", i))
                    banks.moves(dve.scalar_tensor_tensor(x2_next[:, i, :], psum_of(t, ("merge", i)), ZW_UNSCALE, x1[:, i, :],
                                                         ALU.mult, ALU.add), t, ("merge", i))
                for i in range(TT):
                    banks.wait_moved(dve, t, ("merge", i))
                layernorm(dve, nth, x2_next, xn, stat, ln_step, xn_ready, by_code=True)

            merge_and_normalise(None, 0)
            second_halves(None, 0)

            def tile(t, last_tile):
                for b in range(FB):
                    banks.wait_moved(dve, t, ("gate", b))
                    banks.wait_filled(dve, t, ("up", b))
                    if b >= 2:
                        dve.wait_ge(h_lo_done, t * FB + (b - 1))
                    banks.moves(dve.scalar_tensor_tensor(hidden[:, b % 2, :], psum_of(t, ("up", b)), HS / (XS * FS), gate[:, b % 2, :],
                                                         ALU.mult, ALU.mult), t, ("up", b))
                if not last_tile:
                    merge_and_normalise(t, t + 1)
                    second_halves(t, t + 1)
                dve.wait_ge(squares_done, t * TT + TT)
                n = [0]

                def done(ins):
                    ins.then_inc(rms_step, 1)
                    n[0] += 1
                    dve.wait_ge(rms_step, t * RMS_STEPS + n[0])
                done(dve.tensor_scalar(rms["var"][:, :], squares[:, :], 1.0 / D, RMS_EPS, ALU.mult, ALU.add))
                inverse_root(dve, rms, done)
                assert n[0] == RMS_STEPS
                dve.wait_ge(x2_copied, t + 1)
                for i in range(TT):
                    banks.moves(dve.scalar_tensor_tensor(x2[:, i, :], psum_of(t, ("y", i)), rms["y"][:, i:i + 1], x2[:, i, :],
                                                         ALU.mult, ALU.add), t, ("y", i))

            with nc.vector.Fori(0, NT - 1) as t:
                tile(t, False)
            tile(NT - 1, True)


def whole_kernel(nc, x, ctx_2048, wq, wk, wv, wo, w_q, b_q, w_k, b_k, w_v, b_v, w_o, b_o, gu_codes, gu_scales, down_codes,
                 down_scales, identity, own_new, causal, rope_cos, rope_sin, shifts, out):
    x1 = nc.dram_tensor("x1_scratch", (TOK, D), F32).ap()
    z = nc.dram_tensor("z_scratch", (2, HEADS, DH, TOK), F16).ap()
    with ExitStack() as ctx:
        psum = ctx.enter_context(nc.psum_tensor("psum", [P, 8, 512], F32))
        ident = ctx.enter_context(nc.sbuf_tensor("ident", [P, P], F32))
        with nc.semaphore("identity_loaded") as identity_loaded, nc.Block() as block:
            @block.sync
            def _(sp):
                sp.dma_start(ident[:, :], identity).then_inc(identity_loaded, 16)
                sp.wait_ge(identity_loaded, 16)
        xattn_phase(nc, psum, ident, x.rearrange("b s d -> (b s) d"), ctx_2048.rearrange("b k d -> (b k) d"), wq, wk, wv, wo,
                    own_new, x1)
        heads_phase(nc, psum, ident, x1, w_q, w_k, w_v, b_q, b_k, b_v, rope_cos, rope_sin, causal, z)
        ffn_phase(nc, psum, ident, z, x1, w_o, b_o, gu_codes, gu_scales, down_codes, down_scales, shifts,
                  out.rearrange("b s d -> (b s) d"))


_INS = ["x", "ctx_2048", "L0_xattn_wq", "L0_xattn_wk", "L0_xattn_wv", "L0_xattn_wo",
        "L0_attn_W_Q", "L0_attn_b_Q", "L0_attn_W_K", "L0_attn_b_K", "L0_attn_W_V", "L0_attn_b_V", "L0_attn_W_O", "L0_attn_b_O",
        "L0_ffn_gate_up_packed", "L0_ffn_gate_up_scales", "L0_ffn_down_packed", "L0_ffn_down_scales"]


def _constants():
    import numpy as np
    own_new = np.zeros((P, KV + P), np.float32)
    at = np.arange(P)
    own = at[:, None] // S == at[None, :] // S
    own_new[:, KV:] = np.where(own, 0.0, -1.0e30)
    causal = np.where(own & (at[None, :] <= at[:, None]), 0.0, -1.0e30).astype(np.float32)
    inv_freq = (1.0 / np.float32(10000.0) ** (np.arange(0, DH, 2, dtype=np.float32) / np.float32(DH))).astype(np.float32)
    freqs = np.outer(inv_freq, np.arange(S, dtype=np.float32)).astype(np.float32)
    unscale = np.float32(1.0 / (XS * WS))
    rope = {f"rope_{f.__name__}": np.tile(f(freqs).astype(np.float32) * unscale, (2, 1)) for f in (np.cos, np.sin)}
    shifts = (4 * (at // 16)).astype(np.int32)[:, None]
    return {"identity": np.eye(P, dtype=np.float32), "own_new": own_new, "causal": causal, **rope, "shifts": shifts}


def _hidden_order():
    import numpy as np
    at = np.arange(P)
    whole = [8 * at + j for j in range(8)]
    rest = [8 * (WHOLE + 16 * q + at % 16) + at // 16 for q in range(REST)]
    return np.concatenate(whole + rest)


def _laid_out(name, a):
    import numpy as np
    a = np.asarray(a)
    if name.startswith("L0_xattn_w"):
        return a.T
    if name in ("L0_attn_W_Q", "L0_attn_W_K"):
        return a.reshape(HEADS, D, HALF, 2).transpose(1, 3, 0, 2).reshape(D, HEADS * DH)
    if name == "L0_attn_W_V":
        return a.transpose(1, 0, 2).reshape(D, HEADS * DH)
    if name in ("L0_attn_b_Q", "L0_attn_b_K"):
        return a.reshape(PAIRS, 2, HALF, 2).transpose(1, 2, 3, 0).reshape(P, 2, PAIRS)
    if name == "L0_attn_b_V":
        return a.T
    if name == "L0_attn_b_O":
        return a[None, :]
    both = np.concatenate([_hidden_order(), FF + _hidden_order()])
    if name == "L0_ffn_gate_up_packed":
        return a[both].T
    if name == "L0_ffn_gate_up_scales":
        return a[:, both]
    if name == "L0_ffn_down_packed":
        return a.T
    return a


def kernel(**inputs):
    import numpy as _np
    import concourse.bacc as _bacc
    from concourse import mybir as _mybir
    from concourse.bass_utils import run_bass_kernel_spmd as _run

    nc = _bacc.Bacc("TRN2", target_bir_lowering=False, num_devices=1)
    arrays, args = {}, []
    for name, a in [(n, _laid_out(n, inputs[n])) for n in _INS] + list(_constants().items()):
        a = _np.ascontiguousarray(a)
        arrays[f"in_{name}_dram"] = a
        args.append(nc.dram_tensor(f"in_{name}_dram", a.shape, _mybir.dt.from_np(a.dtype), kind="ExternalInput").ap())
    out = nc.dram_tensor("out_0_dram", (B, S, D), F32, kind="ExternalOutput").ap()
    whole_kernel(nc, *args, out)
    r = _run(nc, [arrays], core_ids=[0])
    return r.results[0]["out_0_dram"]
```

```python
from contextlib import ExitStack

import concourse.bass as bass
from concourse import mybir

F32 = mybir.dt.float32
F16 = mybir.dt.float16
I32 = mybir.dt.int32
ALU = mybir.AluOpType
ACT = mybir.ActivationFunctionType

P = 128
B, S, D = 32, 64, 512
KV = 256
TOK = B * S
TILE = 512
NT = TOK // TILE
TT = TILE // P
KD = D // P
HEADS, DH = 16, 128
HALF = DH // 2
PAIRS = HEADS // 2
FF = 1408
FB = FF // P
LN_EPS = 1e-5
RMS_EPS = 1e-6
LOWEST = -3.0e38

XS = 2.0 ** 8
WS = 2.0 ** 11
AS = 2.0 ** 6
XATTN_SCALE = float(D) ** -0.5
HEAD_SCALE = float(DH) ** -0.5
RSQRT_MAGIC = 0x5F3759DF


class Banks:

    def __init__(self, nc, ctx, name, before, body):
        self.filled = [ctx.enter_context(nc.semaphore(f"{name}_bank{b}_filled")) for b in range(8)]
        self.moved = [ctx.enter_context(nc.semaphore(f"{name}_bank{b}_moved")) for b in range(8)]
        self.ahead, self.uses, self.at = [0] * 8, [0] * 8, {}
        for unit, bank in before:
            self.at["before", unit] = (bank, self.ahead[bank])
            self.ahead[bank] += 1
        for unit, bank in body:
            self.at["body", unit] = (bank, self.uses[bank])
            self.uses[bank] += 1

    def place(self, t, unit):
        if t is None:
            return self.at["before", unit]
        bank, k = self.at["body", unit]
        return bank, t * self.uses[bank] + (self.ahead[bank] + k)

    def bank(self, t, unit):
        return self.place(t, unit)[0]

    def wait_room(self, pe, t, unit):
        bank, earlier = self.place(t, unit)
        if not (isinstance(earlier, int) and earlier == 0):
            pe.wait_ge(self.moved[bank], earlier)

    def wait_filled(self, eng, t, unit):
        bank, earlier = self.place(t, unit)
        eng.wait_ge(self.filled[bank], earlier + 1)

    def wait_moved(self, eng, t, unit):
        bank, earlier = self.place(t, unit)
        eng.wait_ge(self.moved[bank], earlier + 1)

    def before(self, t, unit):
        bank, k = self.at["body", unit]
        behind = self.ahead[bank] + k + 1 - self.uses[bank]
        assert behind >= 0
        return bank, t * self.uses[bank] + behind

    def wait_filled_before(self, eng, t, unit):
        bank, count = self.before(t, unit)
        eng.wait_ge(self.filled[bank], count)

    def wait_moved_before(self, eng, t, unit):
        bank, count = self.before(t, unit)
        eng.wait_ge(self.moved[bank], count)

    def fills(self, ins, t, unit):
        ins.then_inc(self.filled[self.bank(t, unit)], 1)

    def moves(self, ins, t, unit):
        ins.then_inc(self.moved[self.bank(t, unit)], 1)


ROOT_STEPS = 2 + 9
LN_STEPS = 2 * TT + 1 + ROOT_STEPS + 1
RMS_STEPS = 1 + ROOT_STEPS


def inverse_root(dve, stat, done):
    var, half, y, y2 = stat["var"], stat["half"], stat["y"], stat["y2"]
    done(dve.tensor_scalar(half[:, :], var[:, :].bitcast(I32), 1, None, ALU.logical_shift_right))
    done(dve.tensor_scalar(y[:, :].bitcast(I32), half[:, :], -1, RSQRT_MAGIC, ALU.mult, ALU.add))
    for _ in range(3):
        done(dve.tensor_tensor(y2[:, :], y[:, :], y[:, :], ALU.mult))
        done(dve.scalar_tensor_tensor(y2[:, :], y2[:, :], -0.5, var[:, :], ALU.mult, ALU.mult))
        done(dve.scalar_tensor_tensor(y[:, :], y2[:, :], 1.5, y[:, :], ALU.add, ALU.mult))


def layernorm(dve, t, src, dst, stat, step, ready, by_code=False, parts=(1, 2)):
    n = [0]

    def all_done():
        dve.wait_ge(step, t * LN_STEPS + n[0])
        if not isinstance(t, int):
            dve.nop(nofuse=True)

    def done(ins, wait=True):
        ins.then_inc(step, 1)
        n[0] += 1
        if wait:
            all_done()

    if 1 in parts:
        for i in range(TT):
            done(dve.bn_stats(stat["six"][:, i, :], src[:, i, :]), wait=(i == TT - 1))
        for i in range(TT):
            done(dve.bn_aggr(stat["meanvar"][:, i, :], stat["six"][:, i, :]), wait=(i == TT - 1))
    if 2 not in parts:
        return
    n[0] = 2 * TT
    done(dve.tensor_scalar(stat["var"][:, :], stat["meanvar"][:, :, 1], LN_EPS, None, ALU.add))
    inverse_root(dve, stat, done)
    y = stat["y"]
    done(dve.tensor_scalar(y[:, :], y[:, :], XS, None, ALU.mult))
    for i in range(TT):
        to, from_ = dst[:, i, :], src[:, i, :]
        if by_code:
            to = to.rearrange("p (j u w) -> p j u w", j=4, u=2)
            from_ = from_.rearrange("p (w u j) -> p j u w", j=4, u=2)
        dve.tensor_scalar(to, from_, stat["meanvar"][:, i, 0:1], y[:, i:i + 1], ALU.subtract, ALU.mult).then_inc(ready, 1)
    assert n[0] == LN_STEPS


def three_passes(pe, out, left, right):
    k = len(left)
    for i in range(k):
        (lh, ll), (rh, rl) = left[i], right[i]
        pe.matmul(out, lh, rh, start=(i == 0), stop=False)
        pe.matmul(out, lh, rl, start=False, stop=False)
        last = pe.matmul(out, ll, rh, start=False, stop=(i == k - 1))
    return last


def stat_buffers(sb):
    return {"six": sb("ln_six", [P, TT, 6], F32), "meanvar": sb("ln_meanvar", [P, TT, 2], F32),
            "var": sb("ln_var", [P, TT], F32), "half": sb("ln_half", [P, TT], I32),
            "y": sb("ln_y", [P, TT], F32), "y2": sb("ln_y2", [P, TT], F32)}


def xattn_phase(nc, psum, ident, x_rows, ctx_kv, wq, wk, wv, wo, own_new, x1_rows, w_hi, w_lo, w_rows, xn, stat,
                head_weights, hqk_hi, hqk_lo):
    with ExitStack() as ctx:
        def sb(name, shape, dt):
            return ctx.enter_context(nc.sbuf_tensor("xa_" + name, shape, dt))

        def sem(name):
            return ctx.enter_context(nc.semaphore("xa_" + name))

        xt_hi, xt_lo = sb("xt_hi", [P, KD, TILE], F16), sb("xt_lo", [P, KD, TILE], F16)
        q_t, k_t = sb("q_t", [P, KD, TILE], F32), sb("k_t", [P, KD, TILE], F32)
        att = q_t
        v_new = sb("v_new", [P, TT, D], F32)
        kv = sb("kv", [P, TT, 4, D], F32)
        kv_t = sb("kv_t", [P, KD, 2 * KV], F32)
        mask = sb("mask", [P, KV + P], F32)
        probs = sb("probs", [P, KV + P], F32)
        probs_t = sb("probs_t", [P, 3, P], F32)
        top, low_top = sb("top", [P, TT], F32), sb("low_top", [P, TT], F32)
        total, inv_total = sb("total", [P, TT], F32), sb("inv_total", [P, TT], F32)
        att_hi, att_lo = sb("att_hi", [P, KD, P], F16), sb("att_lo", [P, KD, P], F16)
        x1 = sb("x1", [P, TT, D], F32)

        ones = sb("ones", [P, 1], F32)

        rows_loaded = [sem("rows0_loaded"), sem("rows1_loaded")]
        x_loaded, res_loaded = sem("x_loaded"), sem("res_loaded")
        kv_loaded = [sem(f"kv{p}_loaded") for p in range(TT)]
        head_step, ones_set = sem("head_step"), sem("ones_set")
        w_hi_done, w_lo_done, ln_step, xn_ready, xt_hi_done = sem("w_hi_done"), sem("w_lo_done"), sem("ln_step"), sem("xn_ready"), sem("xt_hi_done")
        low_top_ready, exp_done = sem("low_top_ready"), sem("exp_done")
        inv_ready, att_hi_done = sem("inv_ready"), sem("att_hi_done")
        mask_loaded_x1_stored = sem("mask_loaded_x1_stored")

        turn_x = [(("x", k), 4 + k) for k in range(KD)]
        warm = [(("warm", i), i % 4) for i in range(8)]
        before = warm + turn_x
        body = [(("q", e), e) for e in range(4)] + [(("k", e), 4 + e) for e in range(4)] + [(("v", p), p) for p in range(TT)]
        def turn_kv(p):
            return [(("kv", p, k), 4 + k) for k in range(KD)]

        body += turn_kv(0)
        for p in range(TT):
            body += [(("scores", p), 0)]
            body += [(("turn", p - 1), 3)] if p else []
            body += turn_kv(p + 1) if p + 1 < TT else turn_x
            body += [(("probs", p), 1)]
            body += [(("out", p - 1), 3)] if p else []
            body += [(("att", p), 2)]
        body += [(("turn", TT - 1), 3), (("out", TT - 1), 3)]
        banks = Banks(nc, ctx, "xa", before, body)

        def psum_of(t, unit, n=512):
            return psum[:, banks.bank(t, unit), 0:n]

        def rows_of(tensor, first, n):
            return tensor[bass.ds(first, n), :].rearrange("(b p) d -> p b d", p=P)

        block = ctx.enter_context(nc.Block())

        @block.sync
        def _(sp):
            def load_kv(t, p):
                for s in range(2):
                    sp.dma_start(kv[:, p, 2 * s:2 * s + 2, :],
                                 ctx_kv[bass.ds(t * (2 * TT * KV) + (2 * p + s) * KV, KV), :]
                                 .rearrange("(b p) d -> p b d", p=P)).then_inc(kv_loaded[p], 16)

            sp.dma_start(xn[:, :, :], rows_of(x_rows, 0, TILE)).then_inc(x_loaded, 16)
            for i, w in enumerate((wq, wk, wv, wo)):
                if i >= 2:
                    sp.wait_ge(w_lo_done, KD * (i - 1))
                sp.dma_start(w_rows[:, i % 2, :].rearrange("p (b d) -> p b d", d=D), rows_of(w, 0, D)).then_inc(rows_loaded[i % 2], 16)
                if i == 1:
                    load_kv(0, 0)
            for p in range(1, TT):
                load_kv(0, p)
            sp.dma_start(x1[:, :, :], rows_of(x_rows, 0, TILE)).then_inc(res_loaded, 16)

            def load_head_weights(t):
                sp.wait_ge(w_lo_done, t * 2 + 4 * KD)
                sp.nop(nofuse=True)
                for i in range(2):
                    sp.dma_start(w_rows[:, i, :], head_weights[bass.ds(t * (2 * P) + i * P, P), :]).then_inc(rows_loaded[i], 16)

            def tile(t, last_tile):
                if not last_tile:
                    sp.wait_ge(xt_hi_done, t * KD + KD)
                    sp.dma_start(xn[:, :, :], rows_of(x_rows, t * TILE + TILE, TILE)).then_inc(x_loaded, 16)
                else:
                    sp.wait_ge(mask_loaded_x1_stored, 16 + 16 * TT * (NT - 1))
                    sp.wait_ge(xt_hi_done, NT * KD)
                    sp.dma_start(xn[:, :, :], rows_of(x1_rows, 0, TILE)).then_inc(x_loaded, 16)
                load_head_weights(t)
                if last_tile:
                    return
                for p in range(TT):
                    banks.wait_filled(sp, t, ("att", p))
                    load_kv(t + 1, p)
                sp.wait_ge(mask_loaded_x1_stored, t * (16 * TT) + (16 * TT + 16))
                sp.nop(nofuse=True)
                sp.dma_start(x1[:, :, :], rows_of(x_rows, t * TILE + TILE, TILE)).then_inc(res_loaded, 16)

            with nc.sync.Fori(0, NT - 1) as t:
                tile(t, False)
            tile(NT - 1, True)
            sp.wait_ge(w_lo_done, 4 * KD + 2 * KD)
            for i in range(2):
                sp.dma_start(w_rows[:, i, :], head_weights[(2 * KD + i) * P:(2 * KD + i + 1) * P, :]).then_inc(rows_loaded[i], 16)
                sp.wait_ge(rows_loaded[i], 16 * (2 + NT + 1))

        @block.gpsimd
        def _(pool):
            pool.memset(ones[:, :], 1.0).then_inc(ones_set, 1)
            pool.wait_ge(ones_set, 1)
            pool.dma_start(mask[:, :], own_new).then_inc(mask_loaded_x1_stored, 16)
            with nc.gpsimd.Fori(0, NT) as t:
                for i in range(2):
                    hi, lo = (pair[:, bass.ds(t * 2 + i, 1), :].rearrange("p a w -> p (a w)") for pair in (hqk_hi, hqk_lo))
                    pool.wait_ge(rows_loaded[i], t * 16 + 16 * 3)
                    pool.nop(nofuse=True)
                    pool.tensor_scalar(w_rows[:, i, :], w_rows[:, i, :], WS, None, ALU.mult).then_inc(head_step, 1)
                    pool.wait_ge(head_step, t * 4 + (2 * i + 1))
                    pool.nop(nofuse=True)
                    pool.tensor_tensor(hi, w_rows[:, i, :], ones[:, :].broadcast_to([P, HEADS * DH]), ALU.mult).then_inc(head_step, 1)
                    pool.wait_ge(head_step, t * 4 + (2 * i + 2))
                    pool.nop(nofuse=True)
                    pool.tensor_tensor(lo, w_rows[:, i, :], hi, ALU.subtract).then_inc(w_lo_done, 1)
                for p in range(TT):
                    banks.wait_moved(pool, t, ("out", p))
                    pool.dma_start(x1_rows[bass.ds(t * TILE + p * P, P), :], x1[:, p, :]).then_inc(mask_loaded_x1_stored, 16)
            pool.wait_ge(mask_loaded_x1_stored, 16 + 16 * NT * TT)

        @block.tensor
        def _(pe):
            def transposes(t, unit, blocks):
                banks.wait_room(pe, t, unit)
                for i, from_ in enumerate(blocks):
                    last = pe.transpose(psum[:, banks.bank(t, unit), i * P:(i + 1) * P], from_, ident[:, :])
                banks.fills(last, t, unit)

            def turn_xn(t, nth):
                pe.wait_ge(xn_ready, nth * TT + TT)
                for k in range(KD):
                    transposes(t, ("x", k), [xn[:, i, k * P:(k + 1) * P] for i in range(TT)])

            for unit, _ in warm:
                transposes(None, unit, [ident[:, :]])
            turn_xn(None, 0)

            def cols(hi, lo, at):
                return [(hi[:, k, at], lo[:, k, at]) for k in range(KD)]

            def weight(w, at):
                return cols(w_hi[:, w * KD:(w + 1) * KD, :], w_lo[:, w * KD:(w + 1) * KD, :], at)

            def block_of(i):
                return slice(i * P, (i + 1) * P)

            def tile(t, last_tile):
                def project(unit, left, right):
                    banks.wait_room(pe, t, unit)
                    banks.fills(three_passes(pe, psum_of(t, unit), left, right), t, unit)

                def turn_ctx(p):
                    pe.wait_ge(kv_loaded[p], t * 32 + 32)
                    for k in range(KD):
                        transposes(t, ("kv", p, k), [kv[:, p, i, block_of(k)] for i in range(4)])

                def scores(p):
                    unit = ("scores", p)
                    for k in range(KD):
                        banks.wait_moved(pe, t, ("kv", p, k))
                    banks.wait_room(pe, t, unit)
                    b = banks.bank(t, unit)
                    for k in range(KD):
                        pe.matmul(psum[:, b, KV:KV + P], q_t[:, k, block_of(p)], k_t[:, k, block_of(p)],
                                  start=(k == 0), stop=(k == KD - 1), skip_group_check=True)
                    for s in range(2):
                        for k in range(KD):
                            last = pe.matmul(psum[s * S:(s + 1) * S, b, 0:KV], q_t[:, k, p * P + s * S:p * P + (s + 1) * S],
                                             kv_t[:, k, s * KV:(s + 1) * KV], start=False, stop=(k == KD - 1),
                                             skip_group_check=True)
                    banks.fills(last, t, unit)

                def attend(p):
                    unit = ("att", p)
                    banks.wait_moved(pe, t, ("probs", p))
                    banks.wait_room(pe, t, unit)
                    b = banks.bank(t, unit)
                    pe.matmul(psum[:, b, :], probs_t[:, 2, :], v_new[:, p, :], start=True, stop=True, skip_group_check=True)
                    for s in range(2):
                        for i in range(2):
                            last = pe.matmul(psum[s * S:(s + 1) * S, b, :], probs_t[:, i, s * S:(s + 1) * S],
                                             kv[:, p, 2 * s + i, :], start=False, stop=(i == 1), skip_group_check=True)
                    banks.fills(last, t, unit)

                def turn_att(p):
                    banks.wait_moved(pe, t, ("att", p))
                    transposes(t, ("turn", p), [att[:, k, block_of(p)] for k in range(KD)])

                def project_out(p):
                    banks.wait_moved(pe, t, ("turn", p))
                    project(("out", p), cols(att_hi, att_lo, slice(0, P)), weight(3, slice(0, D)))

                for k in range(KD):
                    banks.wait_moved_before(pe, t, ("x", k))
                xt = cols(xt_hi, xt_lo, slice(0, TILE))
                pe.wait_ge(w_lo_done, KD)
                for e in range(4):
                    project(("q", e), weight(0, block_of(e)), xt)
                pe.wait_ge(w_lo_done, 2 * KD)
                for e in range(4):
                    project(("k", e), weight(1, block_of(e)), xt)
                turn_ctx(0)
                pe.wait_ge(w_lo_done, 3 * KD)
                for p in range(TT):
                    project(("v", p), cols(xt_hi, xt_lo, block_of(p)), weight(2, slice(0, D)))
                pe.wait_ge(w_lo_done, 4 * KD)
                for p in range(TT):
                    scores(p)
                    if p:
                        turn_att(p - 1)
                    if p + 1 < TT:
                        turn_ctx(p + 1)
                    elif not last_tile:
                        turn_xn(t, t + 1)
                    pe.wait_ge(exp_done, t * TT + (p + 1))
                    transposes(t, ("probs", p), [probs[:, block_of(i)] for i in range(3)])
                    if p:
                        project_out(p - 1)
                    attend(p)
                turn_att(TT - 1)
                project_out(TT - 1)

            with nc.tensor.Fori(0, NT - 1) as t:
                tile(t, False)
            tile(NT - 1, True)

        unscale = 1.0 / (XS * WS)
        acts_part = {"q": (0, 2), "k": (0, 2), "v": (0, 2), "kv": (0, 1)}
        dves_part = {"q": (1, 3), "k": (1, 3), "v": (1, 3), "kv": (2, 3)}
        home = {"q": q_t, "k": k_t, "v": v_new}

        @block.scalar
        def _(act):
            def first_halves(t):
                for k in range(KD):
                    banks.wait_filled(act, t, ("x", k))
                    act.activation(xt_hi[:, k, :], psum_of(t, ("x", k)), ACT.Copy).then_inc(xt_hi_done, 1)

            for unit, _ in warm:
                banks.wait_filled(act, None, unit)
                banks.moves(act.activation(total[:, unit[1] % TT:unit[1] % TT + 1], psum_of(None, unit, 1), ACT.Copy), None, unit)
            first_halves(None)
            for w in range(4):
                act.wait_ge(rows_loaded[w % 2], 16 * (w // 2 + 1))
                for k in range(KD):
                    act.activation(w_hi[:, w * KD + k, :], w_rows[:, w % 2, k * D:(k + 1) * D], ACT.Copy, scale=WS).then_inc(w_hi_done, 1)

            def tile(t, last_tile):
                def move(unit, out, scale=1.0):
                    banks.wait_filled(act, t, unit)
                    n = 3 * P if unit[0] == "probs" else 512
                    banks.moves(act.activation(out, psum_of(t, unit, n), ACT.Copy, scale=scale), t, unit)

                def softmax(p):
                    act.wait_ge(low_top_ready, t * TT + (p + 1))
                    act.activation(probs[:, :], probs[:, :], ACT.Exp, bias=low_top[:, p:p + 1], scale=XATTN_SCALE,
                                   accum_out=total[:, p:p + 1]).then_inc(exp_done, 1)

                def move_ctx(p):
                    for k in acts_part["kv"]:
                        move(("kv", p, k), kv_t[:, k, :])

                def att_first_half(p):
                    banks.wait_filled(act, t, ("turn", p))
                    act.activation(att_hi[:, :, :].rearrange("p a b -> p (a b)"), psum_of(t, ("turn", p)), ACT.Copy,
                                   scale=AS).then_inc(att_hi_done, 1)

                def move_att(p):
                    act.wait_ge(inv_ready, t * TT + (p + 1))
                    unit = ("att", p)
                    banks.wait_filled(act, t, unit)
                    banks.moves(act.activation(att[:, :, p * P:(p + 1) * P], psum_of(t, unit).rearrange("p (k d) -> p k d", k=KD),
                                               ACT.Copy, scale=inv_total[:, p:p + 1]), t, unit)

                def move_all(kind):
                    for e in acts_part[kind]:
                        move((kind, e), home[kind][:, e, :], unscale)

                move_all("q")
                move_all("k")
                move_ctx(0)
                move_all("v")
                for p in range(TT):
                    if p:
                        att_first_half(p - 1)
                    softmax(p)
                    if p + 1 < TT:
                        move_ctx(p + 1)
                    elif not last_tile:
                        first_halves(t)
                    move(("probs", p), probs_t[:, :, :].rearrange("p a b -> p (a b)"))
                    move_att(p)
                att_first_half(TT - 1)

            with nc.scalar.Fori(0, NT - 1) as t:
                tile(t, False)
            tile(NT - 1, True)

        @block.vector
        def _(dve):
            def second_halves(t, nth):
                for k in range(KD):
                    dve.wait_ge(xt_hi_done, nth * KD + (k + 1))
                    banks.moves(dve.tensor_tensor(xt_lo[:, k, :], psum_of(t, ("x", k)), xt_hi[:, k, :], ALU.subtract), t, ("x", k))

            dve.wait_ge(x_loaded, 16)
            layernorm(dve, 0, xn, xn, stat, ln_step, xn_ready)
            second_halves(None, 0)
            for w in range(4):
                for k in range(KD):
                    dve.wait_ge(w_hi_done, w * KD + k + 1)
                    dve.scalar_tensor_tensor(w_lo[:, w * KD + k, :], w_rows[:, w % 2, k * D:(k + 1) * D], WS, w_hi[:, w * KD + k, :],
                                             ALU.mult, ALU.subtract).then_inc(w_lo_done, 1)
            dve.wait_ge(mask_loaded_x1_stored, 16)

            def tile(t, last_tile):
                def move(unit, out, scale=1.0):
                    banks.wait_filled(dve, t, unit)
                    banks.moves(dve.tensor_scalar(out, psum_of(t, unit), scale, None, ALU.mult), t, unit)

                def move_ctx(p):
                    for k in dves_part["kv"]:
                        banks.wait_filled(dve, t, ("kv", p, k))
                        banks.moves(dve.tensor_copy(kv_t[:, k, :], psum_of(t, ("kv", p, k))), t, ("kv", p, k))

                def maximum(p):
                    unit = ("scores", p)
                    banks.wait_filled(dve, t, unit)
                    dve.nop(nofuse=True)
                    banks.moves(dve.tensor_tensor_reduce(probs[:, :], psum_of(t, unit, KV + P), mask[:, :], 1.0, LOWEST,
                                                         ALU.add, ALU.max, top[:, p:p + 1]), t, unit)
                    banks.wait_moved(dve, t, unit)
                    dve.tensor_scalar(low_top[:, p:p + 1], top[:, p:p + 1], -XATTN_SCALE, None, ALU.mult).then_inc(low_top_ready, 1)

                def inverse(p):
                    dve.wait_ge(exp_done, t * TT + (p + 1))
                    dve.reciprocal(inv_total[:, p:p + 1], total[:, p:p + 1]).then_inc(inv_ready, 1)

                def att_second_half(p):
                    dve.wait_ge(att_hi_done, t * TT + (p + 1))
                    banks.moves(dve.scalar_tensor_tensor(att_lo[:, :, :].rearrange("p a b -> p (a b)"), psum_of(t, ("turn", p)), AS,
                                                         att_hi[:, :, :].rearrange("p a b -> p (a b)"), ALU.mult, ALU.subtract),
                                t, ("turn", p))

                def residual(p):
                    if p == 0:
                        dve.wait_ge(res_loaded, t * 16 + 16)
                    banks.wait_filled(dve, t, ("out", p))
                    banks.moves(dve.scalar_tensor_tensor(x1[:, p, :], psum_of(t, ("out", p)), 1.0 / (AS * WS), x1[:, p, :],
                                                         ALU.mult, ALU.add), t, ("out", p))

                def move_all(kind):
                    for e in dves_part[kind]:
                        move((kind, e), home[kind][:, e, :], unscale)

                move_all("q")
                move_all("k")
                move_ctx(0)
                dve.wait_ge(x_loaded, t * 16 + 32)
                layernorm(dve, t + 1, xn, xn, stat, ln_step, xn_ready)
                move_all("v")
                for p in range(TT):
                    maximum(p)
                    if p:
                        att_second_half(p - 1)
                    inverse(p)
                    if p + 1 < TT:
                        move_ctx(p + 1)
                    elif not last_tile:
                        second_halves(t, t + 1)
                    if p:
                        residual(p - 1)
                att_second_half(TT - 1)
                residual(TT - 1)

            with nc.vector.Fori(0, NT - 1) as t:
                tile(t, False)
            tile(NT - 1, True)


class Sections:

    def __init__(self, nc, ctx, name, sections):
        self.filled = [ctx.enter_context(nc.semaphore(f"{name}_bank{b}_filled")) for b in range(8)]
        self.moved = [ctx.enter_context(nc.semaphore(f"{name}_bank{b}_moved")) for b in range(8)]
        self.uses = {s: [0] * 8 for s in sections}
        self.where = {}
        for s, units in sections.items():
            for unit, bank in units:
                self.where[unit] = (bank, self.uses[s][bank])
                self.uses[s][bank] += 1

    def bank(self, unit):
        return self.where[unit][0]

    def earlier(self, runs, unit):
        bank, count = self.where[unit]
        for s, n in runs.items():
            if self.uses[s][bank]:
                count = n * self.uses[s][bank] + count
        return count

    def wait_room(self, pe, runs, unit):
        n = self.earlier(runs, unit)
        if not (isinstance(n, int) and n == 0):
            pe.wait_ge(self.moved[self.bank(unit)], n)

    def wait_filled(self, eng, runs, unit):
        eng.wait_ge(self.filled[self.bank(unit)], self.earlier(runs, unit) + 1)

    def wait_moved(self, eng, runs, unit):
        eng.wait_ge(self.moved[self.bank(unit)], self.earlier(runs, unit) + 1)

    def fills(self, ins, unit):
        ins.then_inc(self.filled[self.bank(unit)], 1)

    def moves(self, ins, unit):
        ins.then_inc(self.moved[self.bank(unit)], 1)


def z_of(z_scratch, hi_or_lo, half, t):
    n = HEADS // 2
    return z_scratch[hi_or_lo, half * n:(half + 1) * n, :, bass.ds(t * TILE, TILE)].rearrange("h d t -> d h t")


def heads_phase(nc, psum, ident, x1_rows, xn, stat, head_weights, hqk_hi, hqk_lo, w_rows, b_q, b_k, b_v, rope_cos, rope_sin, causal, w_o, wo_hi, wo_lo, z_scratch,
                first_z):
    with ExitStack() as ctx:
        def sb(name, shape, dt):
            return ctx.enter_context(nc.sbuf_tensor("hd_" + name, shape, dt))

        def sem(name):
            return ctx.enter_context(nc.semaphore("hd_" + name))

        WIDE = HEADS * DH
        wv_hi, wv_lo = sb("wv_hi", [P, KD, WIDE], F16), sb("wv_lo", [P, KD, WIDE], F16)
        xt_hi, xt_lo = sb("xt_hi", [P, KD, TILE], F16), sb("xt_lo", [P, KD, TILE], F16)
        bias = sb("bias", [P, 2, 2, PAIRS], F32)
        bias_v = sb("bias_v", [P, HEADS], F32)
        cos, sin = sb("cos", [P, S], F32), sb("sin", [P, S], F32)
        mask = sb("mask", [P, P], F32)
        products = sb("products", [P, 2, 4, TILE], F32)
        rotated = sb("rotated", [P, 2, 2, TILE], F32)
        v = sb("v", [P, TT, 2 * DH], F32)
        probs = sb("probs", [P, 2, TT, P], F32)
        probs_t = sb("probs_t", [P, 2, TT, P], F32)
        top, low_top = sb("top", [P, 2, TT], F32), sb("low_top", [P, 2, TT], F32)
        total, inv_total = sb("total", [P, 2, TT], F32), sb("inv_total", [P, 2, TT], F32)
        z_hi, z_lo = sb("z_hi", [P, 2, TILE], F16), sb("z_lo", [P, 2, TILE], F16)

        loaded = [sem("rows0_loaded"), sem("rows1_loaded")]
        w_hi_done, w_lo_done = sem("w_hi_done"), sem("w_lo_done")
        small_loaded_z_stored = sem("small_loaded_z_stored")
        x_loaded, bias_scaled = sem("x_loaded"), sem("bias_scaled")
        wo_scaled, wo_hi_done = sem("wo_scaled"), sem("wo_hi_done")
        ln_step, xn_ready, xt_hi_done = sem("ln_step"), sem("xn_ready"), sem("xt_hi_done")
        added_dve, added_pool = sem("added_dve"), sem("added_pool")
        low_top_ready, exp_done, inv_done, probs_ready = sem("low_top_ready"), sem("exp_done"), sem("inv_done"), sem("probs_ready")
        z_hi_done, first_z_loaded = sem("z_hi_done"), sem("first_z_loaded")
        SMALL = 6

        banks = Sections(nc, ctx, "hd", {
            "turn": [(("x", k), k) for k in range(KD)],
            "proj": [(("q", 0), 0), (("q", 1), 1), (("k", 0), 2), (("k", 1), 3), (("v", 0), 6), (("v", 1), 7)],
            "scores": [(("scores", 0), 4), (("scores", 1), 5)],
            "att": [(("probs", 0), 4), (("probs", 1), 5), (("z", 0), 0), (("z", 1), 1)],
        })

        def psum_of(unit):
            return psum[:, banks.bank(unit), :]

        def rows_of(first):
            return x1_rows[bass.ds(first, TILE), :].rearrange("(b p) d -> p b d", p=P)

        class Step:

            def __init__(self, a, turns, pair, next_pair, turn_next=False, att=True, proj=True, first_of=None):
                self.a, self.pair, self.next_pair = a, pair, next_pair
                self.first_token = (turns - 1) * TILE
                self.turn_next, self.att, self.proj = turn_next, att, proj
                self.first_of = first_of
                self.turns = turns
                self.runs_scores = {"turn": turns, "scores": a, "att": a}
                self.runs_turn = {"turn": turns, "proj": a + 1, "att": a}
                self.turns_now = turns + 1 if turn_next else turns
                g = a + 1
                self.runs_proj = {"turn": self.turns_now, "proj": g, "att": a if att else 0}
                self.runs_probs = {"turn": self.turns_now, "scores": a + 1, "att": a}
                self.runs_z = {"turn": self.turns_now, "proj": g + 1 if proj else g, "att": a}

        def for_each_step(eng, on_the_side, step):
            step(Step(-1, 1, None, 0, att=False))
            def tile(t, last_tile):
                step(Step(t * PAIRS, t + 1, 0, 1, first_of=None if last_tile else t))
                on_the_side(t, last_tile)
                with eng.Fori(1, PAIRS - 1) as n:
                    step(Step(t * PAIRS + n, t + 1, n, n + 1))
                if not last_tile:
                    step(Step(t * PAIRS + (PAIRS - 1), t + 1, PAIRS - 1, 0, turn_next=True))
            with eng.Fori(0, NT - 1) as t:
                tile(t, False)
            tile(NT - 1, True)
            step(Step(NT * PAIRS - 1, NT, PAIRS - 1, None, proj=False))

        block = ctx.enter_context(nc.Block())

        @block.sync
        def _(sp):
            for dst, src in ((cos, rope_cos), (sin, rope_sin), (mask, causal)):
                sp.dma_start(dst[:, :], src).then_inc(small_loaded_z_stored, 16)
            for w, b in enumerate((b_q, b_k)):
                sp.dma_start(bias[:, w, :, :], b).then_inc(small_loaded_z_stored, 16)
            sp.dma_start(bias_v[:, :], b_v).then_inc(small_loaded_z_stored, 16)
            for k in range(2, KD):
                sp.wait_ge(w_lo_done, k - 1)
                sp.dma_start(w_rows[:, k % 2, :], head_weights[(2 * KD + k) * P:(2 * KD + k + 1) * P, :]).then_inc(loaded[k % 2], 16)

            def on_the_side(t, last_tile):
                if not last_tile:
                    load_wo(t + 1)

            def load_first_z():
                sp.wait_ge(w_lo_done, KD + NT)
                sp.wait_ge(small_loaded_z_stored, 16 * (SMALL + 2 * (NT - 1) * PAIRS))
                for half in range(2):
                    sp.dma_start(first_z[half], z_of(z_scratch, half, 0, 0)).then_inc(first_z_loaded, 16)

            def load_wo(t):
                sp.wait_ge(w_lo_done, t + KD)
                sp.nop(nofuse=True)
                sp.dma_start(w_rows[:, 0, :], w_o[:, bass.ds(t * (4 * D), 4 * D)]).then_inc(loaded[0], 16)

            def step(s):
                if not s.att:
                    load_wo(0)
                    return
                if not s.proj:
                    load_first_z()
                if s.first_of is not None:
                    t = s.first_of
                    sp.wait_ge(xt_hi_done, t * KD + KD)
                    sp.nop(nofuse=True)
                    sp.dma_start(xn[:, :, :], rows_of(t * TILE + TILE)).then_inc(x_loaded, 16)
                for h in range(2):
                    banks.wait_moved(sp, s.runs_z, ("z", h))
                    sp.nop(nofuse=True)
                for half, z in enumerate((z_hi, z_lo)):
                    sp.dma_start(z_scratch[half, bass.ds(s.pair * 2, 2), :, bass.ds(s.first_token, TILE)].rearrange("h d t -> d h t"),
                                 z[:, :, :]).then_inc(small_loaded_z_stored, 16)

            for_each_step(nc.sync, on_the_side, step)
            sp.wait_ge(first_z_loaded, 32)
            sp.wait_ge(small_loaded_z_stored, 16 * (SMALL + 2 * NT * PAIRS))

        @block.gpsimd
        def _(pool):
            def step(s):
                if not s.proj:
                    return
                for w in range(2):
                    banks.wait_moved(pool, s.runs_proj, ("qk"[w], 1))
                    pool.tensor_tensor(rotated[0:HALF, w, 0, :], products[0:HALF, w, 0, :], products[0:HALF, w, 2, :], ALU.subtract)
                    pool.tensor_tensor(rotated[HALF:P, w, 1, :], products[HALF:P, w, 1, :], products[HALF:P, w, 3, :],
                                       ALU.add).then_inc(added_pool, 1)

            def on_the_side(t, last_tile):
                pool.wait_ge(added_pool, t * (2 * PAIRS) + 4)
                pool.wait_ge(wo_hi_done, t + 1)
                pool.nop(nofuse=True)
                pool.tensor_tensor(wo_lo[:, bass.ds(t * 4, 4), :].rearrange("p n m -> p (n m)"), w_rows[:, 0, :],
                                   wo_hi[:, bass.ds(t * 4, 4), :].rearrange("p n m -> p (n m)"), ALU.subtract).then_inc(w_lo_done, 1)
                pool.wait_ge(w_lo_done, t + (KD + 1))
                pool.nop(nofuse=True)

            for_each_step(nc.gpsimd, on_the_side, step)

        @block.tensor
        def _(pe):
            def turn_xn(runs, nth):
                if nth is not None:
                    pe.wait_ge(xn_ready, nth * TT)
                for k in range(KD):
                    banks.wait_room(pe, runs, ("x", k))
                    for i in range(TT):
                        last = pe.transpose(psum_of(("x", k))[:, i * P:(i + 1) * P], xn[:, i, k * P:(k + 1) * P], ident[:, :])
                    banks.fills(last, ("x", k))

            turn_xn({}, None)
            for k in range(KD):
                banks.wait_moved(pe, {}, ("x", k))
            xt = [(xt_hi[:, k, :], xt_lo[:, k, :]) for k in range(KD)]

            def project(s, w, half):
                unit = ("qk"[w], half)
                banks.wait_room(pe, s.runs_proj, unit)
                pair = s.next_pair
                cols = bass.ds(pair * DH + half * (WIDE // 2), DH)
                left = [(hqk_hi[:, w * KD + k, cols], hqk_lo[:, w * KD + k, cols]) for k in range(KD)]
                banks.fills(three_passes(pe, psum_of(unit), left, xt), unit)

            def step(s):
                if s.turn_next:
                    turn_xn(s.runs_turn, s.turns)
                if s.att:
                    pe.wait_ge(added_dve, s.a * 2 + 2)
                    pe.wait_ge(added_pool, s.a * 2 + 2)
                    for h in range(2):
                        unit = ("scores", h)
                        banks.wait_room(pe, s.runs_scores, unit)
                        for i in range(TT):
                            cols = slice(i * P, (i + 1) * P)
                            last = pe.matmul(psum_of(unit)[:, cols], rotated[:, 0, h, cols], rotated[:, 1, h, cols], start=True, stop=True)
                        banks.fills(last, unit)
                if s.turn_next:
                    for k in range(KD):
                        banks.wait_moved(pe, s.runs_turn, ("x", k))
                if s.proj:
                    project(s, 0, 0)
                    project(s, 0, 1)
                    project(s, 1, 0)
                if s.att:
                    for h in range(2):
                        unit = ("probs", h)
                        pe.wait_ge(probs_ready, s.a * 2 + (h + 1))
                        banks.wait_room(pe, s.runs_probs, unit)
                        for i in range(TT):
                            last = pe.transpose(psum_of(unit)[:, i * P:(i + 1) * P], probs[:, h, i, :], ident[:, :])
                        banks.fills(last, unit)
                if s.proj:
                    project(s, 1, 1)
                if s.att:
                    for half in range(2):
                        banks.wait_moved(pe, {"turn": s.turns, "proj": s.a}, ("v", half))
                    for h in range(2):
                        unit = ("z", h)
                        banks.wait_moved(pe, s.runs_probs, ("probs", h))
                        banks.wait_room(pe, s.runs_z, unit)
                        for i in range(TT):
                            last = pe.matmul(psum_of(unit)[:, i * P:(i + 1) * P], v[:, i, h * DH:(h + 1) * DH], probs_t[:, h, i, :],
                                             start=True, stop=True)
                        banks.fills(last, unit)
                if not s.att:
                    pe.wait_ge(w_lo_done, KD)
                if s.proj:
                    for half in range(2):
                        unit = ("v", half)
                        banks.wait_room(pe, s.runs_proj, unit)
                        pair_cols = bass.ds(s.next_pair * (2 * DH), 2 * DH)
                        right = [(wv_hi[:, k, pair_cols], wv_lo[:, k, pair_cols]) for k in range(KD)]
                        for i in range(2):
                            cols = slice((2 * half + i) * P, (2 * half + i + 1) * P)
                            last = three_passes(pe, psum_of(unit)[:, i * 2 * DH:(i + 1) * 2 * DH],
                                                [(xt_hi[:, k, cols], xt_lo[:, k, cols]) for k in range(KD)], right)
                        banks.fills(last, unit)

            for_each_step(nc.tensor, lambda t, last_tile: None, step)

        @block.scalar
        def _(act):
            def first_halves(runs):
                for k in range(KD):
                    banks.wait_filled(act, runs, ("x", k))
                    act.activation(xt_hi[:, k, :], psum_of(("x", k)), ACT.Copy).then_inc(xt_hi_done, 1)

            first_halves({})
            for k in range(KD):
                if k >= 2:
                    act.wait_ge(loaded[k % 2], 16)
                act.activation(wv_hi[:, k, :], w_rows[:, k % 2, :], ACT.Copy, scale=WS).then_inc(w_hi_done, 1)

            def step(s):
                if s.turn_next:
                    first_halves(s.runs_turn)
                if s.att:
                    for h in range(2):
                        act.wait_ge(low_top_ready, s.a * 2 + (h + 1))
                        for i in range(TT):
                            last = act.activation(probs[:, h, i, :], probs[:, h, i, :], ACT.Exp, bias=low_top[:, h, i:i + 1],
                                                  scale=HEAD_SCALE, accum_out=total[:, h, i:i + 1])
                        last.then_inc(exp_done, 1)
                    for h in range(2):
                        unit = ("probs", h)
                        banks.wait_filled(act, s.runs_probs, unit)
                        banks.moves(act.activation(probs_t[:, h, :, :].rearrange("p i k -> p (i k)"), psum_of(unit), ACT.Copy), unit)
                    for h in range(2):
                        banks.wait_filled(act, s.runs_z, ("z", h))
                        if h == 0:
                            act.wait_ge(small_loaded_z_stored, s.a * 32 + 16 * SMALL)
                            act.nop(nofuse=True)
                        act.activation(z_hi[:, h, :], psum_of(("z", h)), ACT.Identity,
                                       bias=bias_v[:, bass.ds(s.pair * 2 + h, 1)]).then_inc(z_hi_done, 1)
                if s.proj:
                    for half in range(2):
                        unit = ("v", half)
                        banks.wait_filled(act, s.runs_proj, unit)
                        banks.moves(act.activation(v[:, 2 * half:2 * half + 2, :].rearrange("p i d -> p (i d)"), psum_of(unit), ACT.Copy,
                                                   scale=AS / (XS * WS)), unit)

            act.wait_ge(bias_scaled, 2)

            def on_the_side(t, last_tile):
                act.wait_ge(loaded[0], t * 16 + 32)
                act.activation(w_rows[:, 0, :], w_rows[:, 0, :], ACT.Copy, scale=WS).then_inc(wo_scaled, 1)
                act.wait_ge(wo_scaled, t + 1)
                act.activation(wo_hi[:, bass.ds(t * 4, 4), :].rearrange("p n m -> p (n m)"), w_rows[:, 0, :], ACT.Copy).then_inc(wo_hi_done, 1)
            for_each_step(nc.scalar, on_the_side, step)

        @block.vector
        def _(dve):
            def second_halves(runs, nth):
                for k in range(KD):
                    dve.wait_ge(xt_hi_done, nth * KD + (k + 1))
                    banks.moves(dve.tensor_tensor(xt_lo[:, k, :], psum_of(("x", k)), xt_hi[:, k, :], ALU.subtract), ("x", k))

            second_halves({}, 0)
            for k in range(KD):
                dve.wait_ge(w_hi_done, k + 1)
                dve.scalar_tensor_tensor(wv_lo[:, k, :], w_rows[:, k % 2, :], WS, wv_hi[:, k, :],
                                         ALU.mult, ALU.subtract).then_inc(w_lo_done, 1)
            dve.wait_ge(small_loaded_z_stored, 16 * SMALL)
            dve.tensor_scalar(bias[:, :, :, :].rearrange("p a b q -> p (a b q)"), bias[:, :, :, :].rearrange("p a b q -> p (a b q)"),
                              XS * WS, None, ALU.mult).then_inc(bias_scaled, 1)
            dve.tensor_scalar(bias_v[:, :], bias_v[:, :], AS, None, ALU.mult).then_inc(bias_scaled, 1)
            dve.wait_ge(bias_scaled, 2)

            def by_sequence(ap):
                return ap.rearrange("p (s n) -> p s n", n=S)

            def table(t):
                return t[:, :].unsqueeze(1).broadcast_to([P, TILE // S, S])

            def on_the_side(t, last_tile):
                if not last_tile:
                    layernorm(dve, t, xn, xn, stat, ln_step, xn_ready, parts=(2,))

            def rotate(s, w):
                for half, (first, second) in enumerate((((cos, 0), (sin, 1)), ((sin, 2), (cos, 3)))):
                    unit = ("qk"[w], half)
                    banks.wait_filled(dve, s.runs_proj, unit)
                    for tab, slot in (first, second):
                        last = dve.scalar_tensor_tensor(by_sequence(products[:, w, slot, :]), by_sequence(psum_of(unit)),
                                                        bias[:, w, half, bass.ds(s.next_pair, 1)], table(tab), ALU.add, ALU.mult)
                    banks.moves(last, unit)
                banks.wait_moved(dve, s.runs_proj, ("qk"[w], 1))
                dve.tensor_tensor(rotated[HALF:P, w, 0, :], products[0:HALF, w, 1, :], products[0:HALF, w, 3, :], ALU.add)
                dve.tensor_tensor(rotated[0:HALF, w, 1, :], products[HALF:P, w, 0, :], products[HALF:P, w, 2, :],
                                  ALU.subtract).then_inc(added_dve, 1)

            def step(s):
                if s.turn_next:
                    second_halves(s.runs_turn, s.turns)
                if s.att:
                    for h in range(2):
                        unit = ("scores", h)
                        banks.wait_filled(dve, s.runs_scores, unit)
                        dve.nop(nofuse=True)
                        for i in range(TT):
                            last = dve.tensor_tensor_reduce(probs[:, h, i, :], psum_of(unit)[:, i * P:(i + 1) * P], mask[:, :], 1.0, LOWEST,
                                                            ALU.add, ALU.max, top[:, h, i:i + 1])
                        banks.moves(last, unit)
                        banks.wait_moved(dve, s.runs_scores, unit)
                        dve.tensor_scalar(low_top[:, h, :], top[:, h, :], -HEAD_SCALE, None, ALU.mult).then_inc(low_top_ready, 1)
                if s.att:
                    for h in range(2):
                        dve.wait_ge(exp_done, s.a * 2 + (h + 1))
                        dve.reciprocal(inv_total[:, h, :], total[:, h, :]).then_inc(inv_done, 1)
                        dve.wait_ge(inv_done, s.a * 2 + (h + 1))
                        dve.tensor_tensor(probs[:, h, :, :], probs[:, h, :, :], inv_total[:, h, :].unsqueeze(2).broadcast_to([P, TT, P]),
                                          ALU.mult).then_inc(probs_ready, 1)
                if s.first_of is not None:
                    t = s.first_of
                    dve.wait_ge(x_loaded, t * 16 + 16)
                    layernorm(dve, t, xn, xn, stat, ln_step, xn_ready, parts=(1,))
                if s.proj:
                    rotate(s, 0)
                    rotate(s, 1)
                if s.att:
                    for h in range(2):
                        dve.wait_ge(z_hi_done, s.a * 2 + (h + 1))
                        banks.moves(dve.scalar_tensor_tensor(z_lo[:, h, :], psum_of(("z", h)), bias_v[:, bass.ds(s.pair * 2 + h, 1)],
                                                             z_hi[:, h, :], ALU.add, ALU.subtract), ("z", h))

            for_each_step(nc.vector, on_the_side, step)


ZW_UNSCALE = 1.0 / (AS * WS)
FS = 2.0 ** 6
HS = 1.0 / FS
FP4_AS_F16 = 2.0 ** 14
GU = 2 * FF
WORDS_GU, WORDS_DOWN = D // 8, FF // 8
WHOLE = P
REST = (WORDS_DOWN - WHOLE) // 16


def decode_fp4(dve, last, codes, sign, magnitude, shift):
    dve.tensor_scalar(sign, codes, 12 - shift, 0x8000, ALU.logical_shift_left, ALU.bitwise_and)
    if shift <= 9:
        last(dve.tensor_scalar(magnitude, codes, 9 - shift, 0x0E00, ALU.logical_shift_left, ALU.bitwise_and))
    else:
        last(dve.tensor_scalar(magnitude, codes, shift - 9, 0x0E00, ALU.logical_shift_right, ALU.bitwise_and))
    last(dve.tensor_tensor(sign, sign, magnitude, ALU.bitwise_or))


def merge_phase(nc, psum, z_scratch, x1_rows, b_o, wo_hi, wo_lo, gu_codes, gu_scales, down_codes, down_scales, shifts,
                first_z, x2, xn, stat, gu_hi, gu_lo, down_hi, down_lo):
    with ExitStack() as ctx:
        def sb(name, shape, dt):
            return ctx.enter_context(nc.sbuf_tensor("mg_" + name, shape, dt))

        def sem(name):
            return ctx.enter_context(nc.semaphore("mg_" + name))

        HH = HEADS // 2
        z_pairs = first_z, (sb("z_hi", [P, HH, TILE], F16)[:, :, :], sb("z_lo", [P, HH, TILE], F16)[:, :, :])
        b_o_all = sb("b_o_all", [P, D], F32)
        codes = sb("codes", [P, GU], I32)
        gu_scale = sb("gu_scale", [P, GU], F16)
        down_c = sb("down_c", [P, 1 + REST, D], I32)
        down_scale = sb("down_scale", [P, 1 + REST, D], F16)
        shift = sb("shift", [P, 1], I32)
        PIECE, HALF_DOWN = 352, D // 2
        sign, magnitude = sb("sign", [P, PIECE], I32), sb("magnitude", [P, PIECE], I32)
        value = sb("value", [P, 2, PIECE], F32)
        gu_loaded, down_loaded, step = sem("gu_loaded"), sem("down_loaded"), sem("step")
        hi_done, lo_done, value_ready = sem("hi_done"), sem("lo_done"), sem("value_ready")
        x1_loaded, b_loaded, x1_ready = sem("x1_loaded"), sem("b_loaded"), sem("x1_ready")
        z_loaded = [sem("z0_loaded"), sem("z1_loaded")]
        z_used = [sem("z0_used"), sem("z1_used")]
        merged, added, ln_step, xn_ready = sem("merged"), sem("added"), sem("ln_step"), sem("xn_ready")

        def bank_of(t, i):
            return t % 2 * TT + i

        block = ctx.enter_context(nc.Block())

        jobs = []
        for j in range(4):
            for c in range(0, GU, PIECE):
                at = slice(c, c + PIECE)
                jobs.append((codes[:, at], 4 * j, gu_scale[:, at], gu_hi[:, j, at], gu_lo[:, j, at]))
        for j in range(8 + REST):
            row, bit = (0, 4 * j) if j < 8 else (j - 7, 0)
            for c in range(0, D, HALF_DOWN):
                at = slice(c, c + HALF_DOWN)
                jobs.append((down_c[:, row, at], bit, down_scale[:, row, at], down_hi[:, j, at], down_lo[:, j, at]))
        GU_LOADS, DOWN_LOADS = 2 + 8, 2 + 8 + 2 * REST

        @block.sync
        def _(sp):
            def load_z(t, half):
                for hi_or_lo, z in enumerate(z_pairs[half]):
                    sp.dma_start(z, z_of(z_scratch, hi_or_lo, half, t)).then_inc(z_loaded[half], 16)

            load_z(0, 1)
            sp.dma_start(x2[:, :, :], x1_rows.rearrange("(b p) d -> p b d", p=P)).then_inc(x1_loaded, 16)
            sp.dma_start(b_o_all[:, :], b_o.broadcast_to([P, D])).then_inc(b_loaded, 16)
            for u in range(2):
                sp.dma_start(codes[u * 64:(u + 1) * 64, :], gu_codes).then_inc(gu_loaded, 16)
                for g in range(4):
                    first = u * 64 + g * 16
                    sp.dma_start(gu_scale[first:first + 16, :], gu_scales[g:g + 1, :].broadcast_to([16, GU])).then_inc(gu_loaded, 16)
            sp.dma_start(shift[:, :], shifts).then_inc(down_loaded, 16)
            sp.dma_start(down_c[:, 0, :], down_codes[0:WHOLE, :]).then_inc(down_loaded, 16)
            for g in range(8):
                sp.dma_start(down_scale[16 * g:16 * g + 16, 0, :], down_scales[g:g + 1, :].broadcast_to([16, D])).then_inc(down_loaded, 16)
            for q in range(REST):
                words = down_codes[WHOLE + 16 * q:WHOLE + 16 * q + 16, :]
                sp.dma_start(down_c[:, 1 + q, :], words.unsqueeze(0).broadcast_to([8, 16, D])).then_inc(down_loaded, 16)
                sp.dma_start(down_scale[:, 1 + q, :], down_scales[8 + q:9 + q, :].broadcast_to([P, D])).then_inc(down_loaded, 16)
            for t in range(1, NT):
                for half in range(2):
                    sp.wait_ge(z_used[half], t)
                    load_z(t, half)

        @block.gpsimd
        def _(pool):
            pool.wait_ge(b_loaded, 16)
            pool.wait_ge(x1_loaded, 16)
            for b in range(NT * TT):
                pool.tensor_tensor(x2[:, b, :], x2[:, b, :], b_o_all[:, :], ALU.add).then_inc(x1_ready, 1)
            for n, (_, _, _, hi, lo) in enumerate(jobs):
                pool.wait_ge(hi_done, n + 1)
                pool.tensor_tensor(lo, value[:, n % 2, 0:hi.shape[-1]], hi, ALU.subtract).then_inc(lo_done, 1)

        @block.tensor
        def _(pe):
            for t in range(NT):
                for half in range(2):
                    if half or t:
                        pe.wait_ge(z_loaded[half], 32 * (t + half))
                    z_hi, z_lo = z_pairs[half]
                    for i in range(TT):
                        at = slice(i * P, (i + 1) * P)
                        bank = bank_of(t, i)
                        if half == 0 and t >= 2:
                            pe.wait_ge(added, (t - 2) * TT + (i + 1))
                        for n in range(HH):
                            head = half * HH + n
                            pe.matmul(psum[:, bank, :], z_hi[:, n, at], wo_hi[:, head, :], start=(head == 0), stop=False)
                            pe.matmul(psum[:, bank, :], z_hi[:, n, at], wo_lo[:, head, :], start=False, stop=False)
                            last = pe.matmul(psum[:, bank, :], z_lo[:, n, at], wo_hi[:, head, :], start=False, stop=(head == HEADS - 1))
                        if half == 1 and i < TT - 1:
                            last.then_inc(merged, 1)
                    last.then_inc(z_used[half], 1)

        @block.scalar
        def _(act):
            for n, (_, _, _, hi, _) in enumerate(jobs):
                act.wait_ge(value_ready, n + 1)
                act.activation(hi, value[:, n % 2, 0:hi.shape[-1]], ACT.Copy).then_inc(hi_done, 1)

        @block.vector
        def _(dve):
            n = [0]

            def last(ins):
                n[0] += 1
                ins.then_inc(step, 1)
                dve.wait_ge(step, n[0])

            def decode(job):
                if job == 0:
                    dve.wait_ge(gu_loaded, 16 * GU_LOADS)
                    last(dve.tensor_scalar(codes[64:P, :], codes[64:P, :], 16, None, ALU.logical_shift_right))
                if job == 4 * (GU // PIECE):
                    dve.wait_ge(down_loaded, 16 * DOWN_LOADS)
                    for q in range(REST):
                        last(dve.tensor_scalar(down_c[:, 1 + q, :], down_c[:, 1 + q, :], shift[:, 0:1], None, ALU.logical_shift_right))
                c, bit, scale, hi, lo = jobs[job]
                w = hi.shape[-1]
                if job:
                    dve.wait_ge(value_ready, job)
                if bit > 12:
                    last(dve.tensor_scalar(magnitude[:, 0:w], c, 16, None, ALU.logical_shift_right))
                    c, bit = magnitude[:, 0:w], bit - 16
                decode_fp4(dve, last, c, sign[:, 0:w], magnitude[:, 0:w], bit)
                if job >= 2:
                    dve.wait_ge(lo_done, job - 1)
                as_f16 = sign[:, 0:w].bitcast(F16).rearrange("p (n two) -> p n two", two=2)[:, :, 0]
                dve.scalar_tensor_tensor(value[:, job % 2, 0:w], as_f16, FP4_AS_F16 * FS, scale, ALU.mult, ALU.mult).then_inc(value_ready, 1)

            def add(t, i):
                if i < TT - 1:
                    dve.wait_ge(merged, t * (TT - 1) + i + 1)
                else:
                    dve.wait_ge(z_used[1], t + 1)
                b = t * TT + i
                dve.wait_ge(x1_ready, b + 1)
                dve.scalar_tensor_tensor(x2[:, b, :], psum[:, bank_of(t, i), :], ZW_UNSCALE, x2[:, b, :], ALU.mult, ALU.add).then_inc(added, 1)

            share = -(-len(jobs) // (NT * TT))
            for b in range(NT * TT):
                for job in range(b * share, min((b + 1) * share, len(jobs))):
                    decode(job)
                add(b // TT, b % TT)
                if b == TT - 1:
                    dve.wait_ge(added, TT)
                    layernorm(dve, 0, x2[:, 0:TT, :], xn, stat, ln_step, xn_ready, by_code=True)


def ffn_phase(nc, psum, ident, x2, xn, stat, gu_hi, gu_lo, down_hi, down_lo, out_rows):
    with ExitStack() as ctx:
        def sb(name, shape, dt):
            return ctx.enter_context(nc.sbuf_tensor("ff_" + name, shape, dt))

        def sem(name):
            return ctx.enter_context(nc.semaphore("ff_" + name))

        xt_hi, xt_lo = sb("xt_hi", [P, KD, TILE], F16), sb("xt_lo", [P, KD, TILE], F16)
        gate = sb("gate", [P, 2, TILE], F32)
        hidden = sb("hidden", [P, 2, TILE], F32)
        h_hi, h_lo = sb("h_hi", [P, FB, TILE], F16), sb("h_lo", [P, FB, TILE], F16)
        result = sb("result", [P, TT, D], F32)
        squares = sb("squares", [P, TT], F32)
        rms = {k: sb("rms_" + k, [P, TT], I32 if k == "half" else F32) for k in ("var", "half", "y", "y2")}

        ln_step, xn_ready, xt_hi_done, out_stored = sem("ln_step"), sem("xn_ready"), sem("xt_hi_done"), sem("out_stored")
        h_hi_done, h_lo_done = sem("h_hi_done"), sem("h_lo_done")
        squares_done, rms_step = sem("squares_done"), sem("rms_step")

        warm = [(("warm", i), i) for i in range(4)]
        turn = [(("x", k), 4 + k) for k in range(KD)]
        hid = [((kind, b), (4 + 2 * b + (kind == "up")) % 8) for b in range(FB) for kind in ("gate", "up")]
        banks = Banks(nc, ctx, "ff", warm + turn, hid + [(("y", i), i) for i in range(TT - 1)] + turn + [(("y", TT - 1), TT - 1)])

        def psum_of(t, unit):
            return psum[:, banks.bank(t, unit), :]

        def block_of(i):
            return slice(i * P, (i + 1) * P)

        block = ctx.enter_context(nc.Block())

        @block.sync
        def _(sp):
            with nc.sync.Fori(0, NT) as t:
                banks.wait_moved(sp, t, ("y", TT - 1))
                sp.dma_start(out_rows[bass.ds(t * TILE, TILE), :].rearrange("(b p) d -> p b d", p=P), result[:, :, :]).then_inc(out_stored, 16)
            sp.wait_ge(out_stored, 16 * NT)

        @block.gpsimd
        def _(pool):
            with nc.gpsimd.Fori(0, NT) as t:
                for b in range(FB):
                    pool.wait_ge(h_hi_done, t * FB + (b + 1))
                    pool.tensor_tensor(h_lo[:, b, :], hidden[:, b % 2, :], h_hi[:, b, :], ALU.subtract).then_inc(h_lo_done, 1)

        @block.tensor
        def _(pe):
            def turn_xn(t, nth):
                if t is not None:
                    pe.wait_ge(xn_ready, nth * TT)
                for k in range(KD):
                    banks.wait_room(pe, t, ("x", k))
                    for i in range(TT):
                        last = pe.transpose(psum_of(t, ("x", k))[:, block_of(i)], xn[:, i, block_of(k)], ident[:, :])
                    banks.fills(last, t, ("x", k))

            def project(t, unit, left, right):
                banks.wait_room(pe, t, unit)
                banks.fills(three_passes(pe, psum_of(t, unit), left, right), t, unit)

            turn_xn(None, 0)
            for unit, _ in warm:
                last = pe.transpose(psum_of(None, unit)[:, 0:P], ident[:, :], ident[:, :])
                banks.fills(last, None, unit)

            def tile(t, last_tile):
                for k in range(KD):
                    banks.wait_moved_before(pe, t, ("x", k))
                for b in range(FB):
                    for first, kind in ((0, "gate"), (FF, "up")):
                        cols = slice(first + b * P, first + (b + 1) * P)
                        project(t, (kind, b), [(gu_hi[:, k, cols], gu_lo[:, k, cols]) for k in range(KD)],
                                [(xt_hi[:, k, :], xt_lo[:, k, :]) for k in range(KD)])
                for i in range(TT):
                    if i == TT - 1 and not last_tile:
                        turn_xn(t, t + 1)
                    banks.wait_room(pe, t, ("y", i))
                    for b in range(FB):
                        if i == 0:
                            pe.wait_ge(h_lo_done, t * FB + (b + 1))
                        pe.matmul(psum_of(t, ("y", i)), h_hi[:, b, block_of(i)], down_hi[:, b, :], start=(b == 0), stop=False)
                        pe.matmul(psum_of(t, ("y", i)), h_hi[:, b, block_of(i)], down_lo[:, b, :], start=False, stop=False)
                        last = pe.matmul(psum_of(t, ("y", i)), h_lo[:, b, block_of(i)], down_hi[:, b, :], start=False, stop=(b == FB - 1))
                    banks.fills(last, t, ("y", i))

            with nc.tensor.Fori(0, NT - 1) as t:
                tile(t, False)
            tile(NT - 1, True)

        @block.scalar
        def _(act):
            def first_halves(t):
                for k in range(KD):
                    banks.wait_filled(act, t, ("x", k))
                    act.activation(xt_hi[:, k, :], psum_of(t, ("x", k)), ACT.Copy).then_inc(xt_hi_done, 1)

            first_halves(None)
            for i, (unit, _) in enumerate(warm):
                banks.wait_filled(act, None, unit)
                banks.moves(act.activation(squares[:, i:i + 1], psum_of(None, unit)[:, 0:1], ACT.Copy), None, unit)

            def tile(t, last_tile):
                def hidden_first_half(b):
                    banks.wait_moved(act, t, ("up", b))
                    act.activation(h_hi[:, b, :], hidden[:, b % 2, :], ACT.Copy).then_inc(h_hi_done, 1)

                for b in range(FB):
                    banks.wait_filled(act, t, ("gate", b))
                    banks.moves(act.activation(gate[:, b % 2, :], psum_of(t, ("gate", b)), ACT.Silu, scale=1.0 / (XS * FS)), t, ("gate", b))
                    if b:
                        hidden_first_half(b - 1)
                hidden_first_half(FB - 1)
                for i in range(TT):
                    if i == TT - 1 and not last_tile:
                        first_halves(t)
                    banks.wait_filled(act, t, ("y", i))
                    if i >= 2:
                        act.wait_ge(squares_done, t * TT + (i - 1))
                    act.activation(gate[:, i % 2, :], psum_of(t, ("y", i)), ACT.Square,
                                   accum_out=squares[:, i:i + 1]).then_inc(squares_done, 1)
                act.wait_ge(squares_done, t * TT + TT)
                act.nop(nofuse=True)

            with nc.scalar.Fori(0, NT - 1) as t:
                tile(t, False)
            tile(NT - 1, True)

        @block.vector
        def _(dve):
            def second_halves(t, nth):
                for k in range(KD):
                    dve.wait_ge(xt_hi_done, nth * KD + (k + 1))
                    banks.moves(dve.tensor_tensor(xt_lo[:, k, :], psum_of(t, ("x", k)), xt_hi[:, k, :], ALU.subtract), t, ("x", k))

            second_halves(None, 0)

            def tile(t, first_tile, last_tile):
                def gated(b):
                    banks.wait_moved(dve, t, ("gate", b))
                    banks.wait_filled(dve, t, ("up", b))
                    if b >= 2:
                        dve.wait_ge(h_lo_done, t * FB + (b - 1))
                    banks.moves(dve.scalar_tensor_tensor(hidden[:, b % 2, :], psum_of(t, ("up", b)), HS / (XS * FS), gate[:, b % 2, :],
                                                         ALU.mult, ALU.mult), t, ("up", b))
                for b in range(FB):
                    gated(b)
                if not last_tile:
                    layernorm(dve, t, x2[:, bass.ds(t * TT + TT, TT), :], xn, stat, ln_step, xn_ready, by_code=True)
                    second_halves(t, t + 1)
                dve.wait_ge(squares_done, t * TT + TT)
                n = [0]

                def done(ins):
                    ins.then_inc(rms_step, 1)
                    n[0] += 1
                    dve.wait_ge(rms_step, t * RMS_STEPS + n[0])
                done(dve.tensor_scalar(rms["var"][:, :], squares[:, :], 1.0 / D, RMS_EPS, ALU.mult, ALU.add))
                inverse_root(dve, rms, done)
                assert n[0] == RMS_STEPS
                if not first_tile:
                    dve.wait_ge(out_stored, t * 16)
                    dve.nop(nofuse=True)
                for i in range(TT):
                    banks.moves(dve.scalar_tensor_tensor(result[:, i, :], psum_of(t, ("y", i)), rms["y"][:, i:i + 1],
                                                         x2[:, bass.ds(t * TT + i, 1), :].rearrange("p a d -> p (a d)"),
                                                         ALU.mult, ALU.add), t, ("y", i))

            tile(0, True, False)
            with nc.vector.Fori(1, NT - 1) as t:
                tile(t, False, False)
            tile(NT - 1, False, True)


def whole_kernel(nc, x, ctx_2048, wq, wk, wv, wo, head_weights, b_q, b_k, b_v, w_o, b_o, gu_codes, gu_scales, down_codes,
                 down_scales, identity, own_new, causal, rope_cos, rope_sin, shifts, out):
    x1 = nc.dram_tensor("x1_scratch", (TOK, D), F32).ap()
    z = nc.dram_tensor("z_scratch", (2, HEADS, DH, TOK), F16).ap()
    with ExitStack() as ctx:
        psum = ctx.enter_context(nc.psum_tensor("psum", [P, 8, 512], F32))
        ident = ctx.enter_context(nc.sbuf_tensor("ident", [P, P], F32))
        with nc.semaphore("identity_loaded") as identity_loaded, nc.Block() as block:
            @block.sync
            def _(sp):
                sp.dma_start(ident[:, :], identity).then_inc(identity_loaded, 16)
                sp.wait_ge(identity_loaded, 16)

        def sb(name, shape, dt):
            return ctx.enter_context(nc.sbuf_tensor(name, shape, dt))

        wo_hi, wo_lo = sb("wo_hi", [P, HEADS, D], F16), sb("wo_lo", [P, HEADS, D], F16)
        xn, stat = sb("xn", [P, TT, D], F32), stat_buffers(sb)
        w_rows = sb("w_rows", [P, 2, HEADS * DH], F32)
        first_z = tuple(w_rows[:, i, :].bitcast(F16).rearrange("p (h t) -> p h t", t=TILE) for i in range(2))
        with ExitStack() as heads:
            def for_heads(name, shape, dt):
                return heads.enter_context(nc.sbuf_tensor(name, shape, dt))

            hqk_hi, hqk_lo = for_heads("hqk_hi", [P, 2 * KD, HEADS * DH], F16), for_heads("hqk_lo", [P, 2 * KD, HEADS * DH], F16)
            xattn_phase(nc, psum, ident, x.rearrange("b s d -> (b s) d"), ctx_2048.rearrange("b k d -> (b k) d"), wq, wk, wv, wo,
                        own_new, x1, wo_hi, wo_lo, w_rows, xn, stat, head_weights, hqk_hi, hqk_lo)
            heads_phase(nc, psum, ident, x1, xn, stat, head_weights, hqk_hi, hqk_lo, w_rows, b_q, b_k, b_v,
                        rope_cos, rope_sin, causal, w_o, wo_hi, wo_lo, z, first_z)
        x2 = sb("x2", [P, NT * TT, D], F32)
        gu_hi, gu_lo = sb("gu_hi", [P, KD, GU], F16), sb("gu_lo", [P, KD, GU], F16)
        down_hi, down_lo = sb("down_hi", [P, FB, D], F16), sb("down_lo", [P, FB, D], F16)
        merge_phase(nc, psum, z, x1, b_o, wo_hi, wo_lo, gu_codes, gu_scales, down_codes, down_scales, shifts,
                    first_z, x2, xn, stat, gu_hi, gu_lo, down_hi, down_lo)
        ffn_phase(nc, psum, ident, x2, xn, stat, gu_hi, gu_lo, down_hi, down_lo, out.rearrange("b s d -> (b s) d"))


_INS = ["x", "ctx_2048", "L0_xattn_wq", "L0_xattn_wk", "L0_xattn_wv", "L0_xattn_wo",
        "head_weights", "L0_attn_b_Q", "L0_attn_b_K", "L0_attn_b_V", "L0_attn_W_O", "L0_attn_b_O",
        "L0_ffn_gate_up_packed", "L0_ffn_gate_up_scales", "L0_ffn_down_packed", "L0_ffn_down_scales"]


def _constants():
    import numpy as np
    own_new = np.zeros((P, KV + P), np.float32)
    at = np.arange(P)
    own = at[:, None] // S == at[None, :] // S
    own_new[:, KV:] = np.where(own, 0.0, -1.0e30)
    causal = np.where(own & (at[None, :] <= at[:, None]), 0.0, -1.0e30).astype(np.float32)
    inv_freq = (1.0 / np.float32(10000.0) ** (np.arange(0, DH, 2, dtype=np.float32) / np.float32(DH))).astype(np.float32)
    freqs = np.outer(inv_freq, np.arange(S, dtype=np.float32)).astype(np.float32)
    unscale = np.float32(1.0 / (XS * WS))
    rope = {f"rope_{f.__name__}": np.tile(f(freqs).astype(np.float32) * unscale, (2, 1)) for f in (np.cos, np.sin)}
    shifts = (4 * (at // 16)).astype(np.int32)[:, None]
    return {"identity": np.eye(P, dtype=np.float32), "own_new": own_new, "causal": causal, **rope, "shifts": shifts}


def _hidden_order():
    import numpy as np
    at = np.arange(P)
    whole = [8 * at + j for j in range(8)]
    rest = [8 * (WHOLE + 16 * q + at % 16) + at // 16 for q in range(REST)]
    return np.concatenate(whole + rest)


def _laid_out(name, inputs):
    import numpy as np
    if name == "head_weights":
        return np.concatenate([_laid_out("L0_attn_W_" + kind, inputs) for kind in "QKV"])
    a = np.asarray(inputs[name])
    if name.startswith("L0_xattn_w"):
        return a.T
    if name in ("L0_attn_W_Q", "L0_attn_W_K"):
        return a.reshape(HEADS, D, HALF, 2).transpose(1, 3, 0, 2).reshape(D, HEADS * DH)
    if name == "L0_attn_W_V":
        return a.transpose(1, 0, 2).reshape(D, HEADS * DH)
    if name in ("L0_attn_b_Q", "L0_attn_b_K"):
        return a.reshape(PAIRS, 2, HALF, 2).transpose(1, 2, 3, 0).reshape(P, 2, PAIRS)
    if name == "L0_attn_b_V":
        return a.T
    if name == "L0_attn_W_O":
        return a.transpose(1, 0, 2).reshape(DH, HEADS * D)
    if name == "L0_attn_b_O":
        return a[None, :]
    both = np.concatenate([_hidden_order(), FF + _hidden_order()])
    if name == "L0_ffn_gate_up_packed":
        return a[both].T
    if name == "L0_ffn_gate_up_scales":
        return a[:, both]
    if name == "L0_ffn_down_packed":
        return a.T
    return a


def kernel(**inputs):
    import numpy as _np
    import concourse.bacc as _bacc
    from concourse import mybir as _mybir
    from concourse.bass_utils import run_bass_kernel_spmd as _run

    nc = _bacc.Bacc("TRN2", target_bir_lowering=False, num_devices=1)
    arrays, args = {}, []
    for name, a in [(n, _laid_out(n, inputs)) for n in _INS] + list(_constants().items()):
        a = _np.ascontiguousarray(a)
        arrays[f"in_{name}_dram"] = a
        args.append(nc.dram_tensor(f"in_{name}_dram", a.shape, _mybir.dt.from_np(a.dtype), kind="ExternalInput").ap())
    out = nc.dram_tensor("out_0_dram", (B, S, D), F32, kind="ExternalOutput").ap()
    whole_kernel(nc, *args, out)
    r = _run(nc, [arrays], core_ids=[0])
    return r.results[0]["out_0_dram"]
```

```python
from contextlib import ExitStack

import concourse.bass as bass
from concourse import mybir

F32 = mybir.dt.float32
F16 = mybir.dt.float16
I32 = mybir.dt.int32
ALU = mybir.AluOpType
ACT = mybir.ActivationFunctionType

P = 128
B, S, D = 32, 64, 512
KV = 256
TOK = B * S
TILE = 512
NT = TOK // TILE
TT = TILE // P
KD = D // P
HEADS, DH = 16, 128
HALF = DH // 2
PAIRS = HEADS // 2
FF = 1408
FB = FF // P
LN_EPS = 1e-5
RMS_EPS = 1e-6
LOWEST = -3.0e38

XS = 2.0 ** 8
WS = 2.0 ** 11
AS = 2.0 ** 6
XATTN_SCALE = float(D) ** -0.5
HEAD_SCALE = float(DH) ** -0.5
RSQRT_MAGIC = 0x5F3759DF


class Banks:

    def __init__(self, nc, ctx, name, before, body):
        self.filled = [ctx.enter_context(nc.semaphore(f"{name}_bank{b}_filled")) for b in range(8)]
        self.moved = [ctx.enter_context(nc.semaphore(f"{name}_bank{b}_moved")) for b in range(8)]
        self.ahead, self.uses, self.at = [0] * 8, [0] * 8, {}
        for unit, bank in before:
            self.at["before", unit] = (bank, self.ahead[bank])
            self.ahead[bank] += 1
        for unit, bank in body:
            self.at["body", unit] = (bank, self.uses[bank])
            self.uses[bank] += 1

    def place(self, t, unit):
        if t is None:
            return self.at["before", unit]
        bank, k = self.at["body", unit]
        return bank, t * self.uses[bank] + (self.ahead[bank] + k)

    def bank(self, t, unit):
        return self.place(t, unit)[0]

    def wait_room(self, pe, t, unit):
        bank, earlier = self.place(t, unit)
        if not (isinstance(earlier, int) and earlier == 0):
            pe.wait_ge(self.moved[bank], earlier)

    def wait_filled(self, eng, t, unit):
        bank, earlier = self.place(t, unit)
        eng.wait_ge(self.filled[bank], earlier + 1)

    def wait_moved(self, eng, t, unit):
        bank, earlier = self.place(t, unit)
        eng.wait_ge(self.moved[bank], earlier + 1)

    def before(self, t, unit):
        bank, k = self.at["body", unit]
        behind = self.ahead[bank] + k + 1 - self.uses[bank]
        assert behind >= 0
        return bank, t * self.uses[bank] + behind

    def wait_filled_before(self, eng, t, unit):
        bank, count = self.before(t, unit)
        eng.wait_ge(self.filled[bank], count)

    def wait_moved_before(self, eng, t, unit):
        bank, count = self.before(t, unit)
        eng.wait_ge(self.moved[bank], count)

    def fills(self, ins, t, unit):
        ins.then_inc(self.filled[self.bank(t, unit)], 1)

    def moves(self, ins, t, unit):
        ins.then_inc(self.moved[self.bank(t, unit)], 1)


ROOT_STEPS = 2 + 9
LN_STEPS = 2 * TT + 1 + ROOT_STEPS + 1
RMS_STEPS = 1 + ROOT_STEPS


def inverse_root(dve, stat, done):
    var, half, y, y2 = stat["var"], stat["half"], stat["y"], stat["y2"]
    done(dve.tensor_scalar(half[:, :], var[:, :].bitcast(I32), 1, None, ALU.logical_shift_right))
    done(dve.tensor_scalar(y[:, :].bitcast(I32), half[:, :], -1, RSQRT_MAGIC, ALU.mult, ALU.add))
    for _ in range(3):
        done(dve.tensor_tensor(y2[:, :], y[:, :], y[:, :], ALU.mult))
        done(dve.scalar_tensor_tensor(y2[:, :], y2[:, :], -0.5, var[:, :], ALU.mult, ALU.mult))
        done(dve.scalar_tensor_tensor(y[:, :], y2[:, :], 1.5, y[:, :], ALU.add, ALU.mult))


def layernorm(dve, t, src, dst, stat, step, ready, by_code=False, parts=(1, 2)):
    n = [0]

    def all_done():
        dve.wait_ge(step, t * LN_STEPS + n[0])
        if not isinstance(t, int):
            dve.nop(nofuse=True)

    def done(ins, wait=True):
        ins.then_inc(step, 1)
        n[0] += 1
        if wait:
            all_done()

    if 1 in parts:
        for i in range(TT):
            done(dve.bn_stats(stat["six"][:, i, :], src[:, i, :]), wait=(i == TT - 1))
        for i in range(TT):
            done(dve.bn_aggr(stat["meanvar"][:, i, :], stat["six"][:, i, :]), wait=(i == TT - 1))
    if 2 not in parts:
        return
    n[0] = 2 * TT
    done(dve.tensor_scalar(stat["var"][:, :], stat["meanvar"][:, :, 1], LN_EPS, None, ALU.add))
    inverse_root(dve, stat, done)
    y = stat["y"]
    done(dve.tensor_scalar(y[:, :], y[:, :], XS, None, ALU.mult))
    for i in range(TT):
        to, from_ = dst[:, i, :], src[:, i, :]
        if by_code:
            to = to.rearrange("p (g j w) -> p g j w", g=KD, j=8)
            from_ = from_.rearrange("p (g w j) -> p g j w", g=KD, j=8)
        dve.tensor_scalar(to, from_, stat["meanvar"][:, i, 0:1], y[:, i:i + 1], ALU.subtract, ALU.mult).then_inc(ready, 1)
    assert n[0] == LN_STEPS


def three_passes(pe, out, left, right):
    k = len(left)
    for i in range(k):
        (lh, ll), (rh, rl) = left[i], right[i]
        pe.matmul(out, lh, rh, start=(i == 0), stop=False)
        pe.matmul(out, lh, rl, start=False, stop=False)
        last = pe.matmul(out, ll, rh, start=False, stop=(i == k - 1))
    return last


def stat_buffers(sb):
    return {"six": sb("ln_six", [P, TT, 6], F32), "meanvar": sb("ln_meanvar", [P, TT, 2], F32),
            "var": sb("ln_var", [P, TT], F32), "half": sb("ln_half", [P, TT], I32),
            "y": sb("ln_y", [P, TT], F32), "y2": sb("ln_y2", [P, TT], F32)}


def xattn_phase(nc, psum, ident, x_rows, ctx_kv, wq, wk, wv, wo, own_new, identity, x1_rows, w_hi, w_lo, w_rows, xn, stat,
                head_weights, hqk_hi, hqk_lo, mask_loaded_x1_stored):
    with ExitStack() as ctx:
        def sb(name, shape, dt):
            return ctx.enter_context(nc.sbuf_tensor("xa_" + name, shape, dt))

        def sem(name):
            return ctx.enter_context(nc.semaphore("xa_" + name))

        xt_hi, xt_lo = sb("xt_hi", [P, KD, TILE], F16), sb("xt_lo", [P, KD, TILE], F16)
        q_t, k_t = sb("q_t", [P, KD, TILE], F32), sb("k_t", [P, KD, TILE], F32)
        att = q_t
        v_new = sb("v_new", [P, TT, D], F32)
        kv = sb("kv", [P, TT, 4, D], F32)
        kv_t = sb("kv_t", [P, KD, 2 * KV], F32)
        mask = sb("mask", [P, KV + P], F32)
        probs = sb("probs", [P, KV + P], F32)
        probs_t = sb("probs_t", [P, 3, P], F32)
        top, low_top = sb("top", [P, TT], F32), sb("low_top", [P, TT], F32)
        total, inv_total = sb("total", [P, TT], F32), sb("inv_total", [P, TT], F32)
        att_hi, att_lo = sb("att_hi", [P, KD, P], F16), sb("att_lo", [P, KD, P], F16)
        x1 = sb("x1", [P, TT, D], F32)

        ones = sb("ones", [P, 1], F32)

        rows_loaded = [sem("rows0_loaded"), sem("rows1_loaded")]
        x_loaded, res_loaded = sem("x_loaded"), sem("res_loaded")
        kv_loaded = [sem(f"kv{p}_loaded") for p in range(TT)]
        head_step, ones_set = sem("head_step"), sem("ones_set")
        w_hi_done, w_lo_done, ln_step, xn_ready, xt_hi_done = sem("w_hi_done"), sem("w_lo_done"), sem("ln_step"), sem("xn_ready"), sem("xt_hi_done")
        low_top_ready, exp_done = sem("low_top_ready"), sem("exp_done")
        inv_ready, att_hi_done = sem("inv_ready"), sem("att_hi_done")
        identity_loaded = sem("identity_loaded")

        turn_x = [(("x", k), 4 + k) for k in range(KD)]
        warm = [(("warm", i), i % 4) for i in range(12)]
        before = warm + turn_x
        body = [(("q", e), e) for e in range(4)] + [(("k", e), 4 + e) for e in range(4)] + [(("v", p), p) for p in range(TT)]
        def turn_kv(p):
            return [(("kv", p, k), 4 + k) for k in range(KD)]

        body += turn_kv(0)
        for p in range(TT):
            body += [(("scores", p), 0)]
            body += [(("turn", p - 1), 3)] if p else []
            body += turn_kv(p + 1) if p + 1 < TT else turn_x
            body += [(("probs", p), 1)]
            body += [(("out", p - 1), 3)] if p else []
            body += [(("att", p), 2)]
        body += [(("turn", TT - 1), 3), (("out", TT - 1), 3)]
        banks = Banks(nc, ctx, "xa", before, body)

        def psum_of(t, unit, n=512):
            return psum[:, banks.bank(t, unit), 0:n]

        def rows_of(tensor, first, n):
            return tensor[bass.ds(first, n), :].rearrange("(b p) d -> p b d", p=P)

        block = ctx.enter_context(nc.Block())

        @block.sync
        def _(sp):
            def load_kv(t, p):
                for s in range(2):
                    sp.dma_start(kv[:, p, 2 * s:2 * s + 2, :],
                                 ctx_kv[bass.ds(t * (2 * TT * KV) + (2 * p + s) * KV, KV), :]
                                 .rearrange("(b p) d -> p b d", p=P)).then_inc(kv_loaded[p], 16)

            sp.dma_start(xn[:, :, :], rows_of(x_rows, 0, TILE)).then_inc(x_loaded, 16)
            sp.dma_start(ident[:, :], identity).then_inc(identity_loaded, 16)
            for i, w in enumerate((wq, wk, wv, wo)):
                if i >= 2:
                    sp.wait_ge(w_lo_done, KD * (i - 1))
                sp.dma_start(w_rows[:, i % 2, :].rearrange("p (b d) -> p b d", d=D), rows_of(w, 0, D)).then_inc(rows_loaded[i % 2], 16)
                if i == 1:
                    load_kv(0, 0)
            for p in range(1, TT):
                load_kv(0, p)
            sp.dma_start(x1[:, :, :], rows_of(x_rows, 0, TILE)).then_inc(res_loaded, 16)

            def load_head_weights(t):
                sp.wait_ge(w_lo_done, t * 2 + 4 * KD)
                sp.nop(nofuse=True)
                for i in range(2):
                    sp.dma_start(w_rows[:, i, :], head_weights[bass.ds(t * (2 * P) + i * P, P), :]).then_inc(rows_loaded[i], 16)

            def tile(t, last_tile):
                if not last_tile:
                    sp.wait_ge(xt_hi_done, t * KD + KD)
                    sp.dma_start(xn[:, :, :], rows_of(x_rows, t * TILE + TILE, TILE)).then_inc(x_loaded, 16)
                else:
                    sp.wait_ge(mask_loaded_x1_stored, 16 + 16 * TT * (NT - 1))
                    sp.wait_ge(xt_hi_done, NT * KD)
                    sp.dma_start(xn[:, :, :], rows_of(x1_rows, 0, TILE)).then_inc(x_loaded, 16)
                load_head_weights(t)
                if last_tile:
                    return
                for p in range(TT):
                    banks.wait_filled(sp, t, ("att", p))
                    load_kv(t + 1, p)
                sp.wait_ge(mask_loaded_x1_stored, t * (16 * TT) + (16 * TT + 16))
                sp.nop(nofuse=True)
                sp.dma_start(x1[:, :, :], rows_of(x_rows, t * TILE + TILE, TILE)).then_inc(res_loaded, 16)

            with nc.sync.Fori(0, NT - 1) as t:
                tile(t, False)
            tile(NT - 1, True)
            sp.wait_ge(w_lo_done, 4 * KD + 2 * KD)
            for i in range(2):
                sp.dma_start(w_rows[:, i, :], head_weights[(2 * KD + i) * P:(2 * KD + i + 1) * P, :]).then_inc(rows_loaded[i], 16)
                sp.wait_ge(rows_loaded[i], 16 * (2 + NT + 1))

        @block.gpsimd
        def _(pool):
            pool.memset(ones[:, :], 1.0).then_inc(ones_set, 1)
            pool.wait_ge(ones_set, 1)
            pool.dma_start(mask[:, :], own_new).then_inc(mask_loaded_x1_stored, 16)
            with nc.gpsimd.Fori(0, NT) as t:
                for i in range(2):
                    hi, lo = (pair[:, bass.ds(t * 2 + i, 1), :].rearrange("p a w -> p (a w)") for pair in (hqk_hi, hqk_lo))
                    pool.wait_ge(rows_loaded[i], t * 16 + 16 * 3)
                    pool.nop(nofuse=True)
                    pool.tensor_scalar(w_rows[:, i, :], w_rows[:, i, :], WS, None, ALU.mult).then_inc(head_step, 1)
                    pool.wait_ge(head_step, t * 4 + (2 * i + 1))
                    pool.nop(nofuse=True)
                    pool.tensor_tensor(hi, w_rows[:, i, :], ones[:, :].broadcast_to([P, HEADS * DH]), ALU.mult).then_inc(head_step, 1)
                    pool.wait_ge(head_step, t * 4 + (2 * i + 2))
                    pool.nop(nofuse=True)
                    pool.tensor_tensor(lo, w_rows[:, i, :], hi, ALU.subtract).then_inc(w_lo_done, 1)
                for p in range(TT):
                    banks.wait_moved(pool, t, ("out", p))
                    pool.dma_start(x1_rows[bass.ds(t * TILE + p * P, P), :], x1[:, p, :]).then_inc(mask_loaded_x1_stored, 16)

        @block.tensor
        def _(pe):
            def transposes(t, unit, blocks):
                banks.wait_room(pe, t, unit)
                for i, from_ in enumerate(blocks):
                    last = pe.transpose(psum[:, banks.bank(t, unit), i * P:(i + 1) * P], from_, ident[:, :])
                banks.fills(last, t, unit)

            def turn_xn(t, nth, blocks=range(KD)):
                if 0 in blocks:
                    pe.wait_ge(xn_ready, nth * TT + TT)
                for k in blocks:
                    transposes(t, ("x", k), [xn[:, i, k * P:(k + 1) * P] for i in range(TT)])

            pe.wait_ge(identity_loaded, 16)
            for unit, _ in warm:
                transposes(None, unit, [ident[:, :]] * 4)
            turn_xn(None, 0)

            def cols(hi, lo, at):
                return [(hi[:, k, at], lo[:, k, at]) for k in range(KD)]

            def weight(w, at):
                return cols(w_hi[:, w * KD:(w + 1) * KD, :], w_lo[:, w * KD:(w + 1) * KD, :], at)

            def block_of(i):
                return slice(i * P, (i + 1) * P)

            def tile(t, last_tile):
                def project(unit, left, right):
                    banks.wait_room(pe, t, unit)
                    banks.fills(three_passes(pe, psum_of(t, unit), left, right), t, unit)

                def turn_ctx(p):
                    pe.wait_ge(kv_loaded[p], t * 32 + 32)
                    for k in range(KD):
                        transposes(t, ("kv", p, k), [kv[:, p, i, block_of(k)] for i in range(4)])

                def scores(p):
                    unit = ("scores", p)
                    for k in range(KD):
                        banks.wait_moved(pe, t, ("kv", p, k))
                    banks.wait_room(pe, t, unit)
                    b = banks.bank(t, unit)
                    for k in range(KD):
                        pe.matmul(psum[:, b, KV:KV + P], q_t[:, k, block_of(p)], k_t[:, k, block_of(p)],
                                  start=(k == 0), stop=(k == KD - 1), skip_group_check=True)
                    for s in range(2):
                        for k in range(KD):
                            last = pe.matmul(psum[s * S:(s + 1) * S, b, 0:KV], q_t[:, k, p * P + s * S:p * P + (s + 1) * S],
                                             kv_t[:, k, s * KV:(s + 1) * KV], start=False, stop=(k == KD - 1),
                                             skip_group_check=True)
                    banks.fills(last, t, unit)

                def attend(p):
                    unit = ("att", p)
                    banks.wait_moved(pe, t, ("probs", p))
                    banks.wait_room(pe, t, unit)
                    b = banks.bank(t, unit)
                    pe.matmul(psum[:, b, :], probs_t[:, 2, :], v_new[:, p, :], start=True, stop=True, skip_group_check=True)
                    for s in range(2):
                        for i in range(2):
                            last = pe.matmul(psum[s * S:(s + 1) * S, b, :], probs_t[:, i, s * S:(s + 1) * S],
                                             kv[:, p, 2 * s + i, :], start=False, stop=(i == 1), skip_group_check=True)
                    banks.fills(last, t, unit)

                def turn_att(p):
                    banks.wait_moved(pe, t, ("att", p))
                    transposes(t, ("turn", p), [att[:, k, block_of(p)] for k in range(KD)])

                def project_out(p):
                    banks.wait_moved(pe, t, ("turn", p))
                    project(("out", p), cols(att_hi, att_lo, slice(0, P)), weight(3, slice(0, D)))

                for k in range(KD):
                    banks.wait_moved_before(pe, t, ("x", k))
                xt = cols(xt_hi, xt_lo, slice(0, TILE))
                pe.wait_ge(w_lo_done, KD)
                for e in range(4):
                    project(("q", e), weight(0, block_of(e)), xt)
                pe.wait_ge(w_lo_done, 2 * KD)
                for e in range(4):
                    project(("k", e), weight(1, block_of(e)), xt)
                turn_ctx(0)
                pe.wait_ge(w_lo_done, 3 * KD)

                def project_v(p):
                    project(("v", p), cols(xt_hi, xt_lo, block_of(p)), weight(2, slice(0, D)))

                for p in range(TT - 1):
                    project_v(p)
                pe.wait_ge(w_lo_done, 4 * KD)
                banks.wait_moved(pe, t, ("q", 3))
                for p in range(TT):
                    scores(p)
                    if p:
                        turn_att(p - 1)
                    if p + 1 < TT:
                        turn_ctx(p + 1)
                    elif not last_tile:
                        turn_xn(t, t + 1, (0, 1))
                    pe.wait_ge(exp_done, t * TT + (p + 1))
                    transposes(t, ("probs", p), [probs[:, block_of(i)] for i in range(3)])
                    if p:
                        project_out(p - 1)
                    else:
                        project_v(TT - 1)
                    attend(p)
                if not last_tile:
                    turn_xn(t, t + 1, (2,))
                turn_att(TT - 1)
                if not last_tile:
                    turn_xn(t, t + 1, (3,))
                project_out(TT - 1)

            with nc.tensor.Fori(0, NT - 1) as t:
                tile(t, False)
            tile(NT - 1, True)

        unscale = 1.0 / (XS * WS)
        acts_part = {"q": (0, 2), "k": (0, 2), "v": (0, 2), "kv": (0, 1)}
        dves_part = {"q": (1, 3), "k": (1, 3), "v": (1, 3), "kv": (2, 3)}
        home = {"q": q_t, "k": k_t, "v": v_new}

        @block.scalar
        def _(act):
            def first_halves(t, blocks=range(KD)):
                for k in blocks:
                    banks.wait_filled(act, t, ("x", k))
                    act.activation(xt_hi[:, k, :], psum_of(t, ("x", k)), ACT.Copy).then_inc(xt_hi_done, 1)

            for unit, _ in warm:
                banks.wait_filled(act, None, unit)
                banks.moves(act.activation(total[:, unit[1] % TT:unit[1] % TT + 1], psum_of(None, unit, 1), ACT.Copy), None, unit)
            for w in range(4):
                if w == 1:
                    first_halves(None)
                act.wait_ge(rows_loaded[w % 2], 16 * (w // 2 + 1))
                for k in range(KD):
                    act.activation(w_hi[:, w * KD + k, :], w_rows[:, w % 2, k * D:(k + 1) * D], ACT.Copy, scale=WS).then_inc(w_hi_done, 1)

            def tile(t, last_tile):
                def move(unit, out, scale=1.0):
                    banks.wait_filled(act, t, unit)
                    n = 3 * P if unit[0] == "probs" else 512
                    banks.moves(act.activation(out, psum_of(t, unit, n), ACT.Copy, scale=scale), t, unit)

                def softmax(p):
                    act.wait_ge(low_top_ready, t * TT + (p + 1))
                    act.activation(probs[:, :], probs[:, :], ACT.Exp, bias=low_top[:, p:p + 1], scale=XATTN_SCALE,
                                   accum_out=total[:, p:p + 1]).then_inc(exp_done, 1)

                def move_ctx(p):
                    for k in acts_part["kv"]:
                        move(("kv", p, k), kv_t[:, k, :])

                def att_first_half(p):
                    banks.wait_filled(act, t, ("turn", p))
                    act.activation(att_hi[:, :, :].rearrange("p a b -> p (a b)"), psum_of(t, ("turn", p)), ACT.Copy,
                                   scale=AS).then_inc(att_hi_done, 1)

                def move_att(p):
                    act.wait_ge(inv_ready, t * TT + (p + 1))
                    unit = ("att", p)
                    banks.wait_filled(act, t, unit)
                    banks.moves(act.activation(att[:, :, p * P:(p + 1) * P], psum_of(t, unit).rearrange("p (k d) -> p k d", k=KD),
                                               ACT.Copy, scale=inv_total[:, p:p + 1]), t, unit)

                def move_all(kind):
                    for e in acts_part[kind]:
                        move((kind, e), home[kind][:, e, :], unscale)

                move_all("q")
                move_all("k")
                move_ctx(0)
                move_all("v")
                for p in range(TT):
                    if p:
                        att_first_half(p - 1)
                    softmax(p)
                    if p + 1 < TT:
                        move_ctx(p + 1)
                    elif not last_tile:
                        first_halves(t, (0, 1))
                    move(("probs", p), probs_t[:, :, :].rearrange("p a b -> p (a b)"))
                    move_att(p)
                if not last_tile:
                    first_halves(t, (2,))
                att_first_half(TT - 1)
                if not last_tile:
                    first_halves(t, (3,))

            with nc.scalar.Fori(0, NT - 1) as t:
                tile(t, False)
            tile(NT - 1, True)

        @block.vector
        def _(dve):
            def second_halves(t, nth, blocks=range(KD)):
                for k in blocks:
                    dve.wait_ge(xt_hi_done, nth * KD + (k + 1))
                    banks.moves(dve.tensor_tensor(xt_lo[:, k, :], psum_of(t, ("x", k)), xt_hi[:, k, :], ALU.subtract), t, ("x", k))

            dve.wait_ge(x_loaded, 16)
            layernorm(dve, 0, xn, xn, stat, ln_step, xn_ready)
            for w in range(4):
                if w == 1:
                    second_halves(None, 0)
                for k in range(KD):
                    dve.wait_ge(w_hi_done, w * KD + k + 1)
                    dve.scalar_tensor_tensor(w_lo[:, w * KD + k, :], w_rows[:, w % 2, k * D:(k + 1) * D], WS, w_hi[:, w * KD + k, :],
                                             ALU.mult, ALU.subtract).then_inc(w_lo_done, 1)
            dve.wait_ge(mask_loaded_x1_stored, 16)

            def tile(t, last_tile):
                def move(unit, out, scale=1.0):
                    banks.wait_filled(dve, t, unit)
                    banks.moves(dve.tensor_scalar(out, psum_of(t, unit), scale, None, ALU.mult), t, unit)

                def move_ctx(p):
                    for k in dves_part["kv"]:
                        banks.wait_filled(dve, t, ("kv", p, k))
                        banks.moves(dve.tensor_copy(kv_t[:, k, :], psum_of(t, ("kv", p, k))), t, ("kv", p, k))

                def maximum(p):
                    unit = ("scores", p)
                    banks.wait_filled(dve, t, unit)
                    dve.nop(nofuse=True)
                    banks.moves(dve.tensor_tensor_reduce(probs[:, :], psum_of(t, unit, KV + P), mask[:, :], 1.0, LOWEST,
                                                         ALU.add, ALU.max, top[:, p:p + 1]), t, unit)
                    banks.wait_moved(dve, t, unit)
                    dve.tensor_scalar(low_top[:, p:p + 1], top[:, p:p + 1], -XATTN_SCALE, None, ALU.mult).then_inc(low_top_ready, 1)

                def inverse(p):
                    dve.wait_ge(exp_done, t * TT + (p + 1))
                    dve.reciprocal(inv_total[:, p:p + 1], total[:, p:p + 1]).then_inc(inv_ready, 1)

                def att_second_half(p):
                    dve.wait_ge(att_hi_done, t * TT + (p + 1))
                    banks.moves(dve.scalar_tensor_tensor(att_lo[:, :, :].rearrange("p a b -> p (a b)"), psum_of(t, ("turn", p)), AS,
                                                         att_hi[:, :, :].rearrange("p a b -> p (a b)"), ALU.mult, ALU.subtract),
                                t, ("turn", p))

                def residual(p):
                    if p == 0:
                        dve.wait_ge(res_loaded, t * 16 + 16)
                    banks.wait_filled(dve, t, ("out", p))
                    banks.moves(dve.scalar_tensor_tensor(x1[:, p, :], psum_of(t, ("out", p)), 1.0 / (AS * WS), x1[:, p, :],
                                                         ALU.mult, ALU.add), t, ("out", p))

                def move_all(kind):
                    for e in dves_part[kind]:
                        move((kind, e), home[kind][:, e, :], unscale)

                move_all("q")
                move_all("k")
                move_ctx(0)
                dve.wait_ge(x_loaded, t * 16 + 32)
                layernorm(dve, t + 1, xn, xn, stat, ln_step, xn_ready)
                move(("v", 1), v_new[:, 1, :], unscale)
                for p in range(TT):
                    maximum(p)
                    if p:
                        att_second_half(p - 1)
                    inverse(p)
                    if p + 1 < TT:
                        move_ctx(p + 1)
                    elif not last_tile:
                        second_halves(t, t + 1, (0, 1))
                    if p:
                        residual(p - 1)
                    else:
                        move(("v", 3), v_new[:, 3, :], unscale)
                if not last_tile:
                    second_halves(t, t + 1, (2,))
                att_second_half(TT - 1)
                if not last_tile:
                    second_halves(t, t + 1, (3,))
                residual(TT - 1)

            with nc.vector.Fori(0, NT - 1) as t:
                tile(t, False)
            tile(NT - 1, True)


class Sections:

    def __init__(self, nc, ctx, name, sections):
        self.filled = [ctx.enter_context(nc.semaphore(f"{name}_bank{b}_filled")) for b in range(8)]
        self.moved = [ctx.enter_context(nc.semaphore(f"{name}_bank{b}_moved")) for b in range(8)]
        self.uses = {s: [0] * 8 for s in sections}
        self.where = {}
        for s, units in sections.items():
            for unit, bank in units:
                self.where[unit] = (bank, self.uses[s][bank])
                self.uses[s][bank] += 1

    def bank(self, unit):
        return self.where[unit][0]

    def earlier(self, runs, unit):
        bank, count = self.where[unit]
        for s, n in runs.items():
            if self.uses[s][bank]:
                count = n * self.uses[s][bank] + count
        return count

    def wait_room(self, pe, runs, unit):
        n = self.earlier(runs, unit)
        if not (isinstance(n, int) and n == 0):
            pe.wait_ge(self.moved[self.bank(unit)], n)

    def wait_filled(self, eng, runs, unit):
        eng.wait_ge(self.filled[self.bank(unit)], self.earlier(runs, unit) + 1)

    def wait_moved(self, eng, runs, unit):
        eng.wait_ge(self.moved[self.bank(unit)], self.earlier(runs, unit) + 1)

    def fills(self, ins, unit):
        ins.then_inc(self.filled[self.bank(unit)], 1)

    def moves(self, ins, unit):
        ins.then_inc(self.moved[self.bank(unit)], 1)


HEADS_SMALL = 6


def z_of(z_scratch, hi_or_lo, half, t):
    n = HEADS // 2
    return z_scratch[hi_or_lo, half * n:(half + 1) * n, :, bass.ds(t * TILE, TILE)].rearrange("h d t -> d h t")


def heads_phase(nc, psum, ident, x1_rows, xn, stat, head_weights, hqk_hi, hqk_lo, w_rows, b_q, b_k, b_v, rope_cos, rope_sin, causal, w_o, wo_hi, wo_lo, z_scratch,
                first_z, x1_stored, small_loaded_z_stored):
    with ExitStack() as ctx:
        def sb(name, shape, dt):
            return ctx.enter_context(nc.sbuf_tensor("hd_" + name, shape, dt))

        def sem(name):
            return ctx.enter_context(nc.semaphore("hd_" + name))

        WIDE = HEADS * DH
        SEQS = TILE // S
        wv_hi, wv_lo = sb("wv_hi", [P, KD, WIDE], F16), sb("wv_lo", [P, KD, WIDE], F16)
        xt_hi, xt_lo = sb("xt_hi", [P, KD, TILE], F16), sb("xt_lo", [P, KD, TILE], F16)
        bias = sb("bias", [P, 2, 2, PAIRS], F32)
        bias_v = sb("bias_v", [P, HEADS], F32)
        cos, sin = sb("cos", [P, S], F32), sb("sin", [P, S], F32)
        mask = sb("mask", [P, S], F32)
        products = sb("products", [P, 2, 4, TILE], F32)
        rotated = sb("rotated", [P, 2, 2, TILE], F32)
        v = sb("v", [P, TT, 2 * DH], F32)
        probs = sb("probs", [P, SEQS, S], F32)
        probs_t = sb("probs_t", [P, 2, TT, P], F32)
        top, low_top = sb("top", [P, SEQS], F32), sb("low_top", [P, SEQS], F32)
        total, inv_total = sb("total", [P, SEQS], F32), sb("inv_total", [P, SEQS], F32)
        z_hi, z_lo = sb("z_hi", [P, 2, TILE], F16), sb("z_lo", [P, 2, TILE], F16)

        loaded = [sem("rows0_loaded"), sem("rows1_loaded")]
        w_hi_done, w_lo_done = sem("w_hi_done"), sem("w_lo_done")
        x_loaded, bias_scaled = sem("x_loaded"), sem("bias_scaled")
        wo_scaled, wo_hi_done = sem("wo_scaled"), sem("wo_hi_done")
        ln_step, xn_ready, xt_hi_done = sem("ln_step"), sem("xn_ready"), sem("xt_hi_done")
        added_dve, added_pool = sem("added_dve"), sem("added_pool")
        low_top_ready, exp_done, inv_done, probs_ready = sem("low_top_ready"), sem("exp_done"), sem("inv_done"), sem("probs_ready")
        zeros_set = sem("zeros_set")
        z_hi_done, first_z_loaded = sem("z_hi_done"), sem("first_z_loaded")
        banks = Sections(nc, ctx, "hd", {
            "turn": [(("x", k), k) for k in range(KD)],
            "proj": [(("q", 0), 0), (("q", 1), 1), (("k", 0), 2), (("k", 1), 3), (("v", 0), 6), (("v", 1), 7)],
            "att": [("scores", 4), ("probs", 5), (("z", 0), 0), (("z", 1), 1)],
        })

        def psum_of(unit):
            return psum[:, banks.bank(unit), :]

        def rows_of(first):
            return x1_rows[bass.ds(first, TILE), :].rearrange("(b p) d -> p b d", p=P)

        class Step:

            def __init__(self, a, turns, pair, next_pair, turn_next=False, att=True, proj=True, first_of=None):
                self.a, self.pair, self.next_pair = a, pair, next_pair
                self.first_token = (turns - 1) * TILE
                self.turn_next, self.att, self.proj = turn_next, att, proj
                self.first_of = first_of
                self.turns = turns
                self.runs_scores = {"att": a}
                self.runs_turn = {"turn": turns, "proj": a + 1, "att": a}
                self.turns_now = turns + 1 if turn_next else turns
                g = a + 1
                self.runs_proj = {"turn": self.turns_now, "proj": g, "att": a if att else 0}
                self.runs_z = {"turn": self.turns_now, "proj": g + 1 if proj else g, "att": a}

        def for_each_step(eng, on_the_side, step):
            step(Step(-1, 1, None, 0, att=False))
            def tile(t, last_tile):
                step(Step(t * PAIRS, t + 1, 0, 1, first_of=None if last_tile else t))
                on_the_side(t, last_tile)
                with eng.Fori(1, PAIRS - 1) as n:
                    step(Step(t * PAIRS + n, t + 1, n, n + 1))
                if not last_tile:
                    step(Step(t * PAIRS + (PAIRS - 1), t + 1, PAIRS - 1, 0, turn_next=True))
            with eng.Fori(0, NT - 1) as t:
                tile(t, False)
            tile(NT - 1, True)
            step(Step(NT * PAIRS - 1, NT, PAIRS - 1, None, proj=False))

        block = ctx.enter_context(nc.Block())

        @block.sync
        def _(sp):
            for dst, src in ((cos, rope_cos), (sin, rope_sin), (mask, causal)):
                sp.dma_start(dst[:, :], src).then_inc(small_loaded_z_stored, 16)
            for w, b in enumerate((b_q, b_k)):
                sp.dma_start(bias[:, w, :, :], b).then_inc(small_loaded_z_stored, 16)
            sp.dma_start(bias_v[:, :], b_v).then_inc(small_loaded_z_stored, 16)
            for k in range(2, KD):
                sp.wait_ge(w_lo_done, k - 1)
                sp.dma_start(w_rows[:, k % 2, :], head_weights[(2 * KD + k) * P:(2 * KD + k + 1) * P, :]).then_inc(loaded[k % 2], 16)

            def on_the_side(t, last_tile):
                if not last_tile:
                    load_wo(t + 1)

            def load_first_z():
                sp.wait_ge(w_lo_done, KD + NT)
                sp.wait_ge(small_loaded_z_stored, 16 * (HEADS_SMALL + 2 * (NT - 1) * PAIRS))
                for half in range(2):
                    sp.dma_start(first_z[half], z_of(z_scratch, half, 0, 0)).then_inc(first_z_loaded, 16)

            def load_wo(t):
                sp.wait_ge(w_lo_done, t + KD)
                sp.nop(nofuse=True)
                sp.dma_start(w_rows[:, 0, :], w_o[:, bass.ds(t * (4 * D), 4 * D)]).then_inc(loaded[0], 16)

            def step(s):
                if not s.att:
                    load_wo(0)
                    return
                if not s.proj:
                    load_first_z()
                if s.first_of is not None:
                    t = s.first_of
                    sp.wait_ge(x1_stored, 16 + 16 * NT * TT)
                    sp.wait_ge(xt_hi_done, t * KD + KD)
                    sp.nop(nofuse=True)
                    sp.dma_start(xn[:, :, :], rows_of(t * TILE + TILE)).then_inc(x_loaded, 16)
                for h in range(2):
                    banks.wait_moved(sp, s.runs_z, ("z", h))
                    sp.nop(nofuse=True)
                for half, z in enumerate((z_hi, z_lo)):
                    sp.dma_start(z_scratch[half, bass.ds(s.pair * 2, 2), :, bass.ds(s.first_token, TILE)].rearrange("h d t -> d h t"),
                                 z[:, :, :]).then_inc(small_loaded_z_stored, 16)

            for_each_step(nc.sync, on_the_side, step)
            sp.wait_ge(first_z_loaded, 32)

        @block.gpsimd
        def _(pool):
            def step(s):
                if not s.proj:
                    return
                for w in range(2):
                    banks.wait_moved(pool, s.runs_proj, ("qk"[w], 1))
                    pool.tensor_tensor(rotated[0:HALF, w, 0, :], products[0:HALF, w, 0, :], products[0:HALF, w, 2, :], ALU.subtract)
                    pool.tensor_tensor(rotated[HALF:P, w, 1, :], products[HALF:P, w, 1, :], products[HALF:P, w, 3, :],
                                       ALU.add).then_inc(added_pool, 1)

            def on_the_side(t, last_tile):
                pool.wait_ge(added_pool, t * (2 * PAIRS) + 4)
                pool.wait_ge(wo_hi_done, t + 1)
                pool.nop(nofuse=True)
                pool.tensor_tensor(wo_lo[:, bass.ds(t * 4, 4), :].rearrange("p n m -> p (n m)"), w_rows[:, 0, :],
                                   wo_hi[:, bass.ds(t * 4, 4), :].rearrange("p n m -> p (n m)"), ALU.subtract).then_inc(w_lo_done, 1)
                pool.wait_ge(w_lo_done, t + (KD + 1))
                pool.nop(nofuse=True)

            for_each_step(nc.gpsimd, on_the_side, step)

        @block.tensor
        def _(pe):
            def turn_xn(runs, nth):
                if nth is not None:
                    pe.wait_ge(xn_ready, nth * TT)
                for k in range(KD):
                    banks.wait_room(pe, runs, ("x", k))
                    for i in range(TT):
                        last = pe.transpose(psum_of(("x", k))[:, i * P:(i + 1) * P], xn[:, i, k * P:(k + 1) * P], ident[:, :])
                    banks.fills(last, ("x", k))

            turn_xn({}, None)
            for k in range(KD):
                banks.wait_moved(pe, {}, ("x", k))
            xt = [(xt_hi[:, k, :], xt_lo[:, k, :]) for k in range(KD)]

            def project(s, w, half):
                unit = ("qk"[w], half)
                banks.wait_room(pe, s.runs_proj, unit)
                pair = s.next_pair
                cols = bass.ds(pair * DH + half * (WIDE // 2), DH)
                left = [(hqk_hi[:, w * KD + k, cols], hqk_lo[:, w * KD + k, cols]) for k in range(KD)]
                banks.fills(three_passes(pe, psum_of(unit), left, xt), unit)

            def step(s):
                if s.turn_next:
                    turn_xn(s.runs_turn, s.turns)
                if s.att:
                    pe.wait_ge(added_dve, s.a * 2 + 2)
                    pe.wait_ge(added_pool, s.a * 2 + 2)
                    banks.wait_room(pe, s.runs_scores, "scores")
                    for n in range(SEQS):
                        cols = slice(n * S, (n + 1) * S)
                        for h in range(2):
                            last = pe.matmul(psum_of("scores")[h * S:(h + 1) * S, cols], rotated[:, 0, h, cols],
                                             rotated[:, 1, h, cols], start=True, stop=True, skip_group_check=True)
                    banks.fills(last, "scores")
                if s.turn_next:
                    for k in range(KD):
                        banks.wait_moved(pe, s.runs_turn, ("x", k))
                if s.proj:
                    project(s, 0, 0)
                    project(s, 0, 1)
                    project(s, 1, 0)
                if s.att:
                    pe.wait_ge(probs_ready, s.a + 1)
                    banks.wait_room(pe, s.runs_scores, "probs")
                    for i in range(TT):
                        last = pe.transpose(psum_of("probs")[:, i * P:(i + 1) * P],
                                            probs[:, 2 * i:2 * i + 2, :].rearrange("p n k -> p (n k)"), ident[:, :])
                    banks.fills(last, "probs")
                if s.proj:
                    project(s, 1, 1)
                if s.att:
                    for half in range(2):
                        banks.wait_moved(pe, {"turn": s.turns, "proj": s.a}, ("v", half))
                    banks.wait_moved(pe, s.runs_scores, "probs")
                    for h in range(2):
                        unit = ("z", h)
                        banks.wait_room(pe, s.runs_z, unit)
                        for i in range(TT):
                            last = pe.matmul(psum_of(unit)[:, i * P:(i + 1) * P], v[:, i, h * DH:(h + 1) * DH], probs_t[:, h, i, :],
                                             start=True, stop=True)
                        banks.fills(last, unit)
                if not s.att:
                    pe.wait_ge(w_lo_done, KD)
                if s.proj:
                    for half in range(2):
                        unit = ("v", half)
                        banks.wait_room(pe, s.runs_proj, unit)
                        pair_cols = bass.ds(s.next_pair * (2 * DH), 2 * DH)
                        right = [(wv_hi[:, k, pair_cols], wv_lo[:, k, pair_cols]) for k in range(KD)]
                        for i in range(2):
                            cols = slice((2 * half + i) * P, (2 * half + i + 1) * P)
                            last = three_passes(pe, psum_of(unit)[:, i * 2 * DH:(i + 1) * 2 * DH],
                                                [(xt_hi[:, k, cols], xt_lo[:, k, cols]) for k in range(KD)], right)
                        banks.fills(last, unit)

            for_each_step(nc.tensor, lambda t, last_tile: None, step)

        @block.scalar
        def _(act):
            def first_halves(runs):
                for k in range(KD):
                    banks.wait_filled(act, runs, ("x", k))
                    act.activation(xt_hi[:, k, :], psum_of(("x", k)), ACT.Copy).then_inc(xt_hi_done, 1)

            first_halves({})
            for k in range(KD):
                if k >= 2:
                    act.wait_ge(loaded[k % 2], 16)
                act.activation(wv_hi[:, k, :], w_rows[:, k % 2, :], ACT.Copy, scale=WS).then_inc(w_hi_done, 1)

            def step(s):
                if s.turn_next:
                    first_halves(s.runs_turn)
                if s.att:
                    act.wait_ge(low_top_ready, s.a + 1)
                    for n in range(SEQS):
                        last = act.activation(probs[:, n, :], probs[:, n, :], ACT.Exp, bias=low_top[:, n:n + 1],
                                              scale=HEAD_SCALE, accum_out=total[:, n:n + 1])
                    last.then_inc(exp_done, 1)
                    banks.wait_filled(act, s.runs_scores, "probs")
                    for n in range(2):
                        keys = slice(n * S, (n + 1) * S)
                        last = act.activation(probs_t[keys, :, :, keys], psum_of("probs")[keys, :].rearrange("p (i h q) -> p h i q", h=2, q=S),
                                              ACT.Copy)
                    banks.moves(last, "probs")
                    for h in range(2):
                        banks.wait_filled(act, s.runs_z, ("z", h))
                        if h == 0:
                            act.wait_ge(small_loaded_z_stored, s.a * 32 + 16 * HEADS_SMALL)
                            act.nop(nofuse=True)
                        act.activation(z_hi[:, h, :], psum_of(("z", h)), ACT.Identity,
                                       bias=bias_v[:, bass.ds(s.pair * 2 + h, 1)]).then_inc(z_hi_done, 1)
                if s.proj:
                    for half in range(2):
                        unit = ("v", half)
                        banks.wait_filled(act, s.runs_proj, unit)
                        banks.moves(act.activation(v[:, 2 * half:2 * half + 2, :].rearrange("p i d -> p (i d)"), psum_of(unit), ACT.Copy,
                                                   scale=AS / (XS * WS)), unit)

            act.wait_ge(bias_scaled, 2)
            act.wait_ge(zeros_set, 1)

            def on_the_side(t, last_tile):
                act.wait_ge(loaded[0], t * 16 + 32)
                act.activation(w_rows[:, 0, :], w_rows[:, 0, :], ACT.Copy, scale=WS).then_inc(wo_scaled, 1)
                act.wait_ge(wo_scaled, t + 1)
                act.activation(wo_hi[:, bass.ds(t * 4, 4), :].rearrange("p n m -> p (n m)"), w_rows[:, 0, :], ACT.Copy).then_inc(wo_hi_done, 1)
            for_each_step(nc.scalar, on_the_side, step)

        @block.vector
        def _(dve):
            def second_halves(runs, nth):
                for k in range(KD):
                    dve.wait_ge(xt_hi_done, nth * KD + (k + 1))
                    banks.moves(dve.tensor_tensor(xt_lo[:, k, :], psum_of(("x", k)), xt_hi[:, k, :], ALU.subtract), ("x", k))

            second_halves({}, 0)
            for k in range(KD):
                dve.wait_ge(w_hi_done, k + 1)
                dve.scalar_tensor_tensor(wv_lo[:, k, :], w_rows[:, k % 2, :], WS, wv_hi[:, k, :],
                                         ALU.mult, ALU.subtract).then_inc(w_lo_done, 1)
            dve.wait_ge(small_loaded_z_stored, 16 * HEADS_SMALL)
            dve.tensor_scalar(bias[:, :, :, :].rearrange("p a b q -> p (a b q)"), bias[:, :, :, :].rearrange("p a b q -> p (a b q)"),
                              XS * WS, None, ALU.mult).then_inc(bias_scaled, 1)
            dve.tensor_scalar(bias_v[:, :], bias_v[:, :], AS, None, ALU.mult).then_inc(bias_scaled, 1)
            dve.wait_ge(bias_scaled, 2)

            dve.memset(probs_t[:, :, :, :], 0.0).then_inc(zeros_set, 1)

            def by_sequence(ap):
                return ap.rearrange("p (s n) -> p s n", n=S)

            def table(t):
                return t[:, :].unsqueeze(1).broadcast_to([P, TILE // S, S])

            def on_the_side(t, last_tile):
                if not last_tile:
                    layernorm(dve, t, xn, xn, stat, ln_step, xn_ready, parts=(2,))

            def rotate(s, w):
                for half, (first, second) in enumerate((((cos, 0), (sin, 1)), ((sin, 2), (cos, 3)))):
                    unit = ("qk"[w], half)
                    banks.wait_filled(dve, s.runs_proj, unit)
                    for tab, slot in (first, second):
                        last = dve.scalar_tensor_tensor(by_sequence(products[:, w, slot, :]), by_sequence(psum_of(unit)),
                                                        bias[:, w, half, bass.ds(s.next_pair, 1)], table(tab), ALU.add, ALU.mult)
                    banks.moves(last, unit)
                banks.wait_moved(dve, s.runs_proj, ("qk"[w], 1))
                dve.tensor_tensor(rotated[HALF:P, w, 0, :], products[0:HALF, w, 1, :], products[0:HALF, w, 3, :], ALU.add)
                dve.tensor_tensor(rotated[0:HALF, w, 1, :], products[HALF:P, w, 0, :], products[HALF:P, w, 2, :],
                                  ALU.subtract).then_inc(added_dve, 1)

            def step(s):
                if s.turn_next:
                    second_halves(s.runs_turn, s.turns)
                if s.att:
                    banks.wait_filled(dve, s.runs_scores, "scores")
                    dve.nop(nofuse=True)
                    for n in range(SEQS):
                        last = dve.tensor_tensor_reduce(probs[:, n, :], psum_of("scores")[:, n * S:(n + 1) * S], mask[:, :], 1.0, LOWEST,
                                                        ALU.add, ALU.max, top[:, n:n + 1])
                    banks.moves(last, "scores")
                    banks.wait_moved(dve, s.runs_scores, "scores")
                    dve.tensor_scalar(low_top[:, :], top[:, :], -HEAD_SCALE, None, ALU.mult).then_inc(low_top_ready, 1)
                    dve.wait_ge(exp_done, s.a + 1)
                    dve.reciprocal(inv_total[:, :], total[:, :]).then_inc(inv_done, 1)
                    dve.wait_ge(inv_done, s.a + 1)
                    dve.tensor_tensor(probs[:, :, :], probs[:, :, :], inv_total[:, :].unsqueeze(2).broadcast_to([P, SEQS, S]),
                                      ALU.mult).then_inc(probs_ready, 1)
                if s.first_of is not None:
                    t = s.first_of
                    dve.wait_ge(x_loaded, t * 16 + 16)
                    layernorm(dve, t, xn, xn, stat, ln_step, xn_ready, parts=(1,))
                if s.proj:
                    rotate(s, 0)
                    rotate(s, 1)
                if s.att:
                    for h in range(2):
                        dve.wait_ge(z_hi_done, s.a * 2 + (h + 1))
                        banks.moves(dve.scalar_tensor_tensor(z_lo[:, h, :], psum_of(("z", h)), bias_v[:, bass.ds(s.pair * 2 + h, 1)],
                                                             z_hi[:, h, :], ALU.add, ALU.subtract), ("z", h))

            for_each_step(nc.vector, on_the_side, step)


ZW_UNSCALE = 1.0 / (AS * WS)
FS = 2.0 ** 6
HS = 1.0 / FS
FP4_AS_F16 = 2.0 ** 14
GU = 2 * FF
WORDS_DOWN = FF // 8
WORDS = 16
WHOLE = P
REST = (WORDS_DOWN - WHOLE) // 16


def decode_fp4(dve, last, codes, sign, magnitude, shift):
    dve.tensor_scalar(sign, codes, 12 - shift, 0x8000, ALU.logical_shift_left, ALU.bitwise_and)
    if shift <= 9:
        last(dve.tensor_scalar(magnitude, codes, 9 - shift, 0x0E00, ALU.logical_shift_left, ALU.bitwise_and))
    else:
        last(dve.tensor_scalar(magnitude, codes, shift - 9, 0x0E00, ALU.logical_shift_right, ALU.bitwise_and))
    last(dve.tensor_tensor(sign, sign, magnitude, ALU.bitwise_or))


def merge_phase(nc, psum, z_scratch, x1_rows, b_o, wo_hi, wo_lo, gu_codes, gu_scales, down_codes, down_scales, shifts,
                first_z, z_stored, x2, xn, stat, gu, gu_scale, down_hi, down_lo):
    with ExitStack() as ctx:
        def sb(name, shape, dt):
            return ctx.enter_context(nc.sbuf_tensor("mg_" + name, shape, dt))

        def sem(name):
            return ctx.enter_context(nc.semaphore("mg_" + name))

        HH = HEADS // 2
        z_pairs = first_z, (sb("z_hi", [P, HH, TILE], F16)[:, :, :], sb("z_lo", [P, HH, TILE], F16)[:, :, :])
        b_o_all = sb("b_o_all", [P, D], F32)
        codes = sb("codes", [P, 2, GU], I32)
        gu_scale_f16 = sb("gu_scale_f16", [P, KD * 2 * FB], F16)
        down_c = sb("down_c", [P, 1 + REST, D], I32)
        down_scale = sb("down_scale", [P, 1 + REST, D], F16)
        shift = sb("shift", [P, 1], I32)
        PIECE, HALF_DOWN = 352, D // 2
        sign, magnitude = sb("sign", [P, PIECE], I32), sb("magnitude", [P, PIECE], I32)
        value = sb("value", [P, 2, PIECE], F32)
        gu_loaded, small_loaded = [sem("gu0_loaded"), sem("gu1_loaded")], sem("small_loaded")
        down_loaded, step, gu_decoded = sem("down_loaded"), sem("step"), sem("gu_decoded")
        hi_done, lo_done, value_ready = sem("hi_done"), sem("lo_done"), sem("value_ready")
        x1_loaded, b_loaded, x1_ready = sem("x1_loaded"), sem("b_loaded"), sem("x1_ready")
        z_loaded = [sem("z0_loaded"), sem("z1_loaded")]
        z_used = [sem("z0_used"), sem("z1_used")]
        scale_ready = sem("scale_ready")
        merged, added, ln_step, xn_ready = sem("merged"), sem("added"), sem("ln_step"), sem("xn_ready")

        def bank_of(t, i):
            return t % 2 * TT + i

        block = ctx.enter_context(nc.Block())

        gu_jobs = [(g, slice(c, c + PIECE)) for g in range(KD) for c in range(0, GU, PIECE)]
        jobs = []
        for j in range(8 + REST):
            row, bit = (0, 4 * j) if j < 8 else (j - 7, 0)
            for c in range(0, D, HALF_DOWN):
                at = slice(c, c + HALF_DOWN)
                jobs.append((down_c[:, row, at], bit, down_scale[:, row, at], down_hi[:, j, at], down_lo[:, j, at]))
        SMALL, DOWN_LOADS = 2, 1 + 8 + 2 * REST

        @block.sync
        def _(sp):
            def load_z(t, half):
                for hi_or_lo, z in enumerate(z_pairs[half]):
                    sp.dma_start(z, z_of(z_scratch, hi_or_lo, half, t)).then_inc(z_loaded[half], 16)

            load_z(0, 1)
            sp.dma_start(x2[:, :, :], x1_rows.rearrange("(b p) d -> p b d", p=P)).then_inc(x1_loaded, 16)
            sp.dma_start(b_o_all[:, :], b_o.broadcast_to([P, D])).then_inc(b_loaded, 16)
            sp.dma_start(shift[:, :], shifts).then_inc(small_loaded, 16)
            sp.dma_start(gu_scale_f16[:, :], gu_scales).then_inc(small_loaded, 16)

            def load_codes(g):
                words = gu_codes[WORDS * g:WORDS * (g + 1), :]
                sp.dma_start(codes[:, g % 2, :], words.unsqueeze(0).broadcast_to([8, WORDS, GU])).then_inc(gu_loaded[g % 2], 16)
            load_codes(0)
            load_codes(1)
            sp.dma_start(down_c[:, 0, :], down_codes[0:WHOLE, :]).then_inc(down_loaded, 16)
            for g in range(8):
                sp.dma_start(down_scale[16 * g:16 * g + 16, 0, :], down_scales[g:g + 1, :].broadcast_to([16, D])).then_inc(down_loaded, 16)
            for q in range(REST):
                words = down_codes[WHOLE + 16 * q:WHOLE + 16 * q + 16, :]
                sp.dma_start(down_c[:, 1 + q, :], words.unsqueeze(0).broadcast_to([8, 16, D])).then_inc(down_loaded, 16)
                sp.dma_start(down_scale[:, 1 + q, :], down_scales[8 + q:9 + q, :].broadcast_to([P, D])).then_inc(down_loaded, 16)
            for t in range(1, NT):
                if t == NT - 1:
                    sp.wait_ge(z_stored, 16 * (HEADS_SMALL + 2 * NT * PAIRS))
                for half in range(2):
                    sp.wait_ge(z_used[half], t)
                    load_z(t, half)
                if t <= 2:
                    sp.wait_ge(gu_decoded, t)
                    load_codes(t + 1)

        @block.gpsimd
        def _(pool):
            pool.wait_ge(b_loaded, 16)
            pool.wait_ge(x1_loaded, 16)
            for b in range(NT * TT):
                pool.tensor_tensor(x2[:, b, :], x2[:, b, :], b_o_all[:, :], ALU.add).then_inc(x1_ready, 1)
            for n, (_, _, _, hi, lo) in enumerate(jobs):
                pool.wait_ge(hi_done, n + 1)
                pool.tensor_tensor(lo, value[:, n % 2, 0:hi.shape[-1]], hi, ALU.subtract).then_inc(lo_done, 1)

        @block.tensor
        def _(pe):
            for t in range(NT):
                for half in range(2):
                    if half or t:
                        pe.wait_ge(z_loaded[half], 32 * (t + half))
                    z_hi, z_lo = z_pairs[half]
                    for i in range(TT):
                        at = slice(i * P, (i + 1) * P)
                        bank = bank_of(t, i)
                        if half == 0 and t >= 2:
                            pe.wait_ge(added, (t - 2) * TT + (i + 1))
                        for n in range(HH):
                            head = half * HH + n
                            pe.matmul(psum[:, bank, :], z_hi[:, n, at], wo_hi[:, head, :], start=(head == 0), stop=False)
                            pe.matmul(psum[:, bank, :], z_hi[:, n, at], wo_lo[:, head, :], start=False, stop=False)
                            last = pe.matmul(psum[:, bank, :], z_lo[:, n, at], wo_hi[:, head, :], start=False, stop=(head == HEADS - 1))
                        if half == 1 and i < TT - 1:
                            last.then_inc(merged, 1)
                    last.then_inc(z_used[half], 1)

        @block.scalar
        def _(act):
            for n, (_, _, _, hi, _) in enumerate(jobs):
                act.wait_ge(value_ready, n + 1)
                act.activation(hi, value[:, n % 2, 0:hi.shape[-1]], ACT.Copy).then_inc(hi_done, 1)

        @block.vector
        def _(dve):
            n = [0]

            def last(ins):
                n[0] += 1
                ins.then_inc(step, 1)
                dve.wait_ge(step, n[0])

            def decode_gu(job):
                g, at = gu_jobs[job]
                if job == 0:
                    dve.wait_ge(small_loaded, 16 * SMALL)
                    dve.tensor_scalar(gu_scale[:, :], gu_scale_f16[:, :], 1.0, None, ALU.mult).then_inc(scale_ready, 1)
                if at.start == 0:
                    dve.wait_ge(gu_loaded[g % 2], 16 * (g // 2 + 1))
                    last(dve.tensor_scalar(codes[:, g % 2, :], codes[:, g % 2, :], shift[:, 0:1], None, ALU.logical_shift_right))
                decode_fp4(dve, last, codes[:, g % 2, at], sign[:, :], magnitude[:, :], 0)
                value_f16 = sign[:, :].bitcast(F16).rearrange("p (n two) -> p n two", two=2)[:, :, 0]
                decoded = dve.tensor_scalar(gu[:, g, at], value_f16, FP4_AS_F16, None, ALU.mult)
                if at.stop == GU:
                    decoded.then_inc(gu_decoded, 1)
                    dve.wait_ge(gu_decoded, g + 1)
                else:
                    last(decoded)

            def decode(job):
                if job == 0:
                    dve.wait_ge(down_loaded, 16 * DOWN_LOADS)
                    for q in range(REST):
                        last(dve.tensor_scalar(down_c[:, 1 + q, :], down_c[:, 1 + q, :], shift[:, 0:1], None, ALU.logical_shift_right))
                c, bit, scale, hi, lo = jobs[job]
                w = hi.shape[-1]
                if job:
                    dve.wait_ge(value_ready, job)
                if bit > 12:
                    last(dve.tensor_scalar(magnitude[:, 0:w], c, 16, None, ALU.logical_shift_right))
                    c, bit = magnitude[:, 0:w], bit - 16
                decode_fp4(dve, last, c, sign[:, 0:w], magnitude[:, 0:w], bit)
                if job >= 2:
                    dve.wait_ge(lo_done, job - 1)
                as_f16 = sign[:, 0:w].bitcast(F16).rearrange("p (n two) -> p n two", two=2)[:, :, 0]
                dve.scalar_tensor_tensor(value[:, job % 2, 0:w], as_f16, FP4_AS_F16 * FS, scale, ALU.mult, ALU.mult).then_inc(value_ready, 1)

            def add(t, i):
                if i < TT - 1:
                    dve.wait_ge(merged, t * (TT - 1) + i + 1)
                else:
                    dve.wait_ge(z_used[1], t + 1)
                b = t * TT + i
                dve.wait_ge(x1_ready, b + 1)
                dve.scalar_tensor_tensor(x2[:, b, :], psum[:, bank_of(t, i), :], ZW_UNSCALE, x2[:, b, :], ALU.mult, ALU.add).then_inc(added, 1)

            steps = [(decode_gu, n) for n in range(len(gu_jobs))] + [(decode, n) for n in range(len(jobs))]
            share = -(-len(steps) // (NT * TT))
            for b in range(NT * TT):
                for decode_piece, job in steps[b * share:(b + 1) * share]:
                    decode_piece(job)
                add(b // TT, b % TT)
                if b == TT - 1:
                    dve.wait_ge(added, TT)
                    layernorm(dve, 0, x2[:, 0:TT, :], xn, stat, ln_step, xn_ready, by_code=True)


def ffn_phase(nc, psum, ident, x2, xn, stat, gu, gu_scale, down_hi, down_lo, out_rows):
    with ExitStack() as ctx:
        def sb(name, shape, dt):
            return ctx.enter_context(nc.sbuf_tensor("ff_" + name, shape, dt))

        def sem(name):
            return ctx.enter_context(nc.semaphore("ff_" + name))

        UNITS, SLOTS = 2 * FB, 5
        xt_hi, xt_lo = sb("xt_hi", [P, KD, TILE], F16), sb("xt_lo", [P, KD, TILE], F16)
        part = sb("part", [P, SLOTS, 2, TILE], F32)
        gate = sb("gate", [P, 2, TILE], F32)
        hidden = sb("hidden", [P, 2, TILE], F32)
        h_hi, h_lo = sb("h_hi", [P, FB, TILE], F16), sb("h_lo", [P, FB, TILE], F16)
        result = sb("result", [P, TT, D], F32)
        squares = sb("squares", [P, TT], F32)
        rms = {k: sb("rms_" + k, [P, TT], I32 if k == "half" else F32) for k in ("var", "half", "y", "y2")}

        ln_step, xn_ready, xt_hi_done, out_stored = sem("ln_step"), sem("xn_ready"), sem("xt_hi_done"), sem("out_stored")
        h_hi_done, h_lo_done = sem("h_hi_done"), sem("h_lo_done")
        squares_done, rms_step = sem("squares_done"), sem("rms_step")
        summed, silu_done, hidden_done = sem("summed"), sem("silu_done"), sem("hidden_done")

        warm = [(("warm", i), i) for i in range(4)]
        turn = [(("x", k), 4 + k) for k in range(KD)]
        hid = [((u, g), (4 + 4 * u + g) % 8) for u in range(UNITS) for g in range(KD)]
        banks = Banks(nc, ctx, "ff", warm + turn, hid + [(("y", i), i) for i in range(TT - 1)] + turn + [(("y", TT - 1), TT - 1)])

        def psum_of(t, unit):
            return psum[:, banks.bank(t, unit), :]

        def block_of(i):
            return slice(i * P, (i + 1) * P)

        def scale_of(u, g):
            at = (u % 2 * FB + u // 2) * KD + g
            return gu_scale[:, at:at + 1]

        block = ctx.enter_context(nc.Block())

        @block.sync
        def _(sp):
            with nc.sync.Fori(0, NT) as t:
                for first, n in ((0, TT - 1), (TT - 1, 1)):
                    banks.wait_moved(sp, t, ("y", first + n - 1))
                    sp.nop(nofuse=True)
                    sp.dma_start(out_rows[bass.ds(t * TILE + first * P, n * P), :].rearrange("(b p) d -> p b d", p=P),
                                 result[:, first:first + n, :]).then_inc(out_stored, 16)
            sp.wait_ge(out_stored, 32 * NT)

        @block.gpsimd
        def _(pool):
            with nc.gpsimd.Fori(0, NT) as t:
                for b in range(FB + 2):
                    for u in (2 * b, 2 * b + 1) if b < FB else ():
                        for g in (2, 3):
                            banks.wait_moved(pool, t, (u, g))
                            pool.nop(nofuse=True)
                        pool.tensor_tensor(part[:, u % SLOTS, 0, :], part[:, u % SLOTS, 0, :], part[:, u % SLOTS, 1, :],
                                           ALU.add).then_inc(summed, 1)
                    if b >= 2:
                        pool.wait_ge(h_hi_done, t * FB + (b - 1))
                        pool.tensor_tensor(h_lo[:, b - 2, :], hidden[:, b % 2, :], h_hi[:, b - 2, :], ALU.subtract).then_inc(h_lo_done, 1)

        @block.tensor
        def _(pe):
            def turn_xn(t, nth):
                if t is not None:
                    pe.wait_ge(xn_ready, nth * TT)
                for k in range(KD):
                    banks.wait_room(pe, t, ("x", k))
                    for i in range(TT):
                        last = pe.transpose(psum_of(t, ("x", k))[:, block_of(i)], xn[:, i, block_of(k)], ident[:, :])
                    banks.fills(last, t, ("x", k))

            turn_xn(None, 0)
            for unit, _ in warm:
                last = pe.transpose(psum_of(None, unit)[:, 0:P], ident[:, :], ident[:, :])
                banks.fills(last, None, unit)

            def tile(t, last_tile):
                for k in range(KD):
                    banks.wait_moved_before(pe, t, ("x", k))
                for u in range(UNITS):
                    first = u % 2 * FF + u // 2 * P
                    for g in range(KD):
                        banks.wait_room(pe, t, (u, g))
                        pe.matmul(psum_of(t, (u, g)), gu[:, g, first:first + P], xt_hi[:, g, :], start=True, stop=False)
                        last = pe.matmul(psum_of(t, (u, g)), gu[:, g, first:first + P], xt_lo[:, g, :], start=False, stop=True)
                        banks.fills(last, t, (u, g))
                for i in range(TT):
                    if i == TT - 1 and not last_tile:
                        turn_xn(t, t + 1)
                    banks.wait_room(pe, t, ("y", i))
                    for b in range(FB):
                        if i == 0:
                            pe.wait_ge(h_lo_done, t * FB + (b + 1))
                        pe.matmul(psum_of(t, ("y", i)), h_hi[:, b, block_of(i)], down_hi[:, b, :], start=(b == 0), stop=False)
                        pe.matmul(psum_of(t, ("y", i)), h_hi[:, b, block_of(i)], down_lo[:, b, :], start=False, stop=False)
                        last = pe.matmul(psum_of(t, ("y", i)), h_lo[:, b, block_of(i)], down_hi[:, b, :], start=False, stop=(b == FB - 1))
                    banks.fills(last, t, ("y", i))

            with nc.tensor.Fori(0, NT - 1) as t:
                tile(t, False)
            tile(NT - 1, True)

        @block.scalar
        def _(act):
            def first_halves(t):
                for k in range(KD):
                    banks.wait_filled(act, t, ("x", k))
                    act.activation(xt_hi[:, k, :], psum_of(t, ("x", k)), ACT.Copy).then_inc(xt_hi_done, 1)

            first_halves(None)
            for i, (unit, _) in enumerate(warm):
                banks.wait_filled(act, None, unit)
                banks.moves(act.activation(squares[:, i:i + 1], psum_of(None, unit)[:, 0:1], ACT.Copy), None, unit)

            def tile(t, last_tile):
                def scale_groups(u):
                    if u >= SLOTS:
                        b = (u - SLOTS) // 2
                        act.wait_ge(hidden_done if u % 2 == 0 else silu_done, t * FB + (b + 1))
                        act.nop(nofuse=True)
                    for g in range(2):
                        banks.wait_filled(act, t, (u, g))
                        banks.moves(act.activation(part[:, u % SLOTS, g, :], psum_of(t, (u, g)), ACT.Copy, scale=scale_of(u, g)), t, (u, g))

                def silu(b):
                    if b >= 2:
                        act.wait_ge(hidden_done, t * FB + (b - 1))
                        act.nop(nofuse=True)
                    act.wait_ge(summed, t * UNITS + (2 * b + 1))
                    act.activation(gate[:, b % 2, :], part[:, 2 * b % SLOTS, 0, :], ACT.Silu, scale=1.0 / XS).then_inc(silu_done, 1)

                for b in range(FB + 2):
                    if b < FB:
                        scale_groups(2 * b)
                    if 1 <= b <= FB:
                        silu(b - 1)
                    if b < FB:
                        scale_groups(2 * b + 1)
                    if b >= 2:
                        act.wait_ge(hidden_done, t * FB + (b - 1))
                        act.activation(h_hi[:, b - 2, :], hidden[:, b % 2, :], ACT.Copy).then_inc(h_hi_done, 1)
                for i in range(TT):
                    if i == TT - 1 and not last_tile:
                        first_halves(t)
                    banks.wait_filled(act, t, ("y", i))
                    if i >= 2:
                        act.wait_ge(squares_done, t * TT + (i - 1))
                    act.activation(gate[:, i % 2, :], psum_of(t, ("y", i)), ACT.Square,
                                   accum_out=squares[:, i:i + 1]).then_inc(squares_done, 1)
                act.wait_ge(squares_done, t * TT + TT)
                act.nop(nofuse=True)

            with nc.scalar.Fori(0, NT - 1) as t:
                tile(t, False)
            tile(NT - 1, True)

        @block.vector
        def _(dve):
            def second_halves(t, nth):
                for k in range(KD):
                    dve.wait_ge(xt_hi_done, nth * KD + (k + 1))
                    banks.moves(dve.tensor_tensor(xt_lo[:, k, :], psum_of(t, ("x", k)), xt_hi[:, k, :], ALU.subtract), t, ("x", k))

            second_halves(None, 0)

            def tile(t, first_tile, last_tile):
                def scale_and_add(u):
                    for g in (2, 3):
                        banks.wait_filled(dve, t, (u, g))
                        banks.wait_moved(dve, t, (u, g - 2))
                        dve.nop(nofuse=True)
                        to = part[:, u % SLOTS, g - 2, :]
                        banks.moves(dve.scalar_tensor_tensor(to, psum_of(t, (u, g)), scale_of(u, g), to, ALU.mult, ALU.add), t, (u, g))

                def gated(b):
                    dve.wait_ge(summed, t * UNITS + (2 * b + 2))
                    dve.nop(nofuse=True)
                    if b >= 2:
                        dve.wait_ge(h_lo_done, t * FB + (b - 1))
                        dve.nop(nofuse=True)
                    dve.wait_ge(silu_done, t * FB + (b + 1))
                    dve.scalar_tensor_tensor(hidden[:, b % 2, :], part[:, (2 * b + 1) % SLOTS, 0, :], HS / XS, gate[:, b % 2, :],
                                             ALU.mult, ALU.mult).then_inc(hidden_done, 1)

                for b in range(FB + 1):
                    if b < FB:
                        scale_and_add(2 * b)
                        scale_and_add(2 * b + 1)
                    if b:
                        gated(b - 1)
                if not last_tile:
                    layernorm(dve, t, x2[:, bass.ds(t * TT + TT, TT), :], xn, stat, ln_step, xn_ready, by_code=True)
                    second_halves(t, t + 1)
                for part_, blocks in enumerate((range(TT - 1), range(TT - 1, TT))):
                    at = slice(blocks.start, blocks.stop)
                    dve.wait_ge(squares_done, t * TT + blocks.stop)
                    dve.nop(nofuse=True)
                    n = [part_ * RMS_STEPS]

                    def done(ins):
                        ins.then_inc(rms_step, 1)
                        n[0] += 1
                        dve.wait_ge(rms_step, t * (2 * RMS_STEPS) + n[0])
                    done(dve.tensor_scalar(rms["var"][:, at], squares[:, at], 1.0 / D, RMS_EPS, ALU.mult, ALU.add))
                    inverse_root(dve, {k: v[:, at] for k, v in rms.items()}, done)
                    if part_ == 0 and not first_tile:
                        dve.wait_ge(out_stored, t * 32)
                        dve.nop(nofuse=True)
                    for i in blocks:
                        banks.moves(dve.scalar_tensor_tensor(result[:, i, :], psum_of(t, ("y", i)), rms["y"][:, i:i + 1],
                                                             x2[:, bass.ds(t * TT + i, 1), :].rearrange("p a d -> p (a d)"),
                                                             ALU.mult, ALU.add), t, ("y", i))

            tile(0, True, False)
            with nc.vector.Fori(1, NT - 1) as t:
                tile(t, False, False)
            tile(NT - 1, False, True)


def whole_kernel(nc, x, ctx_2048, wq, wk, wv, wo, head_weights, b_q, b_k, b_v, w_o, b_o, gu_codes, gu_scales, down_codes,
                 down_scales, identity, own_new, causal, rope_cos, rope_sin, shifts, out):
    x1 = nc.dram_tensor("x1_scratch", (TOK, D), F32).ap()
    z = nc.dram_tensor("z_scratch", (2, HEADS, DH, TOK), F16).ap()
    with ExitStack() as ctx:
        psum = ctx.enter_context(nc.psum_tensor("psum", [P, 8, 512], F32))
        ident = ctx.enter_context(nc.sbuf_tensor("ident", [P, P], F32))
        x1_stored, z_stored = ctx.enter_context(nc.semaphore("x1_stored")), ctx.enter_context(nc.semaphore("z_stored"))

        def sb(name, shape, dt):
            return ctx.enter_context(nc.sbuf_tensor(name, shape, dt))

        wo_hi, wo_lo = sb("wo_hi", [P, HEADS, D], F16), sb("wo_lo", [P, HEADS, D], F16)
        xn, stat = sb("xn", [P, TT, D], F32), stat_buffers(sb)
        w_rows = sb("w_rows", [P, 2, HEADS * DH], F32)
        first_z = tuple(w_rows[:, i, :].bitcast(F16).rearrange("p (h t) -> p h t", t=TILE) for i in range(2))
        with ExitStack() as heads:
            def for_heads(name, shape, dt):
                return heads.enter_context(nc.sbuf_tensor(name, shape, dt))

            hqk_hi, hqk_lo = for_heads("hqk_hi", [P, 2 * KD, HEADS * DH], F16), for_heads("hqk_lo", [P, 2 * KD, HEADS * DH], F16)
            xattn_phase(nc, psum, ident, x.rearrange("b s d -> (b s) d"), ctx_2048.rearrange("b k d -> (b k) d"), wq, wk, wv, wo,
                        own_new, identity, x1, wo_hi, wo_lo, w_rows, xn, stat, head_weights, hqk_hi, hqk_lo, x1_stored)
            heads_phase(nc, psum, ident, x1, xn, stat, head_weights, hqk_hi, hqk_lo, w_rows, b_q, b_k, b_v,
                        rope_cos, rope_sin, causal, w_o, wo_hi, wo_lo, z, first_z, x1_stored, z_stored)
        x2 = sb("x2", [P, NT * TT, D], F32)
        gu, gu_scale = sb("gu", [P, KD, GU], F16), sb("gu_scale", [P, 2 * FB * KD], F32)
        down_hi, down_lo = sb("down_hi", [P, FB, D], F16), sb("down_lo", [P, FB, D], F16)
        merge_phase(nc, psum, z, x1, b_o, wo_hi, wo_lo, gu_codes, gu_scales, down_codes, down_scales, shifts,
                    first_z, z_stored, x2, xn, stat, gu, gu_scale, down_hi, down_lo)
        ffn_phase(nc, psum, ident, x2, xn, stat, gu, gu_scale, down_hi, down_lo, out.rearrange("b s d -> (b s) d"))


_INS = ["x", "ctx_2048", "L0_xattn_wq", "L0_xattn_wk", "L0_xattn_wv", "L0_xattn_wo",
        "head_weights", "L0_attn_b_Q", "L0_attn_b_K", "L0_attn_b_V", "L0_attn_W_O", "L0_attn_b_O",
        "L0_ffn_gate_up_packed", "L0_ffn_gate_up_scales", "L0_ffn_down_packed", "L0_ffn_down_scales"]


def _constants():
    import numpy as np
    own_new = np.zeros((P, KV + P), np.float32)
    at = np.arange(P)
    own = at[:, None] // S == at[None, :] // S
    own_new[:, KV:] = np.where(own, 0.0, -1.0e30)
    causal = np.where(at[None, :S] <= at[:, None] % S, 0.0, -1.0e30).astype(np.float32)
    inv_freq = (1.0 / np.float32(10000.0) ** (np.arange(0, DH, 2, dtype=np.float32) / np.float32(DH))).astype(np.float32)
    freqs = np.outer(inv_freq, np.arange(S, dtype=np.float32)).astype(np.float32)
    unscale = np.float32(1.0 / (XS * WS))
    rope = {f"rope_{f.__name__}": np.tile(f(freqs).astype(np.float32) * unscale, (2, 1)) for f in (np.cos, np.sin)}
    shifts = (4 * (at // 16)).astype(np.int32)[:, None]
    return {"identity": np.eye(P, dtype=np.float32), "own_new": own_new, "causal": causal, **rope, "shifts": shifts}


def _hidden_order():
    import numpy as np
    at = np.arange(P)
    whole = [8 * at + j for j in range(8)]
    rest = [8 * (WHOLE + 16 * q + at % 16) + at // 16 for q in range(REST)]
    return np.concatenate(whole + rest)


def _laid_out(name, inputs):
    import numpy as np
    if name == "head_weights":
        return np.concatenate([_laid_out("L0_attn_W_" + kind, inputs) for kind in "QKV"])
    a = np.asarray(inputs[name])
    if name.startswith("L0_xattn_w"):
        return a.T
    if name in ("L0_attn_W_Q", "L0_attn_W_K"):
        return a.reshape(HEADS, D, HALF, 2).transpose(1, 3, 0, 2).reshape(D, HEADS * DH)
    if name == "L0_attn_W_V":
        return a.transpose(1, 0, 2).reshape(D, HEADS * DH)
    if name in ("L0_attn_b_Q", "L0_attn_b_K"):
        return a.reshape(PAIRS, 2, HALF, 2).transpose(1, 2, 3, 0).reshape(P, 2, PAIRS)
    if name == "L0_attn_b_V":
        return a.T
    if name == "L0_attn_W_O":
        return a.transpose(1, 0, 2).reshape(DH, HEADS * D)
    if name == "L0_attn_b_O":
        return a[None, :]
    both = np.concatenate([_hidden_order(), FF + _hidden_order()])
    if name == "L0_ffn_gate_up_packed":
        return a[both].T
    if name == "L0_ffn_gate_up_scales":
        return a[:, both].reshape(KD, 2 * FB, P).transpose(2, 1, 0).reshape(P, 2 * FB * KD)
    if name == "L0_ffn_down_packed":
        return a.T
    return a


def kernel(**inputs):
    import numpy as _np
    import concourse.bacc as _bacc
    from concourse import mybir as _mybir
    from concourse.bass_utils import run_bass_kernel_spmd as _run

    nc = _bacc.Bacc("TRN2", target_bir_lowering=False, num_devices=1)
    arrays, args = {}, []
    for name, a in [(n, _laid_out(n, inputs)) for n in _INS] + list(_constants().items()):
        a = _np.ascontiguousarray(a)
        arrays[f"in_{name}_dram"] = a
        args.append(nc.dram_tensor(f"in_{name}_dram", a.shape, _mybir.dt.from_np(a.dtype), kind="ExternalInput").ap())
    out = nc.dram_tensor("out_0_dram", (B, S, D), F32, kind="ExternalOutput").ap()
    whole_kernel(nc, *args, out)
    r = _run(nc, [arrays], core_ids=[0])
    return r.results[0]["out_0_dram"]
```
